# Optimizing a Trainium2 kernel written in Bass

```python
import numpy as np
import jax
import jax.numpy as jnp

def _softmax(x, axis=-1):
    return jax.nn.softmax(x, axis=axis)

def _gelu(x):
    return jax.nn.gelu(x, approximate=True)

def _silu(x):
    return jax.nn.silu(x)

def _sigmoid(x):
    return jax.nn.sigmoid(x)

def _layernorm(x, axis=-1, eps=1e-05):
    m = jnp.mean(x, axis=axis, keepdims=True)
    v = jnp.var(x, axis=axis, keepdims=True)
    return (x - m) / jnp.sqrt(v + eps)

def _scatter_add(tgt, idx, src, axis=0):
    return tgt.at[idx].add(src)

def _segment_sum(src, seg, n):
    return jax.ops.segment_sum(src, seg, n)
kernel_name = 'mk_xattn_ffn_d2_seqx_r8_0516df'

def setup_inputs(seed: int=0):
    np.random.seed(seed)
    _w = jnp.asarray

    def _rec_inputs():
        import jax
        import jax.numpy as jnp
        _rk = jax.random.key(seed)
        x = -4.161e-06 + 1 * jax.random.normal(jax.random.fold_in(_rk, 1), (4, 256, 256), jnp.float32)
        _lenS = 256 - jax.random.randint(jax.random.fold_in(_rk, 7), (4,), 0, max(1, 256 // 4) + 1, jnp.int32)
        _lenS2 = 64 - jax.random.randint(jax.random.fold_in(_rk, 8), (4,), 0, max(1, 64 // 4) + 1, jnp.int32)
        _ctx_2048P = jax.random.normal(jax.random.fold_in(_rk, 11), (4, 16, 256), jnp.float32)
        _ctx_2048c = jax.random.dirichlet(jax.random.fold_in(_rk, 511), 0.3 * jnp.ones((16,), jnp.float32), (4, 64))
        _ctx_2048t = jnp.einsum('bsk,bkd->bsd', _ctx_2048c, _ctx_2048P)
        _ctx_2048t = _ctx_2048t * jax.lax.rsqrt(jnp.mean(jnp.square(_ctx_2048t)) + 1e-12) * 0.953939
        ctx_2048 = -0.000192764 + 0.999654 * (_ctx_2048t + 0.3 * jax.random.normal(jax.random.fold_in(_rk, 611), (4, 64, 256), jnp.float32))
        itok_BxS_0_1023 = jax.random.randint(jax.random.fold_in(_rk, 12), (4, 256), 0, 128, jnp.int32)
        return (x, ctx_2048, itok_BxS_0_1023)
    x, ctx_2048, itok_BxS_0_1023 = _rec_inputs()

    def _L0_xattn_setup():
        import jax, jax.numpy as jnp
        import numpy as np
        FP8_MAX = 448.0
        EPS = 1e-05

        def _fp8_roundtrip(x):
            return x.astype(jnp.float8_e4m3fn).astype(jnp.float32)

        def _div_clamp_fp8(x, scale):
            y = jnp.clip(x.astype(jnp.float32) / scale, -FP8_MAX, FP8_MAX)
            y = y.astype(jnp.bfloat16).astype(jnp.float32)
            return _fp8_roundtrip(y)

        def _ln(x, w, b):
            mu = jnp.mean(x, axis=-1, keepdims=True)
            var = jnp.mean(jnp.square(x - mu), axis=-1, keepdims=True)
            return (x - mu) * jax.lax.rsqrt(var + EPS) * w + b

        def _fp8_linear_pertensor(x, wq, w_scale, in_scale):
            xq = _div_clamp_fp8(x, in_scale)
            return jnp.einsum('bsi,oi->bso', xq * in_scale, wq) * w_scale

        def _gqa(q, k, v):
            scale = 1.0 / np.sqrt(q.shape[-1])
            scores = jnp.einsum('bsghd,btgd->bghst', q, k) * scale
            p = jax.nn.softmax(scores, axis=-1)
            return jnp.einsum('bghst,btgd->bsghd', p, v)
        key = jax.random.key(seed)
        ks = jax.random.split(key, 8)
        B, S, SC, H, NH, G, D = (2, 256, 64, 256, 16, 8, 128)

        def qw(k, out_f, in_f):
            w = jax.random.normal(k, (out_f, in_f), jnp.float32) * 0.02
            sc = jnp.max(jnp.abs(w)) / FP8_MAX
            return (_fp8_roundtrip(w / sc), sc.astype(jnp.float32))
        wq, wq_s = qw(ks[0], NH * D, H)
        wqx, wqx_s = qw(ks[1], NH * D, H)
        wk, wk_s = qw(ks[2], G * D, H)
        wv, wv_s = qw(ks[3], G * D, H)
        wproj, wp_s = qw(ks[4], H, 2 * NH * D)
        return {'hidden_states': jax.random.normal(ks[5], (B, S, H), jnp.float32), 'cond': jax.random.normal(ks[6], (B, SC, H), jnp.float32), 'ln_w': jnp.ones((H,), jnp.float32), 'ln_b': jnp.zeros((H,), jnp.float32), 'wq': wq, 'wq_scale': wq_s, 'q_in_scale': jnp.full((H,), 0.05, jnp.float32), 'wqx': wqx, 'wqx_scale': wqx_s, 'qx_in_scale': jnp.full((H,), 0.05, jnp.float32), 'wk': wk, 'wk_scale': wk_s, 'k_in_scale': jnp.full((H,), 0.05, jnp.float32), 'wv': wv, 'wv_scale': wv_s, 'v_in_scale': jnp.full((H,), 0.05, jnp.float32), 'w_kv_x': jax.random.normal(ks[7], (2 * G * D, H), jnp.float32) * 0.02, 'qln_w': jnp.ones((D,), jnp.float32), 'qln_b': jnp.zeros((D,), jnp.float32), 'kln_w': jnp.ones((D,), jnp.float32), 'kln_b': jnp.zeros((D,), jnp.float32), 'qxln_w': jnp.ones((D,), jnp.float32), 'qxln_b': jnp.zeros((D,), jnp.float32), 'kxln_w': jnp.ones((D,), jnp.float32), 'kxln_b': jnp.zeros((D,), jnp.float32), 'wproj': wproj, 'proj_w_scale': wp_s, 'proj_in_scale': jnp.asarray(0.05, jnp.float32), 'proj_smooth': jnp.full((2 * NH * D,), 0.05, jnp.float32)}
    _L0_xattn_all = _L0_xattn_setup()
    _L0_xattn_in = {k: v for k, v in _L0_xattn_all.items() if k in ('ln_w', 'ln_b', 'wq', 'wq_scale', 'q_in_scale', 'wqx', 'wqx_scale', 'qx_in_scale', 'wk', 'wk_scale', 'k_in_scale', 'wv', 'wv_scale', 'v_in_scale', 'w_kv_x', 'qln_w', 'qln_b', 'kln_w', 'kln_b', 'qxln_w', 'qxln_b', 'kxln_w', 'kxln_b', 'wproj', 'proj_w_scale', 'proj_in_scale', 'proj_smooth')}
    del _L0_xattn_all

    def _L0_ffn_setup():
        import jax, jax.numpy as jnp
        import numpy as np
        NUM_EXPERTS = 32
        TOP_K = 8
        SELECT_TOP_K = 4
        THRESHOLD = 0.5
        HIDDEN = 256
        D_FF = 96

        def _moe_forward(hidden_states, gate_weight, gate_up_proj, down_proj, similarity):
            B, S_len, H = hidden_states.shape
            E, K, Ssel = (NUM_EXPERTS, TOP_K, SELECT_TOP_K)
            x = hidden_states.reshape(-1, H)
            router_logits = x @ gate_weight.T
            router_probs = jax.nn.softmax(router_logits.astype(jnp.float32), axis=-1).astype(router_logits.dtype)
            router_top_value, router_indices = jax.lax.top_k(router_probs, K)
            routing_weights = router_top_value / jnp.clip(jnp.sum(router_top_value, axis=-1, keepdims=True), 1e-12, None)
            sim = similarity.astype(jnp.float32)
            sim = sim.at[jnp.arange(E), jnp.arange(E)].set(1.0)
            prim = router_indices[:, :Ssel]
            sec = router_indices[:, Ssel:]
            sim_cand = sim[sec[:, :, None], prim[:, None, :]]
            best_sim = jnp.max(sim_cand, axis=-1)
            best_i = jnp.argmax(sim_cand, axis=-1)
            prim_rep = jnp.broadcast_to(prim[:, None, :], sim_cand.shape)
            best_primary = jnp.take_along_axis(prim_rep, best_i[..., None], axis=-1)[..., 0]
            new_sec = jnp.where(best_sim < THRESHOLD, sec, best_primary) if THRESHOLD > 0.0 else best_primary
            rerouted_indices = jnp.concatenate([prim, new_sec], axis=1)
            combine = jnp.sum(jax.nn.one_hot(rerouted_indices, E, dtype=routing_weights.dtype) * routing_weights[..., None], axis=1)

            def expert_step(y, params):
                wgu, wd, cw = params
                gu = x @ wgu.T
                g, u = jnp.split(gu, 2, axis=-1)
                h = jax.nn.silu(g) * u
                y = y + h @ wd.T * cw[:, None]
                return (y, None)
            y0 = jnp.zeros_like(x)
            y, _ = jax.lax.scan(expert_step, y0, (gate_up_proj, down_proj, combine.T))
            return y.reshape(B, S_len, H)
        key = jax.random.key(seed)
        ks = jax.random.split(key, 5)
        hidden_states = jax.random.normal(ks[0], (4, 256, HIDDEN), dtype=jnp.float32)
        gate_weight = jax.random.normal(ks[1], (NUM_EXPERTS, HIDDEN), dtype=jnp.float32) * 0.02
        gate_up_proj = jax.random.normal(ks[2], (NUM_EXPERTS, 2 * D_FF, HIDDEN), dtype=jnp.float32) * 0.02
        down_proj = jax.random.normal(ks[3], (NUM_EXPERTS, HIDDEN, D_FF), dtype=jnp.float32) * 0.02
        similarity = jax.random.uniform(ks[4], (NUM_EXPERTS, NUM_EXPERTS), dtype=jnp.float32)
        return {'hidden_states': hidden_states, 'gate_weight': gate_weight, 'gate_up_proj': gate_up_proj, 'down_proj': down_proj, 'similarity': similarity}
    _L0_ffn_all = _L0_ffn_setup()
    _L0_ffn_in = {k: v for k, v in _L0_ffn_all.items() if k in ('gate_weight', 'gate_up_proj', 'down_proj', 'similarity')}
    del _L0_ffn_all

    def _L1_xattn_setup():
        import jax, jax.numpy as jnp
        import numpy as np
        B, Lq, Lk = (2, 512, 128)
        Q_DIM, KV_DIM = (256, 256)
        H, HD = (16, 128)
        KVC, QC, R = (64, 96, 64)
        LOOKBACK = 8
        NEG = -1e+30

        def _rope(x, L):
            half = x.shape[-1] // 2
            inv_freq = 1.0 / 10000.0 ** (jnp.arange(half, dtype=jnp.float32) / half)
            ang = jnp.arange(L, dtype=jnp.float32)[:, None] * inv_freq
            cos, sin = (jnp.cos(ang), jnp.sin(ang))
            x1, x2 = (x[..., :half], x[..., half:])
            return jnp.concatenate([x1 * cos - x2 * sin, x1 * sin + x2 * cos], axis=-1)
        key = jax.random.key(seed)
        ks = jax.random.split(key, 11)

        def w(k, shape, fan_in):
            return jax.random.normal(k, shape, jnp.float32) / np.sqrt(fan_in).astype(np.float32)
        return {'q': jax.random.normal(ks[0], (B, Lq, Q_DIM), jnp.float32), 'kv': jax.random.normal(ks[1], (B, Lk, KV_DIM), jnp.float32), 'seg_id': jnp.sort(jax.random.randint(ks[2], (B, Lq), 0, Lk), axis=-1), 'W_kvc': w(ks[3], (KV_DIM, KVC), KV_DIM), 'W_dq': w(ks[4], (Q_DIM, QC), Q_DIM), 'W_uq': w(ks[5], (QC, H * HD), QC), 'W_qr': w(ks[6], (QC, H * R), QC), 'W_uk': w(ks[7], (KVC, H * HD), KVC), 'W_kr': w(ks[8], (KVC, R), KVC), 'W_uv': w(ks[9], (KVC, H * HD), KVC), 'W_o': w(ks[10], (H * HD, Q_DIM), H * HD)}
    _L1_xattn_all = _L1_xattn_setup()
    _L1_xattn_in = {k: v for k, v in _L1_xattn_all.items() if k in ('W_kvc', 'W_dq', 'W_uq', 'W_qr', 'W_uk', 'W_kr', 'W_uv', 'W_o')}
    del _L1_xattn_all

    def _L1_ffn_setup():
        import jax, jax.numpy as jnp
        import numpy as np
        DIM = 256
        HID = 704
        ZERO_POINT = 128.0

        def _qlinear(x, wq, scale):
            W = (wq.astype(jnp.float32) - ZERO_POINT) * scale[:, None]
            return jnp.einsum('bsd,hd->bsh', x, W)
        key = jax.random.key(seed)
        ks = jax.random.split(key, 7)
        B, S = (4, 256)
        sg = jax.random.uniform(ks[1], (HID,)) * (0.02 / np.sqrt(DIM)) + 0.0001
        su = jax.random.uniform(ks[3], (HID,)) * (0.02 / np.sqrt(DIM)) + 0.0001
        sd = jax.random.uniform(ks[5], (DIM,)) * (0.02 / np.sqrt(HID)) + 0.0001
        return {'x': jax.random.normal(ks[0], (B, S, DIM), dtype=jnp.float32), 'wq_gate': jax.random.randint(ks[2], (HID, DIM), 0, 32, dtype=jnp.int32), 's_gate': sg, 'wq_up': jax.random.randint(ks[4], (HID, DIM), 0, 32, dtype=jnp.int32), 's_up': su, 'wq_down': jax.random.randint(ks[6], (DIM, HID), 0, 32, dtype=jnp.int32), 's_down': sd}
    _L1_ffn_all = _L1_ffn_setup()
    _L1_ffn_in = {k: v for k, v in _L1_ffn_all.items() if k in ('wq_gate', 's_gate', 'wq_up', 's_up', 'wq_down', 's_down')}
    del _L1_ffn_all
    return {'x': x, 'ctx_2048': ctx_2048, 'itok_BxS_0_1023': itok_BxS_0_1023, 'L0_xattn_ln_w': _L0_xattn_in['ln_w'], 'L0_xattn_ln_b': _L0_xattn_in['ln_b'], 'L0_xattn_wq': _L0_xattn_in['wq'], 'L0_xattn_wq_scale': _L0_xattn_in['wq_scale'], 'L0_xattn_q_in_scale': _L0_xattn_in['q_in_scale'], 'L0_xattn_wqx': _L0_xattn_in['wqx'], 'L0_xattn_wqx_scale': _L0_xattn_in['wqx_scale'], 'L0_xattn_qx_in_scale': _L0_xattn_in['qx_in_scale'], 'L0_xattn_wk': _L0_xattn_in['wk'], 'L0_xattn_wk_scale': _L0_xattn_in['wk_scale'], 'L0_xattn_k_in_scale': _L0_xattn_in['k_in_scale'], 'L0_xattn_wv': _L0_xattn_in['wv'], 'L0_xattn_wv_scale': _L0_xattn_in['wv_scale'], 'L0_xattn_v_in_scale': _L0_xattn_in['v_in_scale'], 'L0_xattn_w_kv_x': _L0_xattn_in['w_kv_x'], 'L0_xattn_qln_w': _L0_xattn_in['qln_w'], 'L0_xattn_qln_b': _L0_xattn_in['qln_b'], 'L0_xattn_kln_w': _L0_xattn_in['kln_w'], 'L0_xattn_kln_b': _L0_xattn_in['kln_b'], 'L0_xattn_qxln_w': _L0_xattn_in['qxln_w'], 'L0_xattn_qxln_b': _L0_xattn_in['qxln_b'], 'L0_xattn_kxln_w': _L0_xattn_in['kxln_w'], 'L0_xattn_kxln_b': _L0_xattn_in['kxln_b'], 'L0_xattn_wproj': _L0_xattn_in['wproj'], 'L0_xattn_proj_w_scale': _L0_xattn_in['proj_w_scale'], 'L0_xattn_proj_in_scale': _L0_xattn_in['proj_in_scale'], 'L0_xattn_proj_smooth': _L0_xattn_in['proj_smooth'], 'L0_ffn_gate_weight': _L0_ffn_in['gate_weight'], 'L0_ffn_gate_up_proj': _L0_ffn_in['gate_up_proj'], 'L0_ffn_down_proj': _L0_ffn_in['down_proj'], 'L0_ffn_similarity': _L0_ffn_in['similarity'], 'L1_xattn_W_kvc': _L1_xattn_in['W_kvc'], 'L1_xattn_W_dq': _L1_xattn_in['W_dq'], 'L1_xattn_W_uq': _L1_xattn_in['W_uq'], 'L1_xattn_W_qr': _L1_xattn_in['W_qr'], 'L1_xattn_W_uk': _L1_xattn_in['W_uk'], 'L1_xattn_W_kr': _L1_xattn_in['W_kr'], 'L1_xattn_W_uv': _L1_xattn_in['W_uv'], 'L1_xattn_W_o': _L1_xattn_in['W_o'], 'L1_ffn_wq_gate': _L1_ffn_in['wq_gate'], 'L1_ffn_s_gate': _L1_ffn_in['s_gate'], 'L1_ffn_wq_up': _L1_ffn_in['wq_up'], 'L1_ffn_s_up': _L1_ffn_in['s_up'], 'L1_ffn_wq_down': _L1_ffn_in['wq_down'], 'L1_ffn_s_down': _L1_ffn_in['s_down']}

def reference(x, ctx_2048, itok_BxS_0_1023, L0_xattn_ln_w, L0_xattn_ln_b, L0_xattn_wq, L0_xattn_wq_scale, L0_xattn_q_in_scale, L0_xattn_wqx, L0_xattn_wqx_scale, L0_xattn_qx_in_scale, L0_xattn_wk, L0_xattn_wk_scale, L0_xattn_k_in_scale, L0_xattn_wv, L0_xattn_wv_scale, L0_xattn_v_in_scale, L0_xattn_w_kv_x, L0_xattn_qln_w, L0_xattn_qln_b, L0_xattn_kln_w, L0_xattn_kln_b, L0_xattn_qxln_w, L0_xattn_qxln_b, L0_xattn_kxln_w, L0_xattn_kxln_b, L0_xattn_wproj, L0_xattn_proj_w_scale, L0_xattn_proj_in_scale, L0_xattn_proj_smooth, L0_ffn_gate_weight, L0_ffn_gate_up_proj, L0_ffn_down_proj, L0_ffn_similarity, L1_xattn_W_kvc, L1_xattn_W_dq, L1_xattn_W_uq, L1_xattn_W_qr, L1_xattn_W_uk, L1_xattn_W_kr, L1_xattn_W_uv, L1_xattn_W_o, L1_ffn_wq_gate, L1_ffn_s_gate, L1_ffn_wq_up, L1_ffn_s_up, L1_ffn_wq_down, L1_ffn_s_down):
    import jax
    import jax.numpy as jnp

    def _L0_xattn_ref(hidden_states, cond, ln_w, ln_b, wq, wq_scale, q_in_scale, wqx, wqx_scale, qx_in_scale, wk, wk_scale, k_in_scale, wv, wv_scale, v_in_scale, w_kv_x, qln_w, qln_b, kln_w, kln_b, qxln_w, qxln_b, kxln_w, kxln_b, wproj, proj_w_scale, proj_in_scale, proj_smooth):
        import jax, jax.numpy as jnp
        import numpy as np
        FP8_MAX = 448.0
        EPS = 1e-05

        def _fp8_roundtrip(x):
            return x.astype(jnp.float8_e4m3fn).astype(jnp.float32)

        def _div_clamp_fp8(x, scale):
            y = jnp.clip(x.astype(jnp.float32) / scale, -FP8_MAX, FP8_MAX)
            y = y.astype(jnp.bfloat16).astype(jnp.float32)
            return _fp8_roundtrip(y)

        def _ln(x, w, b):
            mu = jnp.mean(x, axis=-1, keepdims=True)
            var = jnp.mean(jnp.square(x - mu), axis=-1, keepdims=True)
            return (x - mu) * jax.lax.rsqrt(var + EPS) * w + b

        def _fp8_linear_pertensor(x, wq, w_scale, in_scale):
            xq = _div_clamp_fp8(x, in_scale)
            return jnp.einsum('bsi,oi->bso', xq * in_scale, wq) * w_scale

        def _gqa(q, k, v):
            scale = 1.0 / np.sqrt(q.shape[-1])
            scores = jnp.einsum('bsghd,btgd->bghst', q, k) * scale
            p = jax.nn.softmax(scores, axis=-1)
            return jnp.einsum('bghst,btgd->bsghd', p, v)
        b, s, _ = hidden_states.shape
        sc = cond.shape[1]
        d = qln_w.shape[0]
        nh = wq.shape[0] // d
        g = wk.shape[0] // d
        hpg = nh // g
        ln_out = _ln(hidden_states, ln_w, ln_b)
        q = _fp8_linear_pertensor(ln_out, wq, wq_scale, q_in_scale).reshape(b, s, g, hpg, d)
        q = _ln(q, qln_w, qln_b)
        k = _fp8_linear_pertensor(ln_out, wk, wk_scale, k_in_scale).reshape(b, s, g, d)
        k = _ln(k, kln_w, kln_b)
        v = _fp8_linear_pertensor(ln_out, wv, wv_scale, v_in_scale).reshape(b, s, g, d)
        core = _gqa(q, k, v).reshape(b, s, nh * d)
        qx = _fp8_linear_pertensor(ln_out, wqx, wqx_scale, qx_in_scale).reshape(b, s, g, hpg, d)
        qx = _ln(qx, qxln_w, qxln_b)
        kvx = jnp.einsum('bsi,oi->bso', cond, w_kv_x)
        kx, vx = jnp.split(kvx, 2, axis=-1)
        kx = _ln(kx.reshape(b, sc, g, d), kxln_w, kxln_b)
        vx = vx.reshape(b, sc, g, d)
        xout = _gqa(qx, kx, vx).reshape(b, s, nh * d)
        cat = jnp.concatenate([core, xout], axis=-1)
        catq = _div_clamp_fp8(cat, proj_smooth)
        return jnp.einsum('bsi,oi->bso', catq, wproj) * (proj_in_scale * proj_w_scale)

    def _L0_ffn_ref(hidden_states, gate_weight, gate_up_proj, down_proj, similarity):
        import jax, jax.numpy as jnp
        import numpy as np
        NUM_EXPERTS = 32
        TOP_K = 8
        SELECT_TOP_K = 4
        THRESHOLD = 0.5
        HIDDEN = 256
        D_FF = 96

        def _moe_forward(hidden_states, gate_weight, gate_up_proj, down_proj, similarity):
            B, S_len, H = hidden_states.shape
            E, K, Ssel = (NUM_EXPERTS, TOP_K, SELECT_TOP_K)
            x = hidden_states.reshape(-1, H)
            router_logits = x @ gate_weight.T
            router_probs = jax.nn.softmax(router_logits.astype(jnp.float32), axis=-1).astype(router_logits.dtype)
            router_top_value, router_indices = jax.lax.top_k(router_probs, K)
            routing_weights = router_top_value / jnp.clip(jnp.sum(router_top_value, axis=-1, keepdims=True), 1e-12, None)
            sim = similarity.astype(jnp.float32)
            sim = sim.at[jnp.arange(E), jnp.arange(E)].set(1.0)
            prim = router_indices[:, :Ssel]
            sec = router_indices[:, Ssel:]
            sim_cand = sim[sec[:, :, None], prim[:, None, :]]
            best_sim = jnp.max(sim_cand, axis=-1)
            best_i = jnp.argmax(sim_cand, axis=-1)
            prim_rep = jnp.broadcast_to(prim[:, None, :], sim_cand.shape)
            best_primary = jnp.take_along_axis(prim_rep, best_i[..., None], axis=-1)[..., 0]
            new_sec = jnp.where(best_sim < THRESHOLD, sec, best_primary) if THRESHOLD > 0.0 else best_primary
            rerouted_indices = jnp.concatenate([prim, new_sec], axis=1)
            combine = jnp.sum(jax.nn.one_hot(rerouted_indices, E, dtype=routing_weights.dtype) * routing_weights[..., None], axis=1)

            def expert_step(y, params):
                wgu, wd, cw = params
                gu = x @ wgu.T
                g, u = jnp.split(gu, 2, axis=-1)
                h = jax.nn.silu(g) * u
                y = y + h @ wd.T * cw[:, None]
                return (y, None)
            y0 = jnp.zeros_like(x)
            y, _ = jax.lax.scan(expert_step, y0, (gate_up_proj, down_proj, combine.T))
            return y.reshape(B, S_len, H)
        return _moe_forward(hidden_states, gate_weight, gate_up_proj, down_proj, similarity)

    def _L1_xattn_ref(q, kv, seg_id, W_kvc, W_dq, W_uq, W_qr, W_uk, W_kr, W_uv, W_o):
        import jax, jax.numpy as jnp
        import numpy as np
        B, Lq, Lk = (2, 512, 128)
        Q_DIM, KV_DIM = (256, 256)
        H, HD = (16, 128)
        KVC, QC, R = (64, 96, 64)
        LOOKBACK = 8
        NEG = -1e+30

        def _rope(x, L):
            half = x.shape[-1] // 2
            inv_freq = 1.0 / 10000.0 ** (jnp.arange(half, dtype=jnp.float32) / half)
            ang = jnp.arange(L, dtype=jnp.float32)[:, None] * inv_freq
            cos, sin = (jnp.cos(ang), jnp.sin(ang))
            x1, x2 = (x[..., :half], x[..., half:])
            return jnp.concatenate([x1 * cos - x2 * sin, x1 * sin + x2 * cos], axis=-1)
        b, lq, _ = q.shape
        lk = kv.shape[1]
        kv_c = kv @ W_kvc
        q_c = q @ W_dq
        q_nope = (q_c @ W_uq).reshape(b, lq, H, HD).transpose(0, 2, 1, 3)
        q_rope = (q_c @ W_qr).reshape(b, lq, H, R).transpose(0, 2, 1, 3)
        k_nope = (kv_c @ W_uk).reshape(b, lk, H, HD)
        v = (kv_c @ W_uv).reshape(b, lk, H, HD)
        k_rope = kv_c @ W_kr
        q_rope = _rope(q_rope, lq)
        k_rope = _rope(k_rope, lk)
        scale = 1.0 / np.sqrt(HD + R).astype(np.float32)
        scores = (jnp.einsum('bhqd,bkhd->bhqk', q_nope, k_nope) + jnp.einsum('bhqr,bkr->bhqk', q_rope, k_rope)) * scale
        k_ids = jnp.arange(lk)[None, None, :]
        qs = seg_id[:, :, None]
        good = (k_ids <= qs) & (k_ids >= qs - LOOKBACK)
        scores = jnp.where(good[:, None, :, :], scores, NEG)
        attn = jax.nn.softmax(scores, axis=-1)
        out = jnp.einsum('bhqk,bkhd->bqhd', attn, v).reshape(b, lq, H * HD)
        return out @ W_o

    def _L1_ffn_ref(x, wq_gate, s_gate, wq_up, s_up, wq_down, s_down):
        import jax, jax.numpy as jnp
        import numpy as np
        DIM = 256
        HID = 704
        ZERO_POINT = 128.0

        def _qlinear(x, wq, scale):
            W = (wq.astype(jnp.float32) - ZERO_POINT) * scale[:, None]
            return jnp.einsum('bsd,hd->bsh', x, W)
        gate = _qlinear(x, wq_gate, s_gate)
        gate = jax.nn.silu(gate)
        up = _qlinear(x, wq_up, s_up)
        return _qlinear(gate * up, wq_down, s_down)
    x = x + _L0_xattn_ref(_layernorm(x, axis=-1), ctx_2048, L0_xattn_ln_w, L0_xattn_ln_b, L0_xattn_wq, L0_xattn_wq_scale, L0_xattn_q_in_scale, L0_xattn_wqx, L0_xattn_wqx_scale, L0_xattn_qx_in_scale, L0_xattn_wk, L0_xattn_wk_scale, L0_xattn_k_in_scale, L0_xattn_wv, L0_xattn_wv_scale, L0_xattn_v_in_scale, L0_xattn_w_kv_x, L0_xattn_qln_w, L0_xattn_qln_b, L0_xattn_kln_w, L0_xattn_kln_b, L0_xattn_qxln_w, L0_xattn_qxln_b, L0_xattn_kxln_w, L0_xattn_kxln_b, L0_xattn_wproj, L0_xattn_proj_w_scale, L0_xattn_proj_in_scale, L0_xattn_proj_smooth)
    x = x + _L0_ffn_ref(_layernorm(x, axis=-1), L0_ffn_gate_weight, L0_ffn_gate_up_proj, L0_ffn_down_proj, L0_ffn_similarity)
    x = x + _L1_xattn_ref(_layernorm(x, axis=-1), ctx_2048, itok_BxS_0_1023, L1_xattn_W_kvc, L1_xattn_W_dq, L1_xattn_W_uq, L1_xattn_W_qr, L1_xattn_W_uk, L1_xattn_W_kr, L1_xattn_W_uv, L1_xattn_W_o)
    x = x + _L1_ffn_ref(_layernorm(x, axis=-1), L1_ffn_wq_gate, L1_ffn_s_gate, L1_ffn_wq_up, L1_ffn_s_up, L1_ffn_wq_down, L1_ffn_s_down)
    return x

_drawn_inputs = setup_inputs


def setup_inputs(seed=0):
    import zlib

    import numpy as np

    out = dict(_drawn_inputs(seed))
    spreads = {'L0_xattn_ln_w': (1.0, 0.6),
     'L0_xattn_ln_b': (0.0, 0.285),
     'L0_xattn_q_in_scale': (0.05000000074505806, 0.6),
     'L0_xattn_qx_in_scale': (0.05000000074505806, 0.6),
     'L0_xattn_k_in_scale': (0.05000000074505806, 0.6),
     'L0_xattn_v_in_scale': (0.05000000074505806, 0.6),
     'L0_xattn_qln_w': (1.0, 0.6),
     'L0_xattn_qln_b': (0.0, 0.8),
     'L0_xattn_kln_w': (1.0, 0.6),
     'L0_xattn_kln_b': (0.0, 0.8),
     'L0_xattn_qxln_w': (1.0, 0.6),
     'L0_xattn_qxln_b': (0.0, 0.8),
     'L0_xattn_kxln_w': (1.0, 0.6),
     'L0_xattn_kxln_b': (0.0, 0.8),
     'L0_xattn_proj_smooth': (0.05000000074505806, 0.2)}
    factors = {'L0_ffn_gate_weight': 8.0,
     'L0_ffn_gate_up_proj': 8.0,
     'L0_ffn_down_proj': 8.0,
     'L0_ffn_similarity': 8.0,
     'L1_ffn_s_gate': 8.0,
     'L1_ffn_s_up': 8.0,
     'L1_ffn_s_down': 8.0}
    for name, (base, spread) in spreads.items():
        noise = np.random.default_rng([zlib.crc32(name.encode()), seed]).standard_normal(out[name].shape)
        drawn = base * np.exp(spread * noise) if base else spread * noise
        out[name] = jnp.asarray(drawn.astype(out[name].dtype))
    for name, factor in factors.items():
        out[name] = (out[name] * factor).astype(out[name].dtype)
    return out
```

```python
from contextlib import ExitStack

import concourse.bass as bass
from concourse import mybir
import numpy as np

ALU = mybir.AluOpType
ACT = mybir.ActivationFunctionType
F32 = mybir.dt.float32
FR = mybir.dt.float32r
BF = mybir.dt.bfloat16
U16 = mybir.dt.uint16
U32 = mybir.dt.uint32
I32 = mybir.dt.int32
X = mybir.AxisListType.X

PE, AC, DV, PO, SP = "pe", "ac", "dv", "po", "sp"
EPS = 1e-5
NEG = 1e30


class Queues:

    LIMIT = 3000

    def __init__(self, nc, ctx):
        self.nc, self.ctx = nc, ctx
        self.q = {e: [] for e in (PE, AC, DV, PO, SP)}
        self.sem, self.n, self.made = {}, {}, 0

    def fresh(self, name):
        self.made += 1
        return self.ctx.enter_context(self.nc.semaphore(f"{name}{self.made}"))

    def do(self, e, fns, waits=()):
        if e not in self.sem or self.n[e] >= self.LIMIT:
            self.sem[e], self.n[e] = self.fresh(f"s_{e}_"), 0
        self.n[e] += 1
        self.q[e].append(("run", tuple(w for w in waits if w), fns if isinstance(fns, list) else [fns], self.sem[e], 1))
        return (self.sem[e], self.n[e])

    def dma(self, e, pairs, waits=()):
        s = self.fresh("d_")
        for i, (o, a) in enumerate(pairs):
            self.q[e].append(("dma", tuple(w for w in waits if w) if i == 0 else (), (o, a), s, 16))
        return (s, 16 * len(pairs))

    def wait(self, e, waits):
        self.q[e].append(("wait", tuple(waits), None, None, 0))

    def play(self, e, eng):
        seen = {}
        for kind, waits, what, s, inc in self.q[e]:
            for ws, wv in waits:
                if seen.get(ws.name, 0) < wv:
                    eng.wait_ge(ws, wv)
                    seen[ws.name] = wv
            if kind == "run":
                for f in what:
                    ins = f(eng)
                ins.then_inc(s, inc)
            elif kind == "dma":
                eng.dma_start(what[0], what[1]).then_inc(s, inc)


class Ring:

    def __init__(self, n):
        self.n, self.at, self.users = n, 0, [[] for _ in range(n)]

    def take(self):
        i = self.at % self.n
        self.at += 1
        w, self.users[i] = self.users[i], []
        return i, w

    def free(self, i, *tokens):
        self.users[i] += tokens


def program(nc, A, out, stages=4):
    ctx = ExitStack()
    Q = Queues(nc, ctx)
    do = Q.do

    def bcast(ap, shape):
        return ap.to_broadcast(shape) if hasattr(ap, "to_broadcast") else ap.broadcast_to(shape)

    with ctx:
        def sb(name, shape, dt, c=ctx):
            return c.enter_context(nc.sbuf_tensor(name, shape, dt))

        PS = ctx.enter_context(nc.psum_tensor("PS", [128, 8, 512], F32))
        banks = Ring(8)

        xt = sb("xt", [128, 8, 256], F32)
        idf = sb("idf", [128, 128], F32)
        ctxT = sb("ctxT", [128, 2, 256], F32)
        st = sb("st", [128, 8, 6], F32)
        mv = sb("mv", [128, 8, 2], F32)
        rs = sb("rs", [128, 8], F32)
        xn = sb("xn", [128, 8, 256], F32)

        t_x = Q.dma(SP, [(xt[:], A["x"].rearrange("(c p) d -> p c d", p=128))])
        t_id = Q.dma(AC, [(idf[:], A["idf"])])
        t_ctx = Q.dma(AC, [(ctxT[:], A["ctxT"].rearrange("(k p) t -> p k t", p=128))])

        ve = sb("ve", [128, 8], F32)
        nt = sb("nt", [128, 84], F32)

        def newton(y, v, n, t):
            t = do(DV, lambda e: e.tensor_tensor(n, y, y, ALU.mult), [t])
            t = do(DV, lambda e: e.tensor_tensor(n, n, v, ALU.mult), [t])
            t = do(DV, lambda e: e.tensor_scalar(n, n, -0.5, 1.5, ALU.mult, ALU.add), [t])
            return do(DV, lambda e: e.tensor_tensor(y, y, n, ALU.mult), [t])

        def layernorm(src, ready, dst, free=()):
            last = None
            for c in range(8):
                last = do(DV, lambda e, c=c: e.bn_stats(st[:, c, :], src[:, c, :]), [ready, *free])
            for c in range(8):
                t_mv = do(DV, lambda e, c=c: e.bn_aggr(mv[:, c, :], st[:, c, :]), [last])
            t = do(DV, lambda e: e.tensor_scalar(ve[:, :], mv[:, :, 1], EPS, None, ALU.add), [t_mv])
            t = do(AC, lambda e: e.activation(rs[:, :], ve[:, :], ACT.Sqrt), [t])
            t = do(DV, lambda e: e.reciprocal(rs[:, :], rs[:, :]), [t])
            t = newton(rs[:, :], ve[:, :], nt[:, 0:8], t)
            return [do(DV, lambda e, c=c: e.tensor_scalar(dst[:, c, :], src[:, c, :], mv[:, c, 0:1], rs[:, c:c + 1],
                                                          ALU.subtract, ALU.mult), [t]) for c in range(8)]

        def turn(src, t_src, evac):
            for k in range(2):
                for h in range(2):
                    b, w = banks.take()
                    t = do(PE, [lambda e, b=b, c=c, k=k: e.transpose(PS[:, b, (c % 4) * 128:(c % 4 + 1) * 128],
                                                                    src[:, c, k * 128:(k + 1) * 128], idf[:, :])
                                for c in range(4 * h, 4 * h + 4)], [*w, *t_src[4 * h:4 * h + 4], t_id])
                    banks.free(b, evac(k, h, b, t))

        c0 = ExitStack()
        with c0:
            vec = sb("vec", [128, 12], F32, c0)
            ln8 = sb("ln8", [128, 8], F32, c0)
            smo = sb("smo", [128, 32], F32, c0)
            sca = sb("sca", [128, 6], F32, c0)
            t_vec = Q.dma(AC, [(vec[:], A["vec"]), (ln8[:], A["ln8"]), (smo[:], A["smo"]), (sca[:], A["sca"])])
            xq = [sb(f"xq{i}", [128, 2, 1024], FR, c0) for i in range(4)]
            ivec = sb("ivec", [128, 4, 2], F32, c0)
            ismo = sb("ismo", [128, 32], F32, c0)
            sproj = sb("sproj", [128, 1], F32, c0)

            t_h0 = layernorm(xt, t_x, xn)
            t_hn = layernorm(xn, t_h0[-1], xn)
            t_iv = do(DV, lambda e: e.reciprocal(ivec[:].rearrange("p a b -> p (a b)"), vec[:, 4:12]), [t_vec])
            t_is = do(DV, lambda e: e.reciprocal(ismo[:, :], smo[:, :]), [t_vec])
            t_sp = do(DV, lambda e: e.tensor_tensor(sproj[:], sca[:, 4:5], sca[:, 5:6], ALU.mult), [t_vec])
            t_l8 = [do(DV, lambda e, j=j: e.tensor_scalar(ln8[:, j:j + 2], ln8[:, j:j + 2], float(128 ** -0.5), None, ALU.mult),
                       [t_vec]) for j in (0, 4)]
            t_ln = []
            cq = ExitStack()
            lnT = sb("lnT", [128, 2, 1024], F32, cq)

            def ev_ln(k, h, b, t):
                t = do(AC, lambda e: e.activation(lnT[:, k, h * 512:(h + 1) * 512], PS[:, b, :], ACT.Identity,
                                                  bias=vec[:, 2 + k:3 + k], scale=vec[:, k:k + 1]), [t, t_vec])
                t_ln.append(t)
                return t
            turn(xn, t_hn, ev_ln)

            def quant(y, tmpF, tmpT, dst, t_y, free):
                t = do(DV, lambda e: e.tensor_scalar(y, y, 448.0, -448.0, ALU.min, ALU.max), [*t_y])
                t = do(DV, lambda e: e.tensor_scalar(tmpF.bitcast(U16), y.bitcast(U16), 0x7F80, 0x0040,
                                                     ALU.bitwise_and, ALU.bitwise_or), [t, *free])
                t = do(DV, lambda e: e.tensor_scalar(tmpF, tmpF, 1.5 * 2.0 ** -6, None, ALU.max), [t])
                t = do(DV, lambda e: e.scalar_tensor_tensor(tmpT, tmpF, float(2 ** 20), y, ALU.mult, ALU.add), [t])
                return do(DV, lambda e: e.scalar_tensor_tensor(dst, tmpF, -float(2 ** 20), tmpT, ALU.mult, ALU.add), [t])

            t_xq = []
            with cq:
                yb = sb("yb0", [128, 2048], BF, cq)
                fb = sb("fb0", [128, 2048], BF, cq)
                tb = sb("tb0", [128, 2048], F32, cq)
                rb = sb("rb0", [128, 2048], F32, cq)
                nivec = sb("nivec", [128, 4, 2], F32, cq)
                t_niv = do(DV, lambda e: e.tensor_scalar(nivec[:], ivec[:], -1.0, None, ALU.mult), [t_iv])
                t_prev = []
                for i in range(4):
                    ts = []
                    for k in range(2):
                        q_, s_ = tb[:, k * 1024:(k + 1) * 1024], vec[:, 4 + 2 * i + k:5 + 2 * i + k]
                        r_ = rb[:, k * 1024:(k + 1) * 1024]
                        t = do(DV, lambda e, i=i, k=k, q_=q_: e.tensor_scalar(
                            q_, lnT[:, k, :], ivec[:, i, k:k + 1], None, ALU.mult), [t_iv, *t_ln, *t_prev])
                        t = do(DV, lambda e, k=k, q_=q_, s_=s_, r_=r_: e.scalar_tensor_tensor(
                            r_, q_, s_, lnT[:, k, :], ALU.mult, ALU.subtract), [t, *t_prev])
                        ts.append(do(DV, lambda e, i=i, k=k, q_=q_, r_=r_: e.scalar_tensor_tensor(
                            yb[:, k * 1024:(k + 1) * 1024], r_, nivec[:, i, k:k + 1], q_, ALU.mult, ALU.add), [t, t_niv]))
                    t = quant(yb[:, :], fb[:, :], tb[:, :], xq[i][:].rearrange("p k t -> p (k t)"), ts, t_prev)
                    t_prev = [t]
                    t_xq.append(t)

            wst = [sb(f"wst{i}", [128, 2, 256], F32, c0) for i in range(2)]
            wring = Ring(2)
            WH = sb("WH", [128, 2, 1536], FR, c0)
            WL = sb("WL", [128, 2, 1536], FR, c0)
            w_users = []
            PH = sb("PH", [128, 8, 256], FR, c0)
            PL = sb("PL", [128, 8, 256], FR, c0)
            p_users = []
            KV = sb("KV", [128, 2, 256], F32, c0)
            kv_users = []

            def load_w(gp):
                toks = []
                users = list(w_users)
                w_users.clear()
                for j in range(6):
                    i, w = wring.take()
                    s = (0, 0, 1, 1, 2, 3)[j]
                    td = Q.dma(SP, [(wst[i][:], A["wall"][gp, :, :, j * 256:(j + 1) * 256])], w + t_xq[-1:])
                    t = None
                    for k in range(2):
                        t = do(PO, lambda e, i=i, k=k, s=s: e.tensor_scalar(
                            wst[i][:, k, :], wst[i][:, k, :], vec[:, 4 + 2 * s + k:5 + 2 * s + k], None, ALU.mult), [td, t_vec])
                    th = do(PO, lambda e, i=i, j=j: e.tensor_copy(WH[:, :, j * 256:(j + 1) * 256], wst[i][:]), [t, *users])
                    tl = do(PO, lambda e, i=i, j=j: e.tensor_tensor(
                        WL[:, :, j * 256:(j + 1) * 256], wst[i][:], WH[:, :, j * 256:(j + 1) * 256].bitcast(F32),
                        ALU.subtract), [th, *users])
                    wring.free(i, tl)
                    toks.append(tl)
                return toks

            def load_p(gp):
                toks = []
                users = list(p_users)
                p_users.clear()
                for j in range(4):
                    i, w = wring.take()
                    td = Q.dma(SP, [(wst[i][:], A["wproj"][gp, :, 2 * j:2 * j + 2, :])], w + t_xq[-1:])
                    th = do(PO, lambda e, i=i, j=j: e.tensor_copy(PH[:, 2 * j:2 * j + 2, :], wst[i][:]), [td, *users])
                    tl = do(PO, lambda e, i=i, j=j: e.tensor_tensor(
                        PL[:, 2 * j:2 * j + 2, :], wst[i][:], PH[:, 2 * j:2 * j + 2, :].bitcast(F32), ALU.subtract),
                        [th, *users])
                    wring.free(i, tl)
                    toks.append(tl)
                return toks

            raw = sb("raw", [128, 8, 1280], F32, c0)
            raws = Ring(8)
            vr = sb("vr", [128, 10, 256], F32, c0)
            vrs = Ring(10)
            kraw = xn[:, 6:8, :]
            vx = sb("vx", [64, 4, 256], F32, c0)
            st6 = sb("st6", [128, 24, 6], F32, c0)
            mv2 = [sb(f"mv2{i}", [128, 84, 2], F32, c0) for i in range(2)]
            rs2 = sb("rs2", [128, 84], F32, c0)
            qT = [sb(f"qT{i}", [128, 4, 256], F32, c0) for i in range(2)]
            qxT = [sb(f"qxT{i}", [128, 4, 256], F32, c0) for i in range(2)]
            kT = [sb(f"kT{i}", [128, 2, 256], F32, c0) for i in range(2)]
            kxT = sb("kxT", [128, 2, 256], F32, c0)
            P = [sb(f"P{i}", [128, 4, 256], F32, c0) for i in range(2)]
            PT = [sb(f"PT{i}", [128, 2, 512], F32, c0) for i in range(2)]
            sm = [sb(f"sm{i}", [128, 3, 8], F32, c0) for i in range(2)]
            smr, ptr = Ring(2), Ring(2)
            yT = sb("yT", [128, 8, 256], BF, c0)
            yr = Ring(1)
            yt = xn[:, 0:4, :].rearrange("p a b -> p (a b)")
            yF = xn[:, 4:6, :].rearrange("p a b -> p (a b)").bitcast(BF)
            cat = sb("cat", [128, 8, 256], FR, c0)

            state = {}
            slot, vslot, t_raw, t_st = {}, {}, {}, {}

            def P1(gp, c):
                r, rw = raws.take()
                slot[gp, c] = r
                rv, vw = vrs.take()
                vslot[gp, c] = rv
                tw = state["w", gp]
                tc = slice(c * 128, (c + 1) * 128)
                segs = [[(0, 0, 512, 0)], [(1, 512, 512, 0)], [(2, 1024, 256, 0), (3, 1280, 256, 256)]]
                toks = []
                for seg in segs:
                    b, w = banks.take()
                    fns = []
                    for s, w0, n, o in seg:
                        for k in range(2):
                            for i, W in enumerate((WH, WL)):
                                fns.append(lambda e, s=s, k=k, W=W, w0=w0, n=n, o=o, b=b, i=i: e.matmul(
                                    PS[:, b, o:o + n], xq[s][:, k, tc], W[:, k, w0:w0 + n],
                                    start=(k == 0 and i == 0), stop=(k == 1 and i == 1)))
                    t = do(PE, fns, [*w, *t_xq, *tw])
                    ev = [do(AC, lambda e, s=s, w0=w0, n=n, o=o, b=b: e.activation(
                        vr[:, rv, :] if s == 3 else raw[:, r, w0:w0 + n], PS[:, b, o:o + n], ACT.Copy,
                        scale=sca[:, s:s + 1]), [t, *(vw if s == 3 else rw), t_vec])
                        for s, w0, n, o in seg]
                    banks.free(b, *ev)
                    toks += ev
                w_users.append(t)
                t_raw[gp, c] = toks[3]
                mvb = mv2[gp % 2]
                for h in range(10):
                    ts = do(DV, lambda e, h=h: e.bn_stats(st6[:, c % 2 * 10 + h, :], raw[:, r, h * 128:(h + 1) * 128]),
                            [toks[-2], state.get(("st", c % 2))])
                for h in range(10):
                    ta = do(DV, lambda e, h=h: e.bn_aggr(mvb[:, c * 10 + h, :], st6[:, c % 2 * 10 + h, :]), [ts])
                state["st", c % 2] = ta
                t_st[gp, c] = ta

            def KX(gp):
                td = Q.dma(SP, [(KV[:], A["wkvx"][gp, :, :, 0:256])], kv_users + t_xq[-1:])
                b, w = banks.take()
                t = do(PE, [lambda e, c=c, k=k, b=b: e.matmul(
                    PS[:, b, c * 256:(c + 1) * 256], ctxT[:, k, c * 128:(c + 1) * 128], KV[:, k, :],
                    start=(k == 0), stop=(k == 1)) for c in range(2) for k in range(2)], [*w, td, t_ctx])
                kv_users[:] = [t]
                tk = do(AC, lambda e, b=b: e.activation(kraw.rearrange("p a b -> p (a b)"), PS[:, b, :], ACT.Copy),
                        [t, *state.get("kraw", t_xq[-1:])])
                banks.free(b, tk)
                mvb = mv2[gp % 2]
                for i in range(4):
                    ts = do(DV, lambda e, i=i: e.bn_stats(st6[:, 20 + i, :], kraw[:, i // 2, (i % 2) * 128:(i % 2 + 1) * 128]), [tk, state.get("st2")])
                for i in range(4):
                    ta = do(DV, lambda e, i=i: e.bn_aggr(mvb[:, 80 + i, :], st6[:, 20 + i, :]), [ts])
                state["kxs", gp] = state["st2"] = ta

            def VX(gp):
                td = Q.dma(SP, [(KV[:], A["wkvx"][gp, :, :, 256:512])], kv_users)
                tv = []
                for j in range(2):
                    b, w = banks.take()
                    t = do(PE, [lambda e, i=i, k=k, b=b: e.matmul(
                        PS[0:64, b, (i % 2) * 256:(i % 2 + 1) * 256], ctxT[:, k, i * 64:(i + 1) * 64], KV[:, k, :],
                        start=(k == 0), stop=(k == 1)) for i in (2 * j, 2 * j + 1) for k in range(2)], [*w, td])
                    tv.append(do(AC, lambda e, b=b, j=j: e.activation(
                        vx[:, 2 * j:2 * j + 2, :].rearrange("p a b -> p (a b)"), PS[0:64, b, :], ACT.Copy),
                        [t, *state.get(("vxu", gp - 1), [])]))
                    banks.free(b, tv[-1])
                kv_users[:] = [t]
                state["vx", gp] = tv

            def SQ(gp):
                m, r = mv2[gp % 2], rs2
                v = m[:, :, 1]
                t = do(DV, lambda e: e.tensor_scalar(v, v, EPS, None, ALU.add),
                       [t_st[gp, 7], state["kxs", gp]])
                t = do(AC, lambda e: e.activation(r[:, :], v, ACT.Sqrt), [t, state.get("rsu")])
                t = do(DV, lambda e: e.reciprocal(r[:, :], r[:, :]), [t])
                state["rs", gp] = newton(r[:, :], v, nt[:, :], t)

            def KT(gp):
                m, r, z = mv2[gp % 2], rs2, kxT
                t = None
                for i in range(4):
                    v = kraw[:, i // 2, (i % 2) * 128:(i % 2 + 1) * 128]
                    t = do(DV, lambda e, v=v, i=i: e.tensor_scalar(v, v, m[:, 80 + i, 0:1], r[:, 80 + i:81 + i],
                                                                   ALU.subtract, ALU.mult), [state["rs", gp]])
                b, w = banks.take()
                tp = do(PE, [lambda e, b=b, i=i: e.transpose(
                    PS[:, b, (i % 2) * 256 + (i // 2) * 128:(i % 2) * 256 + (i // 2) * 128 + 128],
                    kraw[:, i // 2, (i % 2) * 128:(i % 2 + 1) * 128], idf[:, :]) for i in range(4)], [*w, t, t_id])
                state["kraw"] = [tp]
                te = do(AC, lambda e, b=b: e.activation(z[:].rearrange("p a b -> p (a b)"), PS[:, b, :], ACT.Identity,
                                                        scale=ln8[:, 6:7], bias=ln8[:, 7:8]),
                        [tp, *state.get(("kxu", gp - 1), [])])
                banks.free(b, te)
                state["kxT", gp] = te

            def P2(s):
                gp, bb = s // 4, s % 4
                m, r = mv2[gp % 2], rs2
                tn = []
                for c in (2 * bb, 2 * bb + 1):
                    for h in range(10):
                        v = raw[:, slot[gp, c], h * 128:(h + 1) * 128]
                        t = do(DV, lambda e, v=v, c=c, h=h: e.tensor_scalar(
                            v, v, m[:, c * 10 + h, 0:1], r[:, c * 10 + h:c * 10 + h + 1], ALU.subtract, ALU.mult),
                            [state["rs", gp]])
                    tn.append(t)
                state["rsu"] = t
                te = []
                for j in range(5):
                    b, w = banks.take()
                    fns = []
                    for hh in range(2):
                        for ci in range(2):
                            fns.append(lambda e, b=b, hh=hh, ci=ci, j=j: e.transpose(
                                PS[:, b, hh * 256 + ci * 128:hh * 256 + ci * 128 + 128],
                                raw[:, slot[gp, 2 * bb + ci], (2 * j + hh) * 128:(2 * j + hh + 1) * 128], idf[:, :]))
                    tp = do(PE, fns, [*w, *tn])
                    dst = (qT, qT, qxT, qxT, kT)[j][s % 2]
                    o = (0, 2, 0, 2, 0)[j]
                    v = (0, 0, 4, 4, 2)[j]
                    te.append(do(AC, lambda e, b=b, dst=dst, o=o, v=v: e.activation(
                        dst[:, o:o + 2, :].rearrange("p a b -> p (a b)"), PS[:, b, :], ACT.Identity,
                        scale=ln8[:, v:v + 1], bias=ln8[:, v + 1:v + 2]), [tp, *t_l8, *state.get(("qu", s - 2), [])]))
                    banks.free(b, te[-1])
                for c in (2 * bb, 2 * bb + 1):
                    raws.free(slot[gp, c], tp)
                state["qT", s] = te

            def a_self(u):
                s, g = u
                gp, bb = s // 4, s % 4
                q_, k_ = qT[s % 2], kT[s % 2]
                i, w = smr.take()
                te = []
                for h in range(2):
                    b, bw = banks.take()
                    t = do(PE, [lambda e, b=b, h=h, c=c: e.matmul(
                        PS[:, b, c * 256:(c + 1) * 256], q_[:, 2 * g + h, c * 128:(c + 1) * 128], k_[:, g, :],
                        start=True, stop=True) for c in range(2)], [*bw, *state["qT", s]])
                    tm = do(DV, lambda e, b=b, h=h: e.tensor_reduce(
                        sm[i][:, 0, 2 * h:2 * h + 2], PS[:, b, :].rearrange("p (c t) -> p c t", c=2), X, ALU.max,
                        negate=True), [t, *w])
                    for c in range(2):
                        x_ = do(AC, lambda e, b=b, h=h, c=c: e.activation(
                            P[i][:, 2 * h + c, :], PS[:, b, c * 256:(c + 1) * 256], ACT.Exp,
                            bias=sm[i][:, 0, 2 * h + c:2 * h + c + 1], accum_out=sm[i][:, 1, 2 * h + c:2 * h + c + 1]), [tm, *w])
                    te.append(x_)
                    banks.free(b, x_)
                state.setdefault(("qu", s), []).append(t)
                tr = do(DV, lambda e: e.reciprocal(sm[i][:, 2, 0:4], sm[i][:, 1, 0:4]), te)
                for j in range(4):
                    tn = do(DV, lambda e, j=j: e.tensor_scalar(P[i][:, j, :], P[i][:, j, :], sm[i][:, 2, j:j + 1], None,
                                                               ALU.mult), [tr])
                return i, tn

            def b_self(u, st_):
                i, tn = st_
                z, zw = ptr.take()
                te = []
                for tc in range(2):
                    b, bw = banks.take()
                    t = do(PE, [lambda e, b=b, j=j, tc=tc: e.transpose(
                        PS[:, b, j * 128:(j + 1) * 128], P[i][:, j, tc * 128:(tc + 1) * 128], idf[:, :])
                        for j in range(4)], [*bw, tn])
                    if tc:
                        x_ = do(AC, lambda e, b=b: e.activation(PT[z][:, 1, :], PS[:, b, :], ACT.Copy), [t, *zw])
                    else:
                        x_ = do(DV, lambda e, b=b: e.tensor_copy(PT[z][:, 0, :], PS[:, b, :]), [t, *zw])
                    te.append(x_)
                    banks.free(b, x_)
                smr.free(i, t)
                return z, te

            def c_self(u, st_):
                s, g = u
                gp, bb = s // 4, s % 4
                z, te = st_
                y, yw = state["y", s]
                b, bw = banks.take()
                t = do(PE, [lambda e, b=b, tc=tc: e.matmul(
                    PS[:, b, :], vr[:, vslot[gp, 2 * bb + tc], g * 128:(g + 1) * 128], PT[z][:, tc, :],
                    start=(tc == 0), stop=(tc == 1)) for tc in range(2)],
                    [*bw, *te, t_raw[gp, 2 * bb], t_raw[gp, 2 * bb + 1]])
                ptr.free(z, t)
                for h in range(2):
                    k = 8 * gp + 2 * g + h
                    x_ = do(AC, lambda e, b=b, h=h, k=k: e.activation(
                        yT[:, 2 * g + h, :], PS[:, b, h * 256:(h + 1) * 256], ACT.Copy, scale=ismo[:, k:k + 1]),
                        [t, t_is, *yw])
                banks.free(b, x_)
                state.setdefault(("yt", s), []).append(x_)
                if g == 1:
                    for c in (2 * bb, 2 * bb + 1):
                        vrs.free(vslot[gp, c], t)

            def a_cross(u):
                s, _ = u
                gp, bb = s // 4, s % 4
                q_ = qxT[s % 2]
                i, w = smr.take()
                b, bw = banks.take()
                t = do(PE, [lambda e, b=b, h=h, c=c: e.matmul(
                    PS[:, b, (2 * h + c) * 64:(2 * h + c + 1) * 64], q_[:, h, c * 128:(c + 1) * 128],
                    kxT[:, h // 2, bb * 64:(bb + 1) * 64], start=True, stop=True)
                    for h in range(4) for c in range(2)], [*bw, *state["qT", s], state["kxT", gp]])
                state.setdefault(("qu", s), []).append(t)
                state.setdefault(("kxu", gp), []).append(t)
                pf = P[i][:].rearrange("p a b -> p (a b)")[:, 0:512]
                p3 = pf.rearrange("p (j t) -> p j t", t=64)
                ps3 = PS[:, b, :].rearrange("p (j t) -> p j t", t=64)
                tm = do(DV, lambda e: e.tensor_reduce(sm[i][:, 0, :], ps3, X, ALU.max), [t, *w])
                ts = do(DV, lambda e: e.tensor_tensor(p3, ps3, sm[i][:, 0, :].unsqueeze(2).to_broadcast([128, 8, 64]),
                                                      ALU.subtract), [tm, *w])
                banks.free(b, ts)
                tx = do(AC, lambda e: e.activation(pf, pf, ACT.Exp), [ts])
                tm = do(DV, lambda e: e.tensor_reduce(sm[i][:, 1, :], p3, X, ALU.add), [tx])
                tr = do(DV, lambda e: e.reciprocal(sm[i][:, 2, :], sm[i][:, 1, :]), [tm])
                tn = do(DV, lambda e: e.tensor_tensor(p3, p3, sm[i][:, 2, :].unsqueeze(2).to_broadcast([128, 8, 64]),
                                                      ALU.mult), [tr])
                return i, tn

            def b_cross(u, st_):
                i, tn = st_
                z, zw = ptr.take()
                te = []
                for g in range(2):
                    b, bw = banks.take()
                    t = do(PE, [lambda e, b=b, j=j, g=g: e.transpose(
                        PS[0:64, b, j * 128:(j + 1) * 128], P[i][:].rearrange("p a b -> p (a b)")[:, (4 * g + j) * 64:(4 * g + j + 1) * 64],
                        idf[:, :]) for j in range(4)], [*bw, tn])
                    if g:
                        x_ = do(AC, lambda e, b=b: e.activation(PT[z][0:64, 1, :], PS[0:64, b, :], ACT.Copy), [t, *zw])
                    else:
                        x_ = do(DV, lambda e, b=b: e.tensor_copy(PT[z][0:64, 0, :], PS[0:64, b, :]), [t, *zw])
                    te.append(x_)
                    banks.free(b, x_)
                smr.free(i, t)
                return z, te

            def c_cross(u, st_):
                s, _ = u
                gp, bb = s // 4, s % 4
                z, te = st_
                y, yw = state["y", s]
                for g in range(2):
                    b, bw = banks.take()
                    t = do(PE, lambda e, b=b, g=g: e.matmul(
                        PS[:, b, :], vx[:, bb, g * 128:(g + 1) * 128], PT[z][0:64, g, :], start=True, stop=True),
                        [*bw, *te, *state["vx", gp]])
                    for h in range(2):
                        k = 8 * gp + 4 + 2 * g + h
                        x_ = do(AC, lambda e, b=b, h=h, k=k, g=g: e.activation(
                            yT[:, 4 + 2 * g + h, :], PS[:, b, h * 256:(h + 1) * 256], ACT.Copy, scale=ismo[:, k:k + 1]),
                            [t, t_is, *yw])
                    banks.free(b, x_)
                ptr.free(z, t)
                state.setdefault(("vxu", gp), []).append(t)
                state.setdefault(("yt", s), []).append(x_)

            def QO(s):
                y, _ = state["y", s]
                ts = []
                for a in range(2):
                    t = quant(yT[:, 4 * a:4 * a + 4, :].rearrange("p a b -> p (a b)"), yF, yt,
                              cat[:, 4 * a:4 * a + 4, :].rearrange("p a b -> p (a b)"), state["yt", s],
                              state.get("catu", []) + state.get("yF", t_xq[-1:]))
                    state["yF"] = [t]
                    ts.append(t)
                yr.free(y, t)
                state["cat", s] = t

            def OP(s):
                gp, bb = s // 4, s % 4
                b, w = banks.take()
                t = do(PE, [lambda e, b=b, c=c, j=j, W=W: e.matmul(
                    PS[:, b, c * 256:(c + 1) * 256], cat[:, j, c * 128:(c + 1) * 128], W[:, j, :],
                    start=(j == 0 and W is PH), stop=(j == 7 and W is PL))
                    for c in range(2) for j in range(8) for W in (PH, PL)], [*w, state["cat", s], *state["p", gp]])
                state["catu"] = [t]
                if bb == 3:
                    p_users.append(t)
                xv = xt[:, 2 * bb:2 * bb + 2, :].rearrange("p a b -> p (a b)")
                tx = do(DV, lambda e, b=b: e.scalar_tensor_tensor(xv, PS[:, b, :], sproj[:, 0:1], xv, ALU.mult, ALU.add),
                        [t, t_sp, t_h0[-1]] + state.get(("x", bb), []))
                banks.free(b, tx)
                state["x", bb] = [tx]

            state["w", 0] = load_w(0)
            state["p", 0] = load_p(0)
            KX(0)
            VX(0)
            for c in range(8):
                P1(0, c)
            SQ(0)
            KT(0)
            P2(0)
            state["w", 1] = load_w(1)
            pend_a, pend_b = [], []

            def flow(kind, u):
                if pend_b:
                    k_, u_, st_ = pend_b.pop(0)
                    (c_self if k_ == "s" else c_cross)(u_, st_)
                if pend_a:
                    k_, u_, st_ = pend_a.pop(0)
                    pend_b.append((k_, u_, (b_self if k_ == "s" else b_cross)(u_, st_)))
                if kind:
                    pend_a.append((kind, u, (a_self if kind == "s" else a_cross)(u)))

            for s in range(16):
                gp, bb = s // 4, s % 4
                flow("s", (s, 0))
                if gp < 3:
                    if bb == 0:
                        KX(gp + 1)
                    P1(gp + 1, 2 * bb)
                flow("s", (s, 1))
                if bb == 0 and s:
                    VX(gp)
                if s:
                    QO(s - 1)
                if gp < 3:
                    P1(gp + 1, 2 * bb + 1)
                if bb == 3 and gp < 3:
                    if gp < 2:
                        state["w", gp + 2] = load_w(gp + 2)
                    SQ(gp + 1)
                state["y", s] = yr.take()
                flow("c", (s, 0))
                if bb == 3 and gp < 3:
                    KT(gp + 1)
                if s < 15:
                    P2(s + 1)
                if s:
                    OP(s - 1)
                if bb == 0 and gp:
                    state["p", gp] = load_p(gp)
            flow(None, None)
            flow(None, None)
            QO(15)
            OP(15)

        def fence(tokens):
            for e in (PE, AC, DV, PO, SP):
                Q.wait(e, tokens)

        def split(src, hi, lo, ready, users, eh=AC, el=DV):
            if eh == AC:
                th = do(AC, lambda e: e.activation(hi, src, ACT.Copy), [*ready, *users])
            else:
                th = do(eh, lambda e: e.tensor_copy(hi, src), [*ready, *users])
            tl = do(el, lambda e: e.tensor_tensor(lo, src, hi.bitcast(F32), ALU.subtract), [*ready, th, *users])
            return [th, tl]

        def split_turn(t_src, hi, lo, toks):
            def ev(k, h, b, t):
                ts = split(PS[:, b, :], hi[:, k, h * 512:(h + 1) * 512], lo[:, k, h * 512:(h + 1) * 512], [t], [])
                toks.extend(ts)
                return ts[1]
            turn(xn, t_src, ev)

        def gated(c, xh, xl, tx, ntile, tile, gate, t_extra, name):
            r4 = Ring(4)
            sg = [sb(f"{name}sg{i}", [128, 512], F32, c) for i in range(2)]
            hf = [sb(f"{name}hf{i}", [128, 512], F32, c) for i in range(2)]
            hh = [sb(f"{name}hh{i}", [128, 512], FR, c) for i in range(2)]
            hl = [sb(f"{name}hl{i}", [128, 512], FR, c) for i in range(2)]
            hr = Ring(2)
            pend = []
            done = []

            def down(last):
                j, h, i, t_h, W, tw, release = pend.pop(0)
                fns = []
                for cc in range(4):
                    ch = 4 * h + cc
                    for p, (a, w) in enumerate(((hh, 0), (hh, 1), (hl, 0))):
                        fns.append(lambda e, a=a, w=w, ch=ch, cc=cc, p=p: e.matmul(
                            PS[:, 4 + ch // 2, ch % 2 * 256:ch % 2 * 256 + 256], a[i][:, cc * 128:(cc + 1) * 128],
                            W[2 + w], start=(j == 0 and p == 0 and ch % 2 == 0), stop=(last and p == 2),
                            skip_group_check=True))
                t = do(PE, fns, [*t_h, *tw])
                hr.free(i, t)
                release(t)
                return t

            for j in range(ntile):
                W, tw, rel = tile(j)
                for h in range(2):
                    cols = slice(h * 512, (h + 1) * 512)
                    bs = []
                    for gu in range(2):
                        b, w = r4.take()
                        fns = []
                        n = 0
                        for k in range(2):
                            for wi, a in ((0, xh), (0, xl), (1, xh)):
                                fns.append(lambda e, b=b, k=k, wi=wi, a=a, n=n, gu=gu, W=W, cols=cols: e.matmul(
                                    PS[:, b, :], W[wi][:, gu, k, :], a[:, k, cols], start=(n == 0), stop=(n == 5)))
                                n += 1
                        bs.append((b, do(PE, fns, [*w, *tx, *tw])))
                    i, hw = hr.take()
                    (bg, tg), (bu, tu) = bs
                    t_h = gate(j, h, i, bg, tg, bu, tu, r4, sg, hf, hh, hl, hw)
                    if pend:
                        done = down(False)
                    pend.append((j, h, i, t_h, W, tw, rel if h == 1 else (lambda t: None)))
            t = down(True)
            return t

        end = [state["x", bb][0] for bb in range(4)] 
        c1 = ExitStack()
        with c1:
            if stages > 1:
                fence([*end, (Q.sem[PO], Q.n[PO])] if Q.n.get(PO) else end)
                banks = Ring(8)
                xh = sb("m_xh", [128, 2, 1024], FR, c1)
                xl = sb("m_xl", [128, 2, 1024], FR, c1)
                cst = sb("m_cst", [128, 32 + 4], F32, c1)
                idb = sb("m_idb", [128, 128], BF, c1)
                sel = sb("m_sel", [96, 3072], BF, c1)
                gst = sb("m_gst", [128, 64], F32, c1)
                gh = sb("m_gh", [128, 2, 32], FR, c1)
                gl = sb("m_gl", [128, 2, 32], FR, c1)
                bd = sb("m_bd", [128, 128], F32, c1)
                pr = sb("m_pr", [128, 8, 32], F32, c1)
                s8 = sb("m_s8", [128, 8], F32, c1)
                v8 = sb("m_v8", [128, 8, 8], F32, c1)
                i8 = sb("m_i8", [128, 8, 8], U32, c1)
                i8f = sb("m_i8f", [128, 64], F32, c1)
                OH = sb("m_OH", [128, 64, 32], F32, c1)
                OT = sb("m_OT", [128, 8, 128], F32, c1)
                RR = sb("m_RR", [128, 8, 128], F32, c1)
                tmp = [sb(f"m_tmp{i}", [128, 512], F32, c1) for i in range(2)]
                cand = sb("m_cand", [128, 32, 4], F32, c1)
                best = sb("m_best", [128, 32], F32, c1)
                e4 = sb("m_e4", [128, 32, 4], F32, c1)
                fi = sb("m_fi", [128, 32], F32, c1)
                ge = sb("m_ge", [128, 32], F32, c1)
                wa = sb("m_wa", [128, 32], F32, c1)
                co = sb("m_co", [128, 8, 8], F32, c1)
                ac_ = sb("m_ac", [128, 8, 4], F32, c1)
                cw = sb("m_cw", [128, 8, 32], F32, c1)
                c3 = sb("m_c3", [128, 8, 96], BF, c1)
                cwT = sb("m_cwT", [96, 1024], BF, c1)
                NW = 3
                ws = [sb(f"m_ws{i}", [128, 2, 2, 128], F32, c1) for i in range(NW)]
                wh = [sb(f"m_wh{i}", [128, 2, 2, 128], FR, c1) for i in range(NW)]
                wl = [sb(f"m_wl{i}", [128, 2, 2, 128], FR, c1) for i in range(NW)]
                ds = [sb(f"m_ds{i}", [128, 256], F32, c1) for i in range(NW)]
                dh = [sb(f"m_dh{i}", [128, 256], FR, c1) for i in range(NW)]
                dl = [sb(f"m_dl{i}", [128, 256], FR, c1) for i in range(NW)]
                wr = Ring(NW)
                t_g = Q.dma(SP, [(gst[:], A["gate"]), (cst[:], A["cst"]), (idb[:], A["idb"]), (sel[:], A["sel"])])
                t_z = do(DV, lambda e: e.memset(bd[:], 0.0))
                t_bd = Q.dma(SP, [(bd[32 * j:32 * j + 32, 32 * j:32 * j + 32], A["sim"]) for j in range(4)], [t_z])
                iota, i48 = cst[:, 0:32], cst[:, 32:36]

                t_n = layernorm(xt, end[-1], xn)
                tx = []
                split_turn(t_n, xh, xl, tx)
                tgs = split(gst[:], gh[:].rearrange("p a b -> p (a b)"), gl[:].rearrange("p a b -> p (a b)"), [t_g], [])
                t = do(DV, lambda e: e.scalar_tensor_tensor(tmp[0][:, 0:128], idf[:, :], -1.0, bd[:], ALU.mult, ALU.mult), [t_bd, t_id])
                t = do(DV, lambda e: e.tensor_tensor(bd[:], bd[:], tmp[0][:, 0:128], ALU.add), [t])
                t_bd = do(DV, lambda e: e.tensor_tensor(bd[:], bd[:], idf[:, :], ALU.add), [t])
                b, w = banks.take()
                fns = []
                for c in range(8):
                    n = 0
                    for k in range(2):
                        for a, g_ in ((xh, gh), (xh, gl), (xl, gh)):
                            fns.append(lambda e, c=c, k=k, a=a, g_=g_, n=n, b=b: e.matmul(
                                PS[:, b, c * 32:(c + 1) * 32], a[:, k, c * 128:(c + 1) * 128], g_[:, k, :],
                                start=(n == 0), stop=(n == 5)))
                            n += 1
                t = do(PE, fns, [*w, *tx, *tgs])
                lg = PS[:, b, 0:256].rearrange("p (c n) -> p c n", n=32)
                up = lambda ap, n: ap.unsqueeze(2).to_broadcast([128, ap.shape[1], n])
                tm = do(DV, lambda e: e.tensor_reduce(s8[:], lg, X, ALU.max), [t])
                t = do(DV, lambda e: e.tensor_tensor(pr[:], lg, up(s8[:], 32), ALU.subtract), [tm])
                banks.free(b, t)
                t = do(AC, lambda e: e.activation(pr[:], pr[:], ACT.Exp), [t])
                t = do(DV, lambda e: e.tensor_reduce(s8[:], pr[:], X, ALU.add), [t])
                t = do(DV, lambda e: e.reciprocal(s8[:], s8[:]), [t])
                t = do(DV, lambda e: e.tensor_tensor(pr[:], pr[:], up(s8[:], 32), ALU.mult), [t])
                for c in range(8):
                    tv = do(DV, lambda e, c=c: e.max(v8[:, c, :], pr[:, c, :]), [t])
                for c in range(8):
                    ti = do(DV, lambda e, c=c: e.max_index(i8[:, c, :], v8[:, c, :], pr[:, c, :]), [tv])
                t = do(DV, lambda e: e.tensor_copy(i8f[:], i8[:].rearrange("p a b -> p (a b)")), [ti])
                t_oh = do(DV, lambda e: e.tensor_tensor(OH[:], up(i8f[:], 32),
                                                        iota.unsqueeze(1).to_broadcast([128, 64, 32]), ALU.is_equal), [t, t_g])
                t = do(DV, lambda e: e.tensor_reduce(s8[:], v8[:], X, ALU.add), [tv])
                t = do(DV, lambda e: e.tensor_scalar(s8[:], s8[:], 1e-12, None, ALU.max), [t])
                t = do(DV, lambda e: e.reciprocal(s8[:], s8[:]), [t])
                t_wt = do(DV, lambda e: e.tensor_tensor(v8[:], v8[:], up(s8[:], 8), ALU.mult), [t, ti])
                te = []
                for hh_ in range(2):
                    b, w = banks.take()
                    t = do(PE, [lambda e, b=b, c=c: e.transpose(
                        PS[:, b, c % 4 * 128:c % 4 * 128 + 128], OH[:, c * 8 + 4:c * 8 + 8, :].rearrange("p a b -> p (a b)"),
                        idf[:, :]) for c in range(4 * hh_, 4 * hh_ + 4)], [*w, t_oh, t_id])
                    te.append(do(AC, lambda e, b=b, hh_=hh_: e.activation(
                        OT[:, 4 * hh_:4 * hh_ + 4, :].rearrange("p a b -> p (a b)"), PS[:, b, :], ACT.Copy), [t]))
                    banks.free(b, te[-1])
                tr = []
                for hh_ in range(2):
                    b, w = banks.take()
                    t = do(PE, [lambda e, b=b, c=c: e.matmul(
                        PS[:, b, c % 4 * 128:c % 4 * 128 + 128], OT[:, c, :], bd[:], start=True, stop=True)
                        for c in range(4 * hh_, 4 * hh_ + 4)], [*w, te[hh_], t_bd])
                    tr.append(do(AC, lambda e, b=b, hh_=hh_: e.activation(
                        RR[:, 4 * hh_:4 * hh_ + 4, :].rearrange("p a b -> p (a b)"), PS[:, b, :], ACT.Copy), [t]))
                    banks.free(b, tr[-1])
                tc_ = [None, None]
                for c in range(8):
                    tt = tmp[c % 2][:].rearrange("p (j i e) -> p j i e", j=4, i=4)
                    r_ = RR[:, c, :].rearrange("p (j e) -> p j e", j=4).unsqueeze(2).to_broadcast([128, 4, 4, 32])
                    o_ = OH[:, c * 8:c * 8 + 4, :].unsqueeze(1).to_broadcast([128, 4, 4, 32])
                    t = do(DV, lambda e, tt=tt, r_=r_, o_=o_: e.tensor_tensor(tt, r_, o_, ALU.mult),
                           [tr[c // 4], t_oh, t_bd, tc_[c % 2]])
                    tc_[c % 2] = do(DV, lambda e, c=c: e.tensor_reduce(
                        cand[:, c * 4:c * 4 + 4, :].rearrange("p a b -> p (a b)"), tmp[c % 2][:].rearrange("p (q e) -> p q e", e=32), X, ALU.add), [t])
                t = do(DV, lambda e: e.tensor_reduce(best[:], cand[:], X, ALU.max), [tc_[1]])
                i4b = i48.unsqueeze(1).to_broadcast([128, 32, 4])
                tb = t
                t = do(DV, lambda e: e.tensor_tensor(e4[:], cand[:], up(best[:], 4), ALU.is_equal), [tb])
                t = do(DV, lambda e: e.tensor_tensor(e4[:], e4[:], i4b, ALU.mult), [t])
                t = do(DV, lambda e: e.tensor_reduce(fi[:], e4[:], X, ALU.min), [t])
                t = do(DV, lambda e: e.tensor_tensor(e4[:], up(fi[:], 4), i4b, ALU.is_equal), [t])
                v3 = v8[:, :, 4:8]
                ge3, wa3 = ge[:].rearrange("p (c j) -> p c j", j=4), wa[:].rearrange("p (c j) -> p c j", j=4)
                tg_ = do(DV, lambda e: e.tensor_scalar(ge[:], best[:], 0.5, None, ALU.is_ge), [tb])
                ta = do(DV, lambda e: e.tensor_tensor(wa3, v3, ge3, ALU.mult), [tg_, t_wt])
                t2 = do(DV, lambda e: e.tensor_tensor(co[:, :, 4:8], v3, wa3, ALU.subtract), [ta])
                t = do(DV, lambda e: e.tensor_tensor(e4[:], e4[:], up(wa[:], 4), ALU.mult), [t, ta])
                t = do(DV, lambda e: e.tensor_reduce(ac_[:], e4[:].rearrange("p (c j) i -> p c i j", j=4), X, ALU.add), [t])
                t = do(DV, lambda e: e.tensor_tensor(co[:, :, 0:4], v8[:, :, 0:4], ac_[:], ALU.add), [t])
                t = do(DV, lambda e: e.tensor_tensor(OH[:], OH[:], up(co[:].rearrange("p a b -> p (a b)"), 32), ALU.mult), [t, t2])
                t = do(DV, lambda e: e.tensor_reduce(cw[:], OH[:].rearrange("p (c r) e -> p c e r", r=8), X, ALU.add), [t])
                for z in range(3):
                    cz = c3[:, :, 32 * z:32 * z + 32]
                    t = do(DV, lambda e, cz=cz: e.tensor_copy(cz, cw[:]), [t])
                    if z < 2:
                        t = do(DV, lambda e, cz=cz: e.tensor_tensor(cw[:], cw[:], cz, ALU.subtract), [t])
                b, w = banks.take()
                pb = PS[0:96, b, :].bitcast(BF)
                t = do(PE, [lambda e, c=c, pb=pb: e.transpose(pb[:, c * 128:(c + 1) * 128], c3[:, c, :], idb[:, :])
                            for c in range(8)], [*w, t, t_g])
                t_cw = do(AC, lambda e, pb=pb: e.activation(cwT[:], pb, ACT.Copy), [t])
                fence([t_cw])

                def moe_tile(j):
                    i, users = wr.take()
                    td = Q.dma(SP, [(ws[i][:], A["wgu"][j])], users)
                    te_ = Q.dma(SP, [(ds[i][:], A["wdn"][j])])
                    t1 = split(ws[i][:], wh[i][:], wl[i][:], [td], users)
                    t2 = split(ds[i][:], dh[i][:], dl[i][:], [te_], users, eh=PO, el=PO)
                    toks = [*t1, *t2]
                    return (wh[i], wl[i], dh[i][:], dl[i][:]), toks, lambda t, i=i, toks=toks: wr.free(i, t, *toks)

                def moe_gate(j, h, i, bg, tg, bu, tu, r4, sg, hf, hh, hl, hw):
                    b, w = r4.take()
                    tcb = do(PE, lambda e: e.matmul(PS[:, b, :], sel[:, j * 128:(j + 1) * 128],
                                                    cwT[:, h * 512:(h + 1) * 512], start=True, stop=True), w)
                    ts = do(AC, lambda e: e.activation(sg[i][:], PS[:, bg, :], ACT.Silu), [tg, *hw])
                    r4.free(bg, ts)
                    t = do(DV, lambda e: e.tensor_tensor(sg[i][:], sg[i][:], PS[:, bu, :], ALU.mult), [ts, tu])
                    r4.free(bu, t)
                    t = do(DV, lambda e: e.tensor_tensor(hf[i][:], sg[i][:], PS[:, b, :], ALU.mult), [t, tcb, *hw])
                    r4.free(b, t)
                    return split(hf[i][:], hh[i][:], hl[i][:], [t], hw)

                t_y = gated(c1, xh, xl, tx, 24, moe_tile, moe_gate, [], "m_")
                end = [do(DV, lambda e, j=j: e.tensor_tensor(
                    xt[:, 2 * j:2 * j + 2, :].rearrange("p a b -> p (a b)"), PS[:, 4 + j, :],
                    xt[:, 2 * j:2 * j + 2, :].rearrange("p a b -> p (a b)"), ALU.add), [t_y]) for j in range(4)]

        c2 = ExitStack()
        with c2:
            if stages > 2:
                fence(end)
                banks = Ring(8)
                fi_ = [sb(f"f_i{i}", [128, 512], I32, c2) for i in range(2)]
                ff_ = [sb(f"f_f{i}", [128, 512], F32, c2) for i in range(2)]
                fh = sb("f_h", [128, 6, 512], FR, c2)
                fl = sb("f_l", [128, 6, 512], FR, c2)
                fdh = sb("f_dh", [128, 6, 256], FR, c2)
                fdl = sb("f_dl", [128, 6, 256], FR, c2)
                t_fw = []
                fr = Ring(2)
                for j in range(9):
                    i, w = fr.take()
                    if j < 6:
                        src, hi, lo = A["fgu"][j], fh[:, j, :], fl[:, j, :]
                    else:
                        q_ = 2 * (j - 6)
                        src, hi, lo = A["fdn"][:, q_ * 256:q_ * 256 + 512], fdh[:, q_:q_ + 2, :].rearrange("p a b -> p (a b)"), \
                            fdl[:, q_:q_ + 2, :].rearrange("p a b -> p (a b)")
                    td = Q.dma(SP, [(fi_[i][:], src)], w)
                    t = do(PO, lambda e, i=i: e.tensor_scalar(ff_[i][:], fi_[i][:], -128.0, None, ALU.add), [td, *w])
                    ts = split(ff_[i][:], hi, lo, [t], [], eh=PO, el=PO)
                    fr.free(i, *ts)
                    t_fw.append(ts[1])
                fsc = sb("f_sc", [128, 12 + 256], F32, c2)
                t_fs = Q.dma(SP, [(fsc[:], A["fsc"])])

                cl = ExitStack()
                with cl:
                    def sl(name, shape, dt=F32):
                        return sb("l_" + name, shape, dt, cl)
                    x2T = sl("x2T", [128, 2, 1024])
                    wdq = sl("wdq", [128, 2, 96])
                    wkvc = sl("wkvc", [128, 2, 64])
                    wuq = sl("wuq", [128, 16, 96])
                    wuk = sl("wuk", [128, 16, 64])
                    wuv = sl("wuv", [128, 16, 64])
                    wo = sl("wo", [128, 16, 256])
                    aw = sl("aw", [96, 16, 128])
                    wrt = sl("wrt", [96, 1024])
                    wkr = sl("wkr", [64, 2, 128])
                    tb_ = sl("tb", [128, 512 + 128 + 64])
                    seg = sl("seg", [128, 8], I32)
                    segf = sl("segf", [128, 8])
                    dd = sl("dd", [128, 8, 64])
                    mk = sl("mk", [128, 8, 64])
                    td1 = Q.dma(AC, [(wdq[:], A["wdq"]), (wkvc[:], A["wkvc"]), (wkr[:], A["wkr"]), (tb_[:], A["rope"]), (seg[:], A["seg"])])
                    td2 = Q.dma(AC, [(wuq[:], A["wuq"]), (wuk[:], A["wuk"]), (aw[:, :, 64:128], A["wqr"]), (wrt[:], A["wrt"])])
                    td3 = Q.dma(AC, [(wuv[:], A["wuv"]), (wo[:], A["wo"])])
                    qcT = sl("qcT", [96, 1024])
                    KA = sl("KA", [128, 256])
                    K2 = sl("K2", [128, 256])
                    kt = sl("kt", [128, 2, 256])
                    KZ = sl("KZ", [128, 4, 2, 64])
                    BDK = sl("BDK", [128, 4, 128])
                    Bp = sl("Bp", [128, 8, 256])
                    QA = [sl(f"QA{i}", [128, 16, 256]) for i in range(2)]
                    QB = [sl(f"QB{i}", [128, 8, 256]) for i in range(2)]
                    S = [sl(f"S{i}", [128, 1024]) for i in range(2)]
                    s16 = [sl(f"s16{i}", [128, 2, 16]) for i in range(2)]
                    PT1 = sl("PT", [128, 8, 256])
                    CT = x2T[:].rearrange("p k (a t) -> p (k a) t", t=256)

                    t = do(DV, lambda e: e.tensor_copy(segf[:], seg[:]), [td1])
                    t = do(DV, lambda e: e.tensor_tensor(dd[:], segf[:].unsqueeze(2).to_broadcast([128, 8, 64]),
                                                         tb_[:, 640:704].unsqueeze(1).to_broadcast([128, 8, 64]), ALU.subtract), [t])
                    t = do(DV, lambda e: e.tensor_scalar(mk[:], dd[:], 0.0, None, ALU.is_ge), [t])
                    t = do(DV, lambda e: e.scalar_tensor_tensor(mk[:], dd[:], 8.0, mk[:], ALU.is_le, ALU.mult), [t])
                    t_mk = do(DV, lambda e: e.tensor_scalar(mk[:], mk[:], NEG, -NEG, ALU.mult, ALU.add), [t])
                    tz1 = do(DV, lambda e: e.memset(KZ[:], 0.0))
                    tz2 = do(DV, lambda e: e.memset(BDK[:], 0.0))

                    b, w = banks.take()
                    t = do(PE, [lambda e, b=b, k=k: e.matmul(PS[0:64, b, 0:256], wkvc[:, k, :], ctxT[:, k, :],
                                                             start=(k == 0), stop=(k == 1)) for k in range(2)], [*w, td1, t_ctx])
                    t_ka = do(AC, lambda e, b=b: e.activation(KA[0:64, :], PS[0:64, b, 0:256], ACT.Copy), [t])
                    banks.free(b, t_ka)
                    b, w = banks.take()
                    t = do(PE, [lambda e, b=b, bb=bb, k=k, o=o: e.matmul(
                        PS[o:o + 64, b, bb * 64:(bb + 1) * 64], ctxT[:, k, bb * 64:(bb + 1) * 64], wkvc[:, k, :],
                        start=(k == 0), stop=(k == 1)) for o in (0, 64) for bb in range(4) for k in range(2)], [*w])
                    for o in (0, 64):
                        t_bk = do(AC, lambda e, b=b, o=o: e.activation(
                            BDK[o:o + 64, :, o:o + 64], PS[o:o + 64, b, 0:256].rearrange("p (a c) -> p a c", a=4), ACT.Copy), [t, tz2])
                    banks.free(b, t_bk)
                    b, w = banks.take()
                    t = do(PE, [lambda e, b=b, z=z: e.matmul(PS[:, b, z * 256:(z + 1) * 256], wkr[:, z, :], KA[0:64, :],
                                                             start=True, stop=True) for z in range(2)], [*w, t_ka])
                    tk_ = [do(DV, lambda e, b=b, z=z: e.tensor_tensor(
                        kt[:, z, :].rearrange("p (a t) -> p a t", a=4), PS[:, b, z * 256:(z + 1) * 256].rearrange("p (a t) -> p a t", a=4),
                        tb_[:, 512 + 64 * z:576 + 64 * z].unsqueeze(1).to_broadcast([128, 4, 64]), ALU.mult), [t, td1]) for z in range(2)]
                    banks.free(b, *tk_)
                    t = do(DV, lambda e: e.tensor_tensor(K2[:], kt[:, 0, :], kt[:, 1, :], ALU.add), tk_)
                    t_kz = [do(AC, lambda e, o=o: e.activation(
                        KZ[o:o + 64, :, o // 64, :], kt[o:o + 64, 0, :].rearrange("p (a t) -> p a t", a=4), ACT.Copy), [t, tz1])
                        for o in ()]
                    k23 = K2[:].rearrange("p (a t) -> p a t", a=4)
                    t_kz += [do(AC, lambda e, o=o: e.activation(KZ[o:o + 64, :, o // 64, :], k23[o:o + 64], ACT.Copy), [t, tz1])
                             for o in (0, 64)]
                    t_kz.append(do(AC, lambda e: e.activation(KA[64:128, :], K2[64:128, :], ACT.Copy), [t]))
                    t_kz.append(t_ka)

                    t_aw = []
                    for z in range(2):
                        b, w = banks.take()
                        t = do(PE, [lambda e, b=b, h=h: e.matmul(PS[0:96, b, h % 8 * 64:h % 8 * 64 + 64], wuq[:, h, :], wuk[:, h, :],
                                                                 start=True, stop=True) for h in range(8 * z, 8 * z + 8)], [*w, td2])
                        t_aw.append(do(AC, lambda e, b=b, z=z: e.activation(
                            aw[:, 8 * z:8 * z + 8, 0:64], PS[0:96, b, :].rearrange("p (h c) -> p h c", h=8), ACT.Copy), [t]))
                        banks.free(b, t_aw[-1])
                    t_bp = []
                    for z in range(4):
                        b, w = banks.take()
                        t = do(PE, [lambda e, b=b, p=p, o=o: e.matmul(
                            PS[64 * o:64 * o + 64, b, p % 2 * 256:p % 2 * 256 + 256], wuv[:, 2 * p + o, :], wo[:, 2 * p + o, :],
                            start=True, stop=True) for o in range(2) for p in (2 * z, 2 * z + 1)], [*w, td3])
                        t_bp.append(do(AC, lambda e, b=b, z=z: e.activation(
                            Bp[:, 2 * z:2 * z + 2, :].rearrange("p a b -> p (a b)"), PS[:, b, :], ACT.Copy), [t]))
                        banks.free(b, t_bp[-1])

                    t_n = layernorm(xt, end[-1], xn)
                    t_x2 = []

                    def ev2(k, h, b, t):
                        t = do(AC, lambda e: e.activation(x2T[:, k, h * 512:(h + 1) * 512], PS[:, b, :], ACT.Copy), [t])
                        t_x2.append(t)
                        return t
                    turn(xn, t_n, ev2)
                    t_qc = []
                    for h in range(2):
                        b, w = banks.take()
                        t = do(PE, [lambda e, b=b, k=k, h=h: e.matmul(PS[0:96, b, :], wdq[:, k, :], x2T[:, k, h * 512:(h + 1) * 512],
                                                                      start=(k == 0), stop=(k == 1)) for k in range(2)], [*w, *t_x2, td1])
                        t_qc.append(do(AC, lambda e, b=b, h=h: e.activation(qcT[:, h * 512:(h + 1) * 512], PS[0:96, b, :], ACT.Copy), [t]))
                        banks.free(b, t_qc[-1])

                    qu = {}

                    def queries(bb):
                        toks = []
                        i = bb % 2
                        for kind, n, W, dst, tab in (("A", 8, aw, QA[i], 0), ("B", 4, None, QB[i], 256)):
                            for p in range(n):
                                b, w = banks.take()
                                t = do(PE, [lambda e, b=b, hh=hh, p=p, kind=kind: e.matmul(
                                    PS[:, b, hh * 256:(hh + 1) * 256],
                                    aw[:, 2 * p + hh, :] if kind == "A" else wrt[:, (2 * p + hh) * 128:(2 * p + hh + 1) * 128],
                                    qcT[:, bb * 256:(bb + 1) * 256], start=True, stop=True) for hh in range(2)],
                                    [*w, *t_qc, *t_aw, td2])
                                toks.append(do(DV, lambda e, b=b, p=p, dst=dst, tab=tab: e.tensor_tensor(
                                    dst[:, 2 * p:2 * p + 2, :], PS[:, b, :].rearrange("p (a t) -> p a t", a=2),
                                    tb_[:, tab:tab + 256].unsqueeze(1).to_broadcast([128, 2, 256]), ALU.mult),
                                    [t, td1, *qu.get(bb - 2, [])]))
                                banks.free(b, toks[-1])
                        return toks

                    su = {}

                    def soft(c, tq):
                        bb, i = c // 2, c % 2
                        cc = c % 2 * 128
                        S_ = S[i]
                        ms = []
                        for z in range(2):
                            b, w = banks.take()
                            fns = []
                            for p in range(4 * z, 4 * z + 4):
                                fns.append(lambda e, b=b, p=p: e.matmul(
                                    PS[:, b, p % 4 * 128:p % 4 * 128 + 128], QB[bb % 2][:, p, cc:cc + 128],
                                    KZ[:, bb, :, :].rearrange("p a t -> p (a t)"), start=True, stop=False, skip_group_check=True))
                                for o in range(2):
                                    fns.append(lambda e, b=b, p=p, o=o: e.matmul(
                                        PS[:, b, p % 4 * 128 + o * 64:p % 4 * 128 + o * 64 + 64], QA[bb % 2][:, 2 * p + o, cc:cc + 128],
                                        KA[:, bb * 64:(bb + 1) * 64], start=False, stop=True, skip_group_check=True))
                            t = do(PE, fns, [*w, *tq, *t_kz])
                            ms.append(do(DV, lambda e, b=b, z=z: e.scalar_tensor_tensor(
                                S_[:, z * 512:(z + 1) * 512].rearrange("p (h t) -> p h t", h=8),
                                PS[:, b, :].rearrange("p (h t) -> p h t", h=8), float(1.0 / np.sqrt(np.float32(192.0))),
                                mk[:, c, :].unsqueeze(1).to_broadcast([128, 8, 64]), ALU.mult, ALU.add),
                                [t, t_mk, *su.get(i, [])]))
                            banks.free(b, ms[-1])
                        qu.setdefault(bb, []).append(t)
                        s3 = S_[:].rearrange("p (h t) -> p h t", h=16)
                        t = do(DV, lambda e: e.tensor_reduce(s16[i][:, 0, :], s3, X, ALU.max), ms)
                        t = do(DV, lambda e: e.tensor_tensor(s3, s3, s16[i][:, 0, :].unsqueeze(2).to_broadcast([128, 16, 64]), ALU.subtract), [t])
                        t = do(AC, lambda e: e.activation(S_[:], S_[:], ACT.Exp), [t])
                        t = do(DV, lambda e: e.tensor_reduce(s16[i][:, 1, :], s3, X, ALU.add), [t])
                        t = do(DV, lambda e: e.reciprocal(s16[i][:, 1, :], s16[i][:, 1, :]), [t])
                        return do(DV, lambda e: e.tensor_tensor(s3, s3, s16[i][:, 1, :].unsqueeze(2).to_broadcast([128, 16, 64]), ALU.mult), [t])

                    pu = {"PT": [], "CT": []}

                    def attend(bb, tsm):
                        te = []
                        for ci in range(2):
                            for z in range(2):
                                b, w = banks.take()
                                t = do(PE, [lambda e, b=b, p=p, ci=ci: e.transpose(
                                    PS[:, b, p % 4 * 128:p % 4 * 128 + 128], S[ci][:, p * 128:(p + 1) * 128], idf[:, :])
                                    for p in range(4 * z, 4 * z + 4)], [*w, tsm[ci]])
                                te.append(do(AC, lambda e, b=b, z=z, ci=ci: e.activation(
                                    PT1[:, 4 * z:4 * z + 4, ci * 128:(ci + 1) * 128], PS[:, b, :].rearrange("p (a t) -> p a t", a=4), ACT.Copy),
                                    [t, *pu["PT"]]))
                                banks.free(b, te[-1])
                            su[ci] = [t]
                        tcx = []
                        for z in range(4):
                            b, w = banks.take()
                            t = do(PE, lambda e, b=b, z=z: e.matmul(PS[:, b, :], BDK[:, bb, :], PT1[:, 2 * z:2 * z + 2, :].rearrange("p a b -> p (a b)"),
                                                                    start=True, stop=True), [*w, *te, t_bk])
                            tcx.append(do(AC, lambda e, b=b, z=z: e.activation(
                                CT[:, 2 * z:2 * z + 2, :].rearrange("p a b -> p (a b)"), PS[:, b, :], ACT.Copy), [t, *pu["CT"], *t_qc]))
                            banks.free(b, tcx[-1])
                        pu["PT"] = [t]
                        b, w = banks.take()
                        t = do(PE, [lambda e, b=b, ci=ci, p=p: e.matmul(
                            PS[:, b, ci * 256:(ci + 1) * 256], CT[:, p, ci * 128:(ci + 1) * 128], Bp[:, p, :],
                            start=(p == 0), stop=(p == 7)) for ci in range(2) for p in range(8)], [*w, *tcx, *t_bp])
                        pu["CT"] = [t]
                        xv = xt[:, 2 * bb:2 * bb + 2, :].rearrange("p a b -> p (a b)")
                        t = do(DV, lambda e, b=b: e.tensor_tensor(xv, PS[:, b, :], xv, ALU.add), [t, *t_n])
                        banks.free(b, t)
                        return t

                    tq = {0: queries(0)}
                    end = []
                    for bb in range(4):
                        ts = [soft(2 * bb, tq[bb]), soft(2 * bb + 1, tq[bb])]
                        if bb < 3:
                            tq[bb + 1] = queries(bb + 1)
                        end.append(attend(bb, ts))

                if stages > 3:
                    fence(end)
                    banks = Ring(8)
                    xh = sb("f_xh", [128, 2, 1024], FR, c2)
                    xl = sb("f_xl", [128, 2, 1024], FR, c2)
                    t_n = layernorm(xt, end[-1], xn)
                    tx = []
                    split_turn(t_n, xh, xl, tx)
                    fence(tx)

                    def ffn_tile(j):
                        v = lambda a: a[:, j, :].rearrange("p (g k m) -> p g k m", g=2, k=2)
                        return (v(fh), v(fl), fdh[:, j, :], fdl[:, j, :]), [*t_fw, t_fs], lambda t: None

                    def ffn_gate(j, h, i, bg, tg, bu, tu, r4, sg, hf, hh, hl, hw):
                        ts = do(AC, lambda e: e.activation(sg[i][:], PS[:, bg, :], ACT.Silu, scale=fsc[:, j:j + 1]), [tg, t_fs, *hw])
                        r4.free(bg, ts)
                        t = do(DV, lambda e: e.scalar_tensor_tensor(hf[i][:], PS[:, bu, :], fsc[:, 6 + j:7 + j], sg[i][:],
                                                                    ALU.mult, ALU.mult), [ts, tu, *hw])
                        r4.free(bu, t)
                        return split(hf[i][:], hh[i][:], hl[i][:], [t], hw)

                    t_y = gated(c2, xh, xl, tx, 6, ffn_tile, ffn_gate, [], "f_")
                    end = []
                    for j in range(4):
                        xv = xt[:, 2 * j:2 * j + 2, :]
                        nv = xn[:, 2 * j:2 * j + 2, :]
                        t = do(DV, lambda e, j=j, nv=nv: e.tensor_tensor(
                            nv, PS[:, 4 + j, :].rearrange("p (a b) -> p a b", a=2),
                            fsc[:, 12:268].unsqueeze(1).to_broadcast([128, 2, 256]), ALU.mult), [t_y, t_fs])
                        end.append(do(DV, lambda e, xv=xv, nv=nv: e.tensor_tensor(xv, xv, nv, ALU.add), [t]))

        t_out = Q.dma(SP, [(out.rearrange("(c p) d -> p c d", p=128), xt[:])], end)
        Q.wait(SP, [t_out])

        block = ctx.enter_context(nc.Block())

        @block.sync
        def _(e):
            Q.play(SP, e)

        @block.scalar
        def _(e):
            Q.play(AC, e)

        @block.vector
        def _(e):
            Q.play(DV, e)

        @block.tensor
        def _(e):
            Q.play(PE, e)

        @block.gpsimd
        def _(e):
            Q.play(PO, e)


def layout(v):
    f = np.ascontiguousarray
    g = {k: np.asarray(a) for k, a in v.items()}
    o = {}
    o["x"] = f(g["x"].reshape(1024, 256))
    o["ctxT"] = f(g["ctx_2048"].reshape(256, 256).T)
    o["idf"] = np.eye(128, dtype=np.float32)
    L = "L0_xattn_"
    two = lambda a: a.reshape(2, 128).T
    o["vec"] = f(np.concatenate([two(g[L + n]) for n in (
        "ln_w", "ln_b", "q_in_scale", "qx_in_scale", "k_in_scale", "v_in_scale")], axis=1))
    o["ln8"] = f(np.stack([g[L + n] for n in (
        "qln_w", "qln_b", "kln_w", "kln_b", "qxln_w", "qxln_b", "kxln_w", "kxln_b")], axis=1))
    s = g[L + "proj_smooth"].reshape(2, 4, 4, 128)
    o["smo"] = f(s.transpose(3, 1, 0, 2).reshape(128, 32))
    o["sca"] = f(np.tile(np.stack([g[L + n].reshape(()) for n in (
        "wq_scale", "wqx_scale", "wk_scale", "wv_scale", "proj_w_scale", "proj_in_scale")])[None], (128, 1)))
    q4 = lambda n, m: g[L + n].reshape(4, m, 2, 128).transpose(0, 3, 2, 1)
    o["wall"] = f(np.concatenate([q4("wq", 512), q4("wqx", 512), q4("wk", 256), q4("wv", 256)], axis=3))
    kv = g[L + "w_kv_x"].reshape(2, 4, 256, 2, 128)
    o["wkvx"] = f(kv.transpose(1, 4, 3, 0, 2).reshape(4, 128, 2, 512))
    wp = g[L + "wproj"].reshape(256, 2, 4, 4, 128)
    o["wproj"] = f(wp.transpose(2, 4, 1, 3, 0).reshape(4, 128, 8, 256))
    wg = g["L0_ffn_gate_up_proj"].reshape(32, 2, 96, 256).transpose(1, 0, 2, 3).reshape(2, 24, 128, 2, 128)
    o["wgu"] = f(wg.transpose(1, 4, 0, 3, 2))
    o["wdn"] = f(g["L0_ffn_down_proj"].transpose(0, 2, 1).reshape(24, 128, 256))
    o["gate"] = f(g["L0_ffn_gate_weight"].reshape(32, 2, 128).transpose(2, 1, 0).reshape(128, 64))
    o["sim"] = f(g["L0_ffn_similarity"])
    o["cst"] = f(np.tile(np.concatenate([np.arange(32), np.arange(4) - 8]).astype(np.float32)[None], (128, 1)))
    bf = mybir.dt.np(BF)
    o["idb"] = np.eye(128, dtype=np.float32).astype(bf)
    o["sel"] = f((np.arange(96)[:, None] % 32 == np.arange(3072)[None] // 96).astype(np.float32).astype(bf))
    M = "L1_xattn_"
    kp = lambda a: a.reshape(2, 128, -1).transpose(1, 0, 2)
    o["wdq"] = f(kp(g[M + "W_dq"]))
    o["wkvc"] = f(kp(g[M + "W_kvc"]))
    hT = lambda a: a.reshape(-1, 16, 128).transpose(2, 1, 0)
    o["wuq"], o["wuk"], o["wuv"] = f(hT(g[M + "W_uq"])), f(hT(g[M + "W_uk"])), f(hT(g[M + "W_uv"]))
    o["wo"] = f(g[M + "W_o"].reshape(16, 128, 256).transpose(1, 0, 2))
    o["wqr"] = f(g[M + "W_qr"].reshape(96, 16, 64))
    o["wrt"] = f(g[M + "W_qr"].reshape(96, 16, 2, 32)[:, :, ::-1].reshape(96, 1024))
    kr = g[M + "W_kr"]
    krr = kr.reshape(64, 2, 32)[:, ::-1].reshape(64, 64)
    o["wkr"] = f(np.stack([np.tile(kr, (1, 2)), np.tile(krr, (1, 2))], axis=1))
    half = np.arange(32, dtype=np.float32)
    inv = (np.float32(1.0) / np.float32(10000.0) ** (half / np.float32(32))).astype(np.float32)
    ang = np.arange(256, dtype=np.float32)[:, None] * inv
    cos, sin = np.cos(ang).T, np.sin(ang).T
    c4, s4 = np.tile(cos, (4, 1)), np.concatenate([-sin, sin, -sin, sin])
    ones = np.ones((64, 256), np.float32)
    o["rope"] = f(np.concatenate([np.concatenate([ones, c4[64:]]), s4, c4[:, :64], s4[:, :64],
                                  np.tile(np.arange(64, dtype=np.float32)[None], (128, 1))], axis=1).astype(np.float32))
    o["seg"] = f(g["itok_BxS_0_1023"].reshape(8, 128).T)
    F = "L1_ffn_"

    def wide(a):
        z = np.full((768, a.shape[1]), 128, a.dtype)
        z[:704] = a
        return z
    gu = np.stack([wide(g[F + "wq_gate"]), wide(g[F + "wq_up"])]).reshape(2, 6, 128, 2, 128)
    o["fgu"] = f(gu.transpose(1, 4, 0, 3, 2).reshape(6, 128, 512))
    o["fdn"] = f(wide(g[F + "wq_down"].T).reshape(6, 128, 256).transpose(1, 0, 2).reshape(128, 1536))
    sc = np.zeros((2, 768), np.float32)
    sc[0, :704], sc[1, :704] = g[F + "s_gate"], g[F + "s_up"]
    o["fsc"] = f(np.concatenate([sc.reshape(12, 128).T, np.tile(g[F + "s_down"][None], (128, 1))], axis=1))
    return o


def kernel(**inputs):
    import concourse.bacc as bacc
    from concourse.bass_utils import run_bass_kernel_spmd

    nc = bacc.Bacc("TRN2", target_bir_lowering=False, num_devices=1)
    arrays = layout(inputs)
    A = {n: nc.dram_tensor(f"in_{n}", a.shape, mybir.dt.from_np(a.dtype), kind="ExternalInput").ap()
         for n, a in arrays.items()}
    out = nc.dram_tensor("out_x", (1024, 256), F32, kind="ExternalOutput").ap()
    program(nc, A, out)
    r = run_bass_kernel_spmd(nc, [{f"in_{n}": a for n, a in arrays.items()}], core_ids=[0])
    return r.results[0]["out_x"].reshape(4, 256, 256)
```

```python
from contextlib import ExitStack

import concourse.bass as bass
from concourse import mybir
import numpy as np

ALU = mybir.AluOpType
ACT = mybir.ActivationFunctionType
F32 = mybir.dt.float32
FR = mybir.dt.float32r
BF = mybir.dt.bfloat16
U16 = mybir.dt.uint16
U32 = mybir.dt.uint32
I32 = mybir.dt.int32
X = mybir.AxisListType.X

PE, AC, DV, PO, SP = "pe", "ac", "dv", "po", "sp"
EPS = 1e-5
NEG = 1e30


class Queues:

    LIMIT = 3000

    def __init__(self, nc, ctx):
        self.nc, self.ctx = nc, ctx
        self.q = {e: [] for e in (PE, AC, DV, PO, SP)}
        self.sem, self.n, self.made = {}, {}, 0

    def fresh(self, name):
        self.made += 1
        return self.ctx.enter_context(self.nc.semaphore(f"{name}{self.made}"))

    def do(self, e, fns, waits=()):
        if e not in self.sem or self.n[e] >= self.LIMIT:
            self.sem[e], self.n[e] = self.fresh(f"s_{e}_"), 0
        self.n[e] += 1
        self.q[e].append(("run", tuple(w for w in waits if w), fns if isinstance(fns, list) else [fns], self.sem[e], 1))
        return (self.sem[e], self.n[e])

    def dma(self, e, pairs, waits=()):
        s = self.fresh("d_")
        for i, (o, a) in enumerate(pairs):
            self.q[e].append(("dma", tuple(w for w in waits if w) if i == 0 else (), (o, a), s, 16))
        return (s, 16 * len(pairs))

    def wait(self, e, waits):
        self.q[e].append(("wait", tuple(waits), None, None, 0))

    def play(self, e, eng):
        seen = {}
        for kind, waits, what, s, inc in self.q[e]:
            for ws, wv in waits:
                if seen.get(ws.name, 0) < wv:
                    eng.wait_ge(ws, wv)
                    seen[ws.name] = wv
            if kind == "run":
                for f in what:
                    ins = f(eng)
                ins.then_inc(s, inc)
            elif kind == "dma":
                eng.dma_start(what[0], what[1]).then_inc(s, inc)


class Ring:

    def __init__(self, n):
        self.n, self.at, self.users = n, 0, [[] for _ in range(n)]

    def take(self):
        i = self.at % self.n
        self.at += 1
        w, self.users[i] = self.users[i], []
        return i, w

    def free(self, i, *tokens):
        self.users[i] += tokens


def program(nc, A, out, stages=4):
    ctx = ExitStack()
    Q = Queues(nc, ctx)
    do = Q.do

    def bcast(ap, shape):
        return ap.to_broadcast(shape) if hasattr(ap, "to_broadcast") else ap.broadcast_to(shape)

    with ctx:
        def sb(name, shape, dt, c=ctx):
            return c.enter_context(nc.sbuf_tensor(name, shape, dt))

        PS = ctx.enter_context(nc.psum_tensor("PS", [128, 8, 512], F32))
        banks = Ring(8)

        xt = sb("xt", [128, 8, 256], F32)
        idf = sb("idf", [128, 128], F32)
        ctxT = sb("ctxT", [128, 2, 256], F32)
        st = sb("st", [128, 8, 6], F32)
        mv = sb("mv", [128, 8, 2], F32)
        rs = sb("rs", [128, 8], F32)
        xn = sb("xn", [128, 8, 256], F32)

        xin = A["x"].rearrange("(c p) d -> p c d", p=128)
        t_x = [Q.dma(SP, [(xt[:, 4 * h:4 * h + 4, :], xin[:, 4 * h:4 * h + 4, :])]) for h in range(2)]
        t_id = Q.dma(AC, [(idf[:], A["idf"])])
        t_ctx = Q.dma(AC, [(ctxT[:], A["ctxT"].rearrange("(k p) t -> p k t", p=128))])

        NWS = 3
        NWS = 3
        wst = [sb(f"wst{i}", [128, 2, 256], F32) for i in range(NWS)]
        wring = Ring(NWS)
        state = {}
        ve = sb("ve", [128, 8], F32)
        nt = sb("nt", [128, 8], F32)
        dring = Ring(2)

        def newton(y, v, n, t):
            t = do(DV, lambda e: e.tensor_tensor(n, y, y, ALU.mult), [t])
            t = do(DV, lambda e: e.tensor_tensor(n, n, v, ALU.mult), [t])
            t = do(DV, lambda e: e.tensor_scalar(n, n, -0.5, 1.5, ALU.mult, ALU.add), [t])
            return do(DV, lambda e: e.tensor_tensor(y, y, n, ALU.mult), [t])

        def layernorm(src, ready, dst, chunks=range(8)):
            c0_, c1_ = chunks[0], chunks[-1] + 1
            for c in chunks:
                t = do(DV, lambda e, c=c: e.bn_stats(st[:, c, :], src[:, c, :]), ready)
            for c in chunks:
                t_mv = do(DV, lambda e, c=c: e.bn_aggr(mv[:, c, :], st[:, c, :]), [t])
            t = do(DV, lambda e: e.tensor_scalar(ve[:, c0_:c1_], mv[:, c0_:c1_, 1], EPS, None, ALU.add), [t_mv])
            t = do(AC, lambda e: e.activation(rs[:, c0_:c1_], ve[:, c0_:c1_], ACT.Sqrt), [t])
            t = do(DV, lambda e: e.reciprocal(rs[:, c0_:c1_], rs[:, c0_:c1_]), [t])
            t = newton(rs[:, c0_:c1_], ve[:, c0_:c1_], nt[:, c0_:c1_], t)
            return [do(DV, lambda e, c=c: e.tensor_scalar(dst[:, c, :], src[:, c, :], mv[:, c, 0:1], rs[:, c:c + 1],
                                                          ALU.subtract, ALU.mult), [t]) for c in chunks]

        def rsqrt(v, y, n, ready, eng):
            t = do(DV, lambda e: e.tensor_scalar(v, v, EPS, None, ALU.add), ready)
            t = do(DV, lambda e: e.tensor_scalar(y.bitcast(I32), v.bitcast(I32), 1, None, ALU.logical_shift_right), [t])
            t = do(DV, lambda e: e.tensor_scalar(y.bitcast(I32), y.bitcast(I32), -1.0, float(0x5F3759DF), ALU.mult, ALU.add), [t])
            for _ in range(3):
                t = do(eng, lambda e: e.tensor_tensor(n, y, y, ALU.mult), [t])
                t = do(eng, lambda e: e.tensor_tensor(n, n, v, ALU.mult), [t])
                t = do(eng, lambda e: e.tensor_scalar(n, n, -0.5, 1.5, ALU.mult, ALU.add), [t])
                t = do(eng, lambda e: e.tensor_tensor(y, y, n, ALU.mult), [t])
            return t

        def split(src, hi, lo, ready, users, eh=AC, el=DV):
            if eh == AC:
                th = do(AC, lambda e: e.activation(hi, src, ACT.Copy), [*ready, *users])
            else:
                th = do(eh, lambda e: e.tensor_copy(hi, src), [*ready, *users])
            tl = do(el, lambda e: e.tensor_tensor(lo, src, hi.bitcast(F32), ALU.subtract), [*ready, th, *users])
            return [th, tl]

        def ln_batch(bb, ready):
            cs, b2 = (2 * bb, 2 * bb + 1), slice(2 * bb, 2 * bb + 2)
            for c in cs:
                t = do(DV, lambda e, c=c: e.bn_stats(st[:, c, :], xt[:, c, :]), ready)
            for c in cs:
                ta = do(DV, lambda e, c=c: e.bn_aggr(mv[:, c, :], st[:, c, :]), [t])
            t = rsqrt(mv[:, b2, 1], rs[:, b2], nt[:, b2], [ta], DV)
            for c in cs:
                t_ = do(DV, lambda e, c=c: e.tensor_scalar(xn[:, c, :], xt[:, c, :], mv[:, c, 0:1], rs[:, c:c + 1],
                                                           ALU.subtract, ALU.mult), [t])
            return t_

        def turn_batch(bb, t_n, evac):
            b, w = banks.take()
            t = do(PE, [lambda e, b=b, k=k, ci=ci: e.transpose(
                PS[:, b, k * 256 + ci * 128:k * 256 + ci * 128 + 128], xn[:, 2 * bb + ci, k * 128:(k + 1) * 128], idf[:, :])
                for k in range(2) for ci in range(2)], [*w, t_n, t_id])
            r = evac(b, t)
            banks.free(b, *r)
            return r

        def turn(src, t_src, evac, halves=(0, 1)):
            for h in halves:
                for k in range(2):
                    b, w = banks.take()
                    t = do(PE, [lambda e, b=b, c=c, k=k: e.transpose(PS[:, b, (c % 4) * 128:(c % 4 + 1) * 128],
                                                                    src[:, c, k * 128:(k + 1) * 128], idf[:, :])
                                for c in range(4 * h, 4 * h + 4)], [*w, *t_src[4 * h:4 * h + 4], t_id])
                    banks.free(b, evac(k, h, b, t))

        cm = ctx.enter_context(ExitStack())
        xq = [sb(f"xq{i}", [128, 2, 1024], FR, cm) for i in range(4)]
        WH = sb("WH", [128, 2, 1536], FR, cm)
        WL = sb("WL", [128, 2, 1536], FR, cm)
        dst_ = [sb(f"dst{i}", [128, 256], F32, cm) for i in range(2)]

        c0 = ExitStack()
        with c0:
            vec = sb("vec", [128, 12], F32, c0)
            ln8 = sb("ln8", [128, 8], F32, c0)
            smo = sb("smo", [128, 32], F32, c0)
            sca = sb("sca", [128, 6], F32, c0)
            t_vec = Q.dma(AC, [(vec[:], A["vec"]), (ln8[:], A["ln8"]), (smo[:], A["smo"]), (sca[:], A["sca"])])
            ivec = sb("ivec", [128, 4, 2], F32, c0)
            ismo = sb("ismo", [128, 32], F32, c0)
            sproj = sb("sproj", [128, 1], F32, c0)

            t_iv = do(DV, lambda e: e.reciprocal(ivec[:].rearrange("p a b -> p (a b)"), vec[:, 4:12]), [t_vec])
            t_is = do(DV, lambda e: e.reciprocal(ismo[:, :], smo[:, :]), [t_vec])
            t_sp = do(DV, lambda e: e.tensor_tensor(sproj[:], sca[:, 4:5], sca[:, 5:6], ALU.mult), [t_vec])
            t_l8 = [do(DV, lambda e, j=j: e.tensor_scalar(ln8[:, j:j + 2], ln8[:, j:j + 2], float(128 ** -0.5), None, ALU.mult),
                       [t_vec]) for j in (0, 4)]
            nivec = sb("nivec", [128, 4, 2], F32, c0)
            t_niv = do(DV, lambda e: e.tensor_scalar(nivec[:], ivec[:], -1.0, None, ALU.mult), [t_iv])
            yb = sb("yb0", [128, 2, 512], BF, c0)
            fb = sb("fb0", [128, 2, 512], BF, c0)
            with ExitStack() as cq:
                lnT = sb("lnT", [128, 2, 1024], F32, cq)
                tbs = sb("tbs", [128, 2, 2, 512], F32, cq)
                rb = sb("rb", [128, 2, 512], F32, cq)
            PH = sb("PH", [128, 8, 256], FR, c0)
            PL = sb("PL", [128, 8, 256], FR, c0)
            cat = sb("cat", [128, 8, 256], FR, c0)
            t_ln = [[], []]

            def ev_ln(k, h, b, t):
                t = do(AC, lambda e: e.activation(lnT[:, k, h * 512:(h + 1) * 512], PS[:, b, :], ACT.Identity,
                                                  bias=vec[:, 2 + k:3 + k], scale=vec[:, k:k + 1]), [t, t_vec])
                t_ln[h].append(t)
                return t

            t_h0 = []
            for h in range(2):
                t_h = layernorm(xt, [t_x[h]], xn, range(4 * h, 4 * h + 4))
                t_h0.append(t_h[-1])
                t_hn = layernorm(xn, [t_h[-1]], xn, range(4 * h, 4 * h + 4))
                turn(xn, [None] * (4 * h) + t_hn, ev_ln, (h,))

            def quant(y, tmpF, tmpT, dst, t_y, free):
                t = do(DV, lambda e: e.tensor_scalar(y, y, 448.0, -448.0, ALU.min, ALU.max), [*t_y])
                t = do(DV, lambda e: e.tensor_scalar(tmpF.bitcast(U16), y.bitcast(U16), 0x7F80, 0x0040,
                                                     ALU.bitwise_and, ALU.bitwise_or), [t, *free])
                t = do(DV, lambda e: e.tensor_scalar(tmpF, tmpF, 1.5 * 2.0 ** -6, None, ALU.max), [t])
                t = do(DV, lambda e: e.scalar_tensor_tensor(tmpT, tmpF, float(2 ** 20), y, ALU.mult, ALU.add), [t])
                return do(DV, lambda e: e.scalar_tensor_tensor(dst, tmpF, -float(2 ** 20), tmpT, ALU.mult, ALU.add), [t])

            t_xq = {}
            t_q = {}
            QORDER = [(h, i) for h in range(2) for i in (2, 3, 0, 1)]

            def div(n):
                h, i = QORDER[n]
                for k in range(2):
                    t_q[n] = do(AC, lambda e, k=k: e.activation(
                        tbs[:, n % 2, k, :], lnT[:, k, h * 512:(h + 1) * 512], ACT.Copy, scale=ivec[:, i, k:k + 1]),
                        [t_iv, *t_ln[h], t_xq.get(n - 2)])

            def quantise(n):
                h, i = QORDER[n]
                ts = []
                for k in range(2):
                    x_, q_, s_ = lnT[:, k, h * 512:(h + 1) * 512], tbs[:, n % 2, k, :], vec[:, 4 + 2 * i + k:5 + 2 * i + k]
                    t = do(DV, lambda e, k=k, x_=x_, q_=q_, s_=s_: e.scalar_tensor_tensor(
                        rb[:, k, :], q_, s_, x_, ALU.mult, ALU.subtract), [t_q[n], t_xq.get(n - 1)])
                    ts.append(do(DV, lambda e, k=k, q_=q_: e.scalar_tensor_tensor(
                        yb[:, k, :], rb[:, k, :], nivec[:, i, k:k + 1], q_, ALU.mult, ALU.add), [t, t_niv]))
                t_xq[n] = t_xq[h, i] = quant(yb[:], fb[:], tbs[:, n % 2, :, :], xq[i][:, :, h * 512:(h + 1) * 512], ts, [])
                if n + 2 < 8:
                    div(n + 2)

            w_users = [[] for _ in range(6)]
            p_users = []

            def pieces(src, hi, lo, users, scale=None, eh=PO, el=PO):
                i, w = wring.take()
                t = Q.dma(SP, [(wst[i][:], src)], w)
                if scale is not None:
                    for k in range(2):
                        ts = do(PO, lambda e, i=i, k=k: e.tensor_scalar(
                            wst[i][:, k, :], wst[i][:, k, :], scale[:, k:k + 1], 1.0, ALU.mult, ALU.mult), [t, t_vec])
                    t = ts
                if eh == AC:
                    th = do(AC, lambda e, i=i: e.activation(hi, wst[i][:], ACT.Copy), [t, *users])
                else:
                    th = do(PO, lambda e, i=i: e.tensor_scalar(hi, wst[i][:], 1.0, 1.0, ALU.mult, ALU.mult), [t, *users])
                tl = do(el, lambda e, i=i: e.tensor_tensor(lo, wst[i][:], hi.bitcast(F32), ALU.subtract), [th, *users])
                wring.free(i, tl)
                return tl

            def load_w(gp, js=range(6)):
                toks = state.setdefault(("w", gp), {})
                for j in js:
                    s, o = (0, 0, 1, 1, 2, 3)[j], slice(j * 256, (j + 1) * 256)
                    toks[j] = pieces(A["wall"][gp, :, :, o], WH[:, :, o], WL[:, :, o], w_users[j], vec[:, 4 + 2 * s:6 + 2 * s])
                    w_users[j] = []

            def load_p(gp, js=range(4), eh=AC, el=DV):
                state.setdefault(("p", gp), []).extend(
                    pieces(A["wproj"][gp, :, 2 * j:2 * j + 2, :], PH[:, 2 * j:2 * j + 2, :], PL[:, 2 * j:2 * j + 2, :],
                           list(p_users), None, eh, el) for j in js)

            qT = [sb(f"qT{i}", [128, 4, 256], F32, c0) for i in range(2)]
            qxT = [sb(f"qxT{i}", [128, 4, 256], F32, c0) for i in range(2)]
            kT = [sb(f"kT{i}", [128, 2, 256], F32, c0) for i in range(2)]
            NP_ = 5
            P = [sb(f"P{i}", [128, 2, 256], F32, c0) for i in range(NP_)]
            raw = sb("raw", [128, 4, 1280], F32, c0)
            raws = Ring(4)
            vr = sb("vr", [128, 8, 256], F32, c0)
            vrs = Ring(8)
            kraw = sb("kraw", [128, 2, 256], F32, c0)
            vx = sb("vx", [64, 4, 256], F32, c0)
            st6 = sb("st6", [128, 24, 6], F32, c0)
            mvq = sb("mvq", [128, 2, 20, 2], F32, c0)
            rsq = sb("rsq", [128, 2, 20], F32, c0)
            ntq = sb("ntq", [128, 20], F32, c0)
            mvk = sb("mvk", [128, 4, 2], F32, c0)
            rsk = sb("rsk", [128, 4], F32, c0)
            kxT = sb("kxT", [128, 2, 256], F32, c0)
            sm = [sb(f"sm{i}", [128, 3, 8], F32, c0) for i in range(NP_)]
            smr = Ring(NP_)
            NPT = 4
            PT = [sb(f"PT{i}", [128, 2, 256], F32, c0) for i in range(NPT)]
            ptr = Ring(NPT)
            yT = sb("yT", [128, 8, 256], BF, c0)
            yt = yb[:].rearrange("p a b -> p (a b)").bitcast(F32)
            yF = fb[:, 0, :]

            slot, vslot, t_st = {}, {}, {}

            SEG = [[(0, 0, 512, 0)], [(1, 512, 512, 0)], [(2, 1024, 256, 0), (3, 1280, 256, 256)]]

            def P1(gp, c, j):
                if (gp, c) not in slot:
                    slot[gp, c], state["rw", gp, c] = raws.take()
                    vslot[gp, c], state["vw", gp, c] = vrs.take()
                r, rv = slot[gp, c], vslot[gp, c]
                rw, vw = state["rw", gp, c], state["vw", gp, c]
                tw = state["w", gp]
                tc = slice(c * 128, (c + 1) * 128)
                b, w = banks.take()
                fns = []
                for s, w0, n, o in SEG[j]:
                    for k in range(2):
                        for i, W in enumerate((WH, WL)):
                            fns.append(lambda e, s=s, k=k, W=W, w0=w0, n=n, o=o, b=b, i=i: e.matmul(
                                PS[:, b, o:o + n], xq[s][:, k, tc], W[:, k, w0:w0 + n],
                                start=(k == 0 and i == 0), stop=(k == 1 and i == 1)))
                t = do(PE, fns, [*w, *[t_xq[c // 4, s] for s, _, _, _ in SEG[j]], tw[2 * j], tw[2 * j + 1]])
                ev = [do(AC, lambda e, s=s, w0=w0, n=n, o=o, b=b: e.activation(
                    vr[:, rv, :] if s == 3 else raw[:, r, w0:w0 + n], PS[:, b, o:o + n], ACT.Copy,
                    scale=sca[:, s:s + 1]), [t, *(vw if s == 3 else rw), t_vec])
                    for s, w0, n, o in SEG[j]]
                banks.free(b, *ev)
                w_users[2 * j] = [t]
                w_users[2 * j + 1] = [t]
                if j == 2:
                    state["v", gp, c] = ev[1]
                state["ev", gp, c, j] = ev[0]

            def ST(gp, c, j):
                r = slot[gp, c]
                par = (gp * 4 + c // 2) % 2
                o = c % 2 * 10
                hs = (range(0, 4), range(4, 8), range(8, 10))[j]
                for h in hs:
                    ts = do(DV, lambda e, h=h: e.bn_stats(st6[:, o + h, :], raw[:, r, h * 128:(h + 1) * 128]),
                            [state["ev", gp, c, j], state.get(("st", o, j))])
                for h in hs:
                    ta = do(DV, lambda e, h=h: e.bn_aggr(mvq[:, par, o + h, :], st6[:, o + h, :]),
                            [ts, state.get(("nm", gp * 4 + c // 2 - 2))])
                state["st", o, j] = ta
                t_st[gp, c, j] = ta

            def NM(s):
                gp, bb = s // 4, s % 4
                par = s % 2
                ready = [t_st[gp, c, j] for c in (2 * bb, 2 * bb + 1) for j in range(3)]
                t = rsqrt(mvq[:, par, :, 1], rsq[:, par, :], ntq[:, :], ready, PO)
                t = do(PO, lambda e: e.tensor_scalar(mvq[:, par, :, 0], mvq[:, par, :, 0], -1.0, 1.0, ALU.mult, ALU.mult), [t])
                for h in (8, 9, 0, 1, 2, 3, 4, 5, 6, 7):
                    for ci in range(2):
                        v = raw[:, slot[gp, 2 * bb + ci], h * 128:(h + 1) * 128]
                        tn = do(PO, lambda e, v=v, ci=ci, h=h: e.tensor_scalar(
                            v, v, mvq[:, par, ci * 10 + h, 0:1], rsq[:, par, ci * 10 + h:ci * 10 + h + 1],
                            ALU.add, ALU.mult), [t])
                        state["nmh", s, ci, h] = tn
                state["nm", s] = tn

            def KX(gp):
                i, w = wring.take()
                td = Q.dma(SP, [(wst[i][:], A["wkvx"][gp, :, :, 0:256])], w)
                b, w = banks.take()
                t = do(PE, [lambda e, c=c, k=k, b=b: e.matmul(
                    PS[:, b, c * 256:(c + 1) * 256], ctxT[:, k, c * 128:(c + 1) * 128], wst[i][:, k, :],
                    start=(k == 0), stop=(k == 1)) for c in range(2) for k in range(2)], [*w, td, t_ctx])
                wring.free(i, t)
                state["kx", gp] = do(AC, lambda e, b=b: e.activation(kraw[:].rearrange("p a b -> p (a b)"), PS[:, b, :], ACT.Copy),
                                     [t, *state.get("kraw", [])])
                banks.free(b, state["kx", gp])

            def KS(gp):
                for i in range(4):
                    ts = do(DV, lambda e, i=i: e.bn_stats(st6[:, 20 + i, :], kraw[:, i // 2, (i % 2) * 128:(i % 2 + 1) * 128]),
                            [state["kx", gp], state.get("st2")])
                for i in range(4):
                    ta = do(DV, lambda e, i=i: e.bn_aggr(mvk[:, i, :], st6[:, 20 + i, :]), [ts, state.get("kn")])
                state["st2"] = ta
                t = rsqrt(mvk[:, :, 1], rsk[:, :], ntq[:, 0:4], [ta], PO)
                t = do(PO, lambda e: e.tensor_scalar(mvk[:, :, 0], mvk[:, :, 0], -1.0, 1.0, ALU.mult, ALU.mult), [t])
                for i in range(4):
                    v = kraw[:, i // 2, (i % 2) * 128:(i % 2 + 1) * 128]
                    t2 = do(PO, lambda e, v=v, i=i: e.tensor_scalar(v, v, mvk[:, i, 0:1], rsk[:, i:i + 1],
                                                                   ALU.add, ALU.mult), [t])
                state["kn"] = t2

            def KT(gp):
                b, w = banks.take()
                tp = do(PE, [lambda e, b=b, i=i: e.transpose(
                    PS[:, b, (i % 2) * 256 + (i // 2) * 128:(i % 2) * 256 + (i // 2) * 128 + 128],
                    kraw[:, i // 2, (i % 2) * 128:(i % 2 + 1) * 128], idf[:, :]) for i in range(4)], [*w, state["kn"], t_id])
                state["kraw"] = [tp]
                te = do(AC, lambda e, b=b: e.activation(kxT[:].rearrange("p a b -> p (a b)"), PS[:, b, :], ACT.Identity,
                                                        scale=ln8[:, 6:7], bias=ln8[:, 7:8]),
                        [tp, *state.get(("kxu", gp - 1), [])])
                banks.free(b, te)
                state["kxT", gp] = te

            def VX(gp):
                i, w = wring.take()
                td = Q.dma(SP, [(wst[i][:], A["wkvx"][gp, :, :, 256:512])], w)
                tv = []
                for j in range(2):
                    b, w = banks.take()
                    t = do(PE, [lambda e, q=q, k=k, b=b: e.matmul(
                        PS[0:64, b, (q % 2) * 256:(q % 2 + 1) * 256], ctxT[:, k, q * 64:(q + 1) * 64], wst[i][:, k, :],
                        start=(k == 0), stop=(k == 1)) for q in (2 * j, 2 * j + 1) for k in range(2)], [*w, td])
                    tv.append(do(AC, lambda e, b=b, j=j: e.activation(
                        vx[:, 2 * j:2 * j + 2, :].rearrange("p a b -> p (a b)"), PS[0:64, b, :], ACT.Copy),
                        [t, *state.get(("vxu", gp - 1), [])]))
                    banks.free(b, tv[-1])
                wring.free(i, t)
                state["vx", gp] = tv

            def P2(s, j):
                gp, bb = s // 4, s % 4
                b, w = banks.take()
                fns = []
                for hh in range(2):
                    for ci in range(2):
                        fns.append(lambda e, b=b, hh=hh, ci=ci: e.transpose(
                            PS[:, b, hh * 256 + ci * 128:hh * 256 + ci * 128 + 128],
                            raw[:, slot[gp, 2 * bb + ci], (2 * j + hh) * 128:(2 * j + hh + 1) * 128], idf[:, :]))
                tp = do(PE, fns, [*w, *[state["nmh", s, ci, 2 * j + 1] for ci in range(2)], t_id])
                dst = (qT, qT, qxT, qxT, kT)[j][s % 2]
                o = (0, 2, 0, 2, 0)[j]
                v = (0, 0, 4, 4, 2)[j]
                te = do(AC, lambda e, b=b: e.activation(
                    dst[:, o:o + 2, :].rearrange("p a b -> p (a b)"), PS[:, b, :], ACT.Identity,
                    scale=ln8[:, v:v + 1], bias=ln8[:, v + 1:v + 2]), [tp, *t_l8, *state.get(("qu", s - 2), [])])
                banks.free(b, te)
                state["qT", s, j] = te
                if j == P2ORDER[-1]:
                    for c in (2 * bb, 2 * bb + 1):
                        raws.free(slot[gp, c], tp)

            P2ORDER = (4, 0, 1, 2, 3)

            def scores(u):
                s, h = u
                g = h // 2
                q_, k_ = qT[s % 2], kT[s % 2]
                i, w = smr.take()
                b, bw = banks.take()
                t = do(PE, [lambda e, b=b, c=c: e.matmul(
                    PS[:, b, c * 256:(c + 1) * 256], q_[:, h, c * 128:(c + 1) * 128], k_[:, g, :],
                    start=True, stop=True) for c in range(2)], [*bw, state["qT", s, h // 2], state["qT", s, 4]])
                tm = do(DV, lambda e, b=b: e.tensor_reduce(
                    sm[i][:, 0, 0:2], PS[:, b, :].rearrange("p (c t) -> p c t", c=2), X, ALU.max, negate=True), [t, *w])
                for c in range(2):
                    tx = do(AC, lambda e, b=b, c=c: e.activation(
                        P[i][:, c, :], PS[:, b, c * 256:(c + 1) * 256], ACT.Exp,
                        bias=sm[i][:, 0, c:c + 1], accum_out=sm[i][:, 1, c:c + 1]), [tm, *w])
                banks.free(b, tx)
                state.setdefault(("qu", s), []).append(t)
                return i, tx

            def norm(u, st_):
                i, tx = st_
                tr = do(DV, lambda e: e.reciprocal(sm[i][:, 2, 0:2], sm[i][:, 1, 0:2]), [tx])
                for j in range(2):
                    tn = do(DV, lambda e, j=j: e.tensor_scalar(P[i][:, j, :], P[i][:, j, :], sm[i][:, 2, j:j + 1], None,
                                                               ALU.mult), [tr])
                return i, tn

            def turn_p(u, st_):
                s, h = u
                i, tn = st_
                z, zw = ptr.take()
                b, bw = banks.take()
                t = do(PE, [lambda e, b=b, c=c, tc=tc: e.transpose(
                    PS[:, b, tc * 256 + c * 128:tc * 256 + c * 128 + 128], P[i][:, c, tc * 128:(tc + 1) * 128], idf[:, :])
                    for tc in range(2) for c in range(2)], [*bw, tn])
                dst = PT[z][:].rearrange("p a b -> p (a b)")
                if h in PTDV:
                    te = do(DV, lambda e, b=b: e.tensor_copy(dst, PS[:, b, :]), [t, *zw])
                else:
                    te = do(AC, lambda e, b=b: e.activation(dst, PS[:, b, :], ACT.Copy), [t, *zw])
                banks.free(b, te)
                smr.free(i, t)
                return z, te

            def times_v(u, st_):
                s, h = u
                gp, bb = s // 4, s % 4
                g = h // 2
                z, te = st_
                b, bw = banks.take()
                t = do(PE, [lambda e, b=b, tc=tc: e.matmul(
                    PS[:, b, 0:256], vr[:, vslot[gp, 2 * bb + tc], g * 128:(g + 1) * 128], PT[z][:, tc, :],
                    start=(tc == 0), stop=(tc == 1)) for tc in range(2)],
                    [*bw, te, state["v", gp, 2 * bb], state["v", gp, 2 * bb + 1]])
                ptr.free(z, t)
                k = 8 * gp + h
                ty = do(AC, lambda e, b=b: e.activation(
                    yT[:, h, :], PS[:, b, 0:256], ACT.Copy, scale=ismo[:, k:k + 1]), [t, t_is, state.get(("q8", s - 1, h // 2))])
                banks.free(b, ty)
                state["yt", s, h] = ty
                if h == 3:
                    for c in (2 * bb, 2 * bb + 1):
                        vrs.free(vslot[gp, c], t)

            def x_scores(u):
                s, _ = u
                gp, bb = s // 4, s % 4
                q_ = qxT[s % 2]
                i, w = smr.take()
                b, bw = banks.take()
                t = do(PE, [lambda e, b=b, h=h, c=c: e.matmul(
                    PS[:, b, (2 * h + c) * 64:(2 * h + c + 1) * 64], q_[:, h, c * 128:(c + 1) * 128],
                    kxT[:, h // 2, bb * 64:(bb + 1) * 64], start=True, stop=True)
                    for h in range(4) for c in range(2)], [*bw, state["qT", s, 2], state["qT", s, 3], state["kxT", gp]])
                state.setdefault(("qu", s), []).append(t)
                state.setdefault(("kxu", gp), []).append(t)
                pf = P[i][:].rearrange("p a b -> p (a b)")
                p3 = pf.rearrange("p (j t) -> p j t", t=64)
                ps3 = PS[:, b, :].rearrange("p (j t) -> p j t", t=64)
                tm = do(DV, lambda e: e.tensor_reduce(sm[i][:, 0, :], ps3, X, ALU.max), [t, *w])
                ts = do(DV, lambda e: e.tensor_tensor(p3, ps3, sm[i][:, 0, :].unsqueeze(2).to_broadcast([128, 8, 64]),
                                                      ALU.subtract), [tm, *w])
                banks.free(b, ts)
                return i, do(AC, lambda e: e.activation(pf, pf, ACT.Exp), [ts])

            def x_norm(u, st_):
                i, tx = st_
                p3 = P[i][:].rearrange("p a b -> p (a b)").rearrange("p (j t) -> p j t", t=64)
                tm = do(DV, lambda e: e.tensor_reduce(sm[i][:, 1, :], p3, X, ALU.add), [tx])
                tr = do(DV, lambda e: e.reciprocal(sm[i][:, 2, :], sm[i][:, 1, :]), [tm])
                return i, do(DV, lambda e: e.tensor_tensor(
                    p3, p3, sm[i][:, 2, :].unsqueeze(2).to_broadcast([128, 8, 64]), ALU.mult), [tr])

            def x_turn(u, st_):
                i, tn = st_
                zs = []
                for g in range(2):
                    z, zw = ptr.take()
                    b, bw = banks.take()
                    t = do(PE, [lambda e, b=b, j=j, g=g: e.transpose(
                        PS[0:64, b, j * 128:(j + 1) * 128],
                        P[i][:].rearrange("p a b -> p (a b)")[:, (4 * g + j) * 64:(4 * g + j + 1) * 64],
                        idf[:, :]) for j in range(4)], [*bw, tn])
                    dst = PT[z][0:64].rearrange("p a b -> p (a b)")
                    if 4 + g in PTDV:
                        te = do(DV, lambda e, b=b, dst=dst: e.tensor_copy(dst, PS[0:64, b, :]), [t, *zw])
                    else:
                        te = do(AC, lambda e, b=b, dst=dst: e.activation(dst, PS[0:64, b, :], ACT.Copy), [t, *zw])
                    zs.append((z, te))
                    banks.free(b, te)
                smr.free(i, t)
                return zs

            def x_times_v(u, zs):
                s, _ = u
                gp, bb = s // 4, s % 4
                for g, (z, te) in enumerate(zs):
                    b, bw = banks.take()
                    t = do(PE, lambda e, b=b, g=g, z=z: e.matmul(
                        PS[:, b, :], vx[:, bb, g * 128:(g + 1) * 128], PT[z][0:64].rearrange("p a b -> p (a b)"),
                        start=True, stop=True), [*bw, te, *state["vx", gp]])
                    ptr.free(z, t)
                    for h in range(2):
                        k = 8 * gp + 4 + 2 * g + h
                        ty = do(AC, lambda e, b=b, h=h, k=k, g=g: e.activation(
                            yT[:, 4 + 2 * g + h, :], PS[:, b, h * 256:(h + 1) * 256], ACT.Copy, scale=ismo[:, k:k + 1]),
                            [t, t_is, state.get(("q8", s - 1, 2 + g))])
                        state["yt", s, 4 + 2 * g + h] = ty
                    banks.free(b, ty)
                state.setdefault(("vxu", gp), []).append(t)

            PTDV = ()

            def QO(s, p):
                two = lambda v: v[:, 2 * p:2 * p + 2, :].rearrange("p a b -> p (a b)")
                state["q8", s, p] = quant(two(yT), yF, yt, two(cat), [state["yt", s, 2 * p + 1]], [state.get("catu")])

            def OP(s):
                gp, bb = s // 4, s % 4
                b, w = banks.take()
                t = do(PE, [lambda e, b=b, c=c, j=j, W=W: e.matmul(
                    PS[:, b, c * 256:(c + 1) * 256], cat[:, j, c * 128:(c + 1) * 128], W[:, j, :],
                    start=(j == 0 and W is PH), stop=(j == 7 and W is PL))
                    for c in range(2) for j in range(8) for W in (PH, PL)],
                    [*w, state["q8", s, 3], *state["p", gp]])
                state["catu"] = t
                if bb == 3:
                    p_users[:] = [t]
                xv = xt[:, 2 * bb:2 * bb + 2, :].rearrange("p a b -> p (a b)")
                tx = do(DV, lambda e, b=b: e.scalar_tensor_tensor(xv, PS[:, b, :], sproj[:, 0:1], xv, ALU.mult, ALU.add),
                        [t, t_sp, *t_h0] + state.get(("x", bb), []))
                banks.free(b, tx)
                state["x", bb] = [tx]

            STEPS = 16
            PARTS = (2, 0, 1)
            KX(0)
            VX(0)
            load_w(0, (4, 5, 0, 1, 2, 3))
            div(0)
            div(1)
            KS(0)
            quantise(0)
            quantise(1)
            KT(0)
            for n, j in enumerate(PARTS):
                for c in range(4):
                    P1(0, c, j)
                if n < 2:
                    quantise(2 + n)
                for c in (0, 1) if n == 2 else range(4):
                    ST(0, c, j)
            NM(0)
            for c in (2, 3):
                ST(0, c, PARTS[2])
            NM(1)
            quantise(4)
            quantise(5)
            for j in P2ORDER:
                P2(0, j)

            xv = xq[0], xq[1]

            def x_split(b, t):
                bb = state["xs"]
                cols = slice(bb * 256, (bb + 1) * 256)
                ps = PS[:, b, :].rearrange("p (k t) -> p k t", k=2)
                return split(ps, xv[0][:, :, cols], xv[1][:, :, cols], [t], state["lastP1"])

            def moe_load(j, el):
                i = j % 6
                v = lambda W: W[:].rearrange("p a b -> p (a b)")[:, i * 512:(i + 1) * 512].rearrange("p (a b) -> p a b", a=2)
                state["gu", j] = pieces(A["wgu"][j].rearrange("p g k m -> p g (k m)"), v(WH), v(WL),
                                        state["lastP1"] if j < 6 else state["guu", j - 6], None, AC, el)

            def dn_load(j):
                i, w = dring.take()
                o = slice(j % 8 * 256, j % 8 * 256 + 256)
                hi, lo = (xq[z][:].rearrange("p a b -> p (a b)")[:, o] for z in (2, 3))
                users = state["lastP1"] if j < 8 else state["dnu", j - 8]
                t = Q.dma(SP, [(dst_[i][:], A["wdn"][j])], w)
                th = do(PO, lambda e: e.tensor_scalar(hi, dst_[i][:], 1.0, 1.0, ALU.mult, ALU.mult), [t, *users])
                tl = do(PO, lambda e: e.tensor_tensor(lo, dst_[i][:], hi.bitcast(F32), ALU.subtract), [th])
                dring.free(i, tl)
                state["dn", j] = tl

            line = []

            def flow(u):
                for n in range(len(line) - 1, -1, -1):
                    u_, k, st_ = line[n]
                    x = u_[1] == 4
                    if k == 2:
                        (x_times_v if x else times_v)(u_, st_)
                        line.pop(n)
                    elif k == 1:
                        line[n] = (u_, 2, (x_turn if x else turn_p)(u_, st_))
                    else:
                        line[n] = (u_, 1, (x_norm if x else norm)(u_, st_))
                if u:
                    line.insert(0, (u, 0, (x_scores if u[1] == 4 else scores)(u)))

            def filler(s, k):
                gp = s // 4
                if s == 0 and k < 2:
                    quantise(6 + k)
                if s + 2 < STEPS:
                    g2, b2 = (s + 2) // 4, (s + 2) % 4
                    if k < 3:
                        for c in (2 * b2, 2 * b2 + 1):
                            P1(g2, c, PARTS[k])
                        if b2 == 3 and g2 < 3:
                            load_w(g2 + 1, (2 * PARTS[k], 2 * PARTS[k] + 1))
                    if 0 < k < 4:
                        for c in (2 * b2, 2 * b2 + 1):
                            ST(g2, c, PARTS[k - 1])
                    if k == 3:
                        NM(s + 2)
                if s + 1 < STEPS and k < 5:
                    P2(s + 1, P2ORDER[k])
                if s == 0 and k > 2:
                    load_p(0, (2 * k - 6, 2 * k - 5))
                if s % 4 == 3 and gp < 3 and k == 2:
                    KX(gp + 1)
                if s % 4 == 3 and gp < 3 and k == 4:
                    KS(gp + 1)
                if s % 4 == 0 and 0 < s < STEPS:
                    if k == 2:
                        KT(gp)
                    elif k == 3:
                        VX(gp)
                if s > 1 and k == 0:
                    OP(s - 2)
                if s and k != 1:
                    QO(s - 1, max(0, k - 1))
                if s == STEPS and k == 4:
                    OP(s - 1)
                if s == 13 and k == 4:
                    state["lastP1"] = [t for u in w_users for t in u]
                if s > 13 and stages > 1:
                    bb = s - 14
                    if k == 1:
                        state["ln", bb] = ln_batch(bb, state["x", bb])
                    elif k == 3:
                        state["xs"] = bb
                        state["xs", bb] = turn_batch(bb, state["ln", bb], x_split)
                    if s == 15:
                        moe_load(k, PO)
                        dn_load(k)
                    if s == 16 and k == 0:
                        moe_load(5, PO)
                    if s == 16 and k < 3:
                        dn_load(5 + k)
                if s % 4 == 1 and 1 < s < STEPS and k > 0:
                    load_p(gp, (k - 1,))

            for s in range(STEPS):
                for k in range(5):
                    flow((s, k))
                    filler(s, k)
            for k in range(5):
                flow(None)
                filler(STEPS, k)
            if stages > 1:
                state["ln", 3] = ln_batch(3, state["x", 3])
                state["xs"] = 3
                state["xs", 3] = turn_batch(3, state["ln", 3], x_split)


        def fence(tokens):
            for e in (PE, AC, DV, PO, SP):
                Q.wait(e, tokens)

        def split_turn(t_src, hi, lo, toks):
            def ev(k, h, b, t):
                ts = split(PS[:, b, :], hi[:, k, h * 512:(h + 1) * 512], lo[:, k, h * 512:(h + 1) * 512], [t], [])
                toks.extend(ts)
                return ts[1]
            turn(xn, t_src, ev)

        def gated(c, xh, xl, name, nb=3):
            r4, hr = Ring(4), Ring(nb)
            sg, hf = ([sb(f"{name}{n}{i}", [128, 512], F32, c) for i in range(nb)] for n in ("sg", "hf"))
            hh, hl = ([sb(f"{name}{n}{i}", [128, 512], FR, c) for i in range(nb)] for n in ("hh", "hl"))
            begun = set()

            def front(W, h, waits):
                out_ = []
                cols = slice(h * 512, (h + 1) * 512)
                for gu in range(2):
                    b, w = r4.take()
                    ops = [(k, wi, a) for k in range(2) for wi, a in ((0, xh), (0, xl), (1, xh))]
                    fns = [lambda e, b=b, k=k, wi=wi, a=a, n=n, gu=gu: e.matmul(
                        PS[:, b, :], W[wi][:, gu, k, :], a[:, k, cols], start=(n == 0), stop=(n == 5))
                        for n, (k, wi, a) in enumerate(ops)]
                    out_ += [b, do(PE, fns, [*w, *waits])]
                return out_

            def down(h, i, D, waits, last=False):
                first = h not in begun
                begun.add(h)
                fns = []
                for cc in range(4):
                    ch = 4 * h + cc
                    for p, (a, w) in enumerate(((hh, 0), (hh, 1), (hl, 0))):
                        fns.append(lambda e, a=a, w=w, ch=ch, cc=cc, p=p: e.matmul(
                            PS[:, 4 + ch // 2, ch % 2 * 256:ch % 2 * 256 + 256], a[i][:, cc * 128:(cc + 1) * 128],
                            D[w], start=(first and p == 0 and ch % 2 == 0), stop=(last and p == 2),
                            skip_group_check=True))
                t = do(PE, fns, waits)
                hr.free(i, t)
                return t

            return r4, hr, sg, hf, hh, hl, front, down

        end = [state["x", bb][0] for bb in range(4)] 
        c1 = ExitStack()
        with c1:
            if stages > 1:
                fence([*end, (Q.sem[PO], Q.n[PO])] if Q.n.get(PO) else end)
                rb4 = Ring(4)
                xh, xl = xq[0], xq[1]
                cst = sb("m_cst", [128, 32 + 4], F32, c1)
                idb = sb("m_idb", [128, 128], BF, c1)
                sel = sb("m_sel", [96, 3072], BF, c1)
                gst = sb("m_gst", [128, 64], F32, c1)
                gh = sb("m_gh", [128, 2, 32], FR, c1)
                gl = sb("m_gl", [128, 2, 32], FR, c1)
                bd = sb("m_bd", [128, 128], F32, c1)
                pr = sb("m_pr", [128, 8, 32], F32, c1)
                s8 = sb("m_s8", [128, 8], F32, c1)
                v8 = sb("m_v8", [128, 8, 8], F32, c1)
                i8 = sb("m_i8", [128, 8, 8], U32, c1)
                i8f = sb("m_i8f", [128, 64], F32, c1)
                OH = sb("m_OH", [128, 64, 32], F32, c1)
                OT = sb("m_OT", [128, 8, 128], F32, c1)
                RR = sb("m_RR", [128, 8, 128], F32, c1)
                tmp = [sb(f"m_tmp{i}", [128, 512], F32, c1) for i in range(2)]
                cand = sb("m_cand", [128, 32, 4], F32, c1)
                best = sb("m_best", [128, 32], F32, c1)
                e4 = sb("m_e4", [128, 32, 4], F32, c1)
                fi = sb("m_fi", [128, 32], F32, c1)
                ge = sb("m_ge", [128, 32], F32, c1)
                wa = sb("m_wa", [128, 32], F32, c1)
                co = sb("m_co", [128, 8, 8], F32, c1)
                ac_ = sb("m_ac", [128, 8, 4], F32, c1)
                cw = sb("m_cw", [128, 8, 32], F32, c1)
                c3 = sb("m_c3", [128, 8, 96], BF, c1)
                cwT = sb("m_cwT", [96, 1024], BF, c1)
                t_g = Q.dma(SP, [(gst[:], A["gate"]), (cst[:], A["cst"]), (idb[:], A["idb"]), (sel[:], A["sel"])])
                t_z = do(DV, lambda e: e.memset(bd[:], 0.0))
                t_bd = Q.dma(SP, [(bd[32 * j:32 * j + 32, 32 * j:32 * j + 32], A["sim"]) for j in range(4)], [t_z])
                iota, i48 = cst[:, 0:32], cst[:, 32:36]

                tx = [t for bb in range(4) for t in state["xs", bb]]
                tgs = split(gst[:], gh[:].rearrange("p a b -> p (a b)"), gl[:].rearrange("p a b -> p (a b)"), [t_g], [])
                t = do(DV, lambda e: e.scalar_tensor_tensor(tmp[0][:, 0:128], idf[:, :], -1.0, bd[:], ALU.mult, ALU.mult), [t_bd, t_id])
                t = do(DV, lambda e: e.tensor_tensor(bd[:], bd[:], tmp[0][:, 0:128], ALU.add), [t])
                t_bd = do(DV, lambda e: e.tensor_tensor(bd[:], bd[:], idf[:, :], ALU.add), [t])
                def rtake():
                    i, w = rb4.take()
                    return i + 4, w

                def rfree(b, *t):
                    rb4.free(b - 4, *t)

                def router():
                    b, w = rtake()
                    fns = []
                    for c in range(8):
                        n = 0
                        for k in range(2):
                            for a, g_ in ((xh, gh), (xh, gl), (xl, gh)):
                                fns.append(lambda e, c=c, k=k, a=a, g_=g_, n=n, b=b: e.matmul(
                                    PS[:, b, c * 32:(c + 1) * 32], a[:, k, c * 128:(c + 1) * 128], g_[:, k, :],
                                    start=(n == 0), stop=(n == 5)))
                                n += 1
                    t = do(PE, fns, [*w, *tx, *tgs])
                    lg = PS[:, b, 0:256].rearrange("p (c n) -> p c n", n=32)
                    up = lambda ap, n: ap.unsqueeze(2).to_broadcast([128, ap.shape[1], n])
                    tm = do(DV, lambda e: e.tensor_reduce(s8[:], lg, X, ALU.max), [t])
                    t = do(DV, lambda e: e.tensor_tensor(pr[:], lg, up(s8[:], 32), ALU.subtract), [tm])
                    rfree(b, t)
                    t = do(AC, lambda e: e.activation(pr[:], pr[:], ACT.Exp), [t])
                    t = do(DV, lambda e: e.tensor_reduce(s8[:], pr[:], X, ALU.add), [t])
                    t = do(DV, lambda e: e.reciprocal(s8[:], s8[:]), [t])
                    t = do(DV, lambda e: e.tensor_tensor(pr[:], pr[:], up(s8[:], 32), ALU.mult), [t])
                    for c in range(8):
                        tv = do(DV, lambda e, c=c: e.max(v8[:, c, :], pr[:, c, :]), [t])
                    for c in range(8):
                        ti = do(DV, lambda e, c=c: e.max_index(i8[:, c, :], v8[:, c, :], pr[:, c, :]), [tv])
                    t = do(DV, lambda e: e.tensor_copy(i8f[:], i8[:].rearrange("p a b -> p (a b)")), [ti])
                    t_oh = do(DV, lambda e: e.tensor_tensor(OH[:], up(i8f[:], 32),
                                                            iota.unsqueeze(1).to_broadcast([128, 64, 32]), ALU.is_equal), [t, t_g])
                    t = do(DV, lambda e: e.tensor_reduce(s8[:], v8[:], X, ALU.add), [tv])
                    t = do(DV, lambda e: e.tensor_scalar(s8[:], s8[:], 1e-12, None, ALU.max), [t])
                    t = do(DV, lambda e: e.reciprocal(s8[:], s8[:]), [t])
                    t_wt = do(DV, lambda e: e.tensor_tensor(v8[:], v8[:], up(s8[:], 8), ALU.mult), [t, ti])
                    yield
                    te = []
                    for hh_ in range(2):
                        b, w = rtake()
                        t = do(PE, [lambda e, b=b, c=c: e.transpose(
                            PS[:, b, c % 4 * 128:c % 4 * 128 + 128], OH[:, c * 8 + 4:c * 8 + 8, :].rearrange("p a b -> p (a b)"),
                            idf[:, :]) for c in range(4 * hh_, 4 * hh_ + 4)], [*w, t_oh, t_id])
                        te.append(do(AC, lambda e, b=b, hh_=hh_: e.activation(
                            OT[:, 4 * hh_:4 * hh_ + 4, :].rearrange("p a b -> p (a b)"), PS[:, b, :], ACT.Copy), [t]))
                        rfree(b, te[-1])
                    yield
                    tr = []
                    for hh_ in range(2):
                        b, w = rtake()
                        t = do(PE, [lambda e, b=b, c=c: e.matmul(
                            PS[:, b, c % 4 * 128:c % 4 * 128 + 128], OT[:, c, :], bd[:], start=True, stop=True)
                            for c in range(4 * hh_, 4 * hh_ + 4)], [*w, te[hh_], t_bd])
                        tr.append(do(AC, lambda e, b=b, hh_=hh_: e.activation(
                            RR[:, 4 * hh_:4 * hh_ + 4, :].rearrange("p a b -> p (a b)"), PS[:, b, :], ACT.Copy), [t]))
                        rfree(b, tr[-1])
                    tc_ = [None, None]
                    for c in range(8):
                        tt = tmp[c % 2][:].rearrange("p (j i e) -> p j i e", j=4, i=4)
                        r_ = RR[:, c, :].rearrange("p (j e) -> p j e", j=4).unsqueeze(2).to_broadcast([128, 4, 4, 32])
                        o_ = OH[:, c * 8:c * 8 + 4, :].unsqueeze(1).to_broadcast([128, 4, 4, 32])
                        t = do(DV, lambda e, tt=tt, r_=r_, o_=o_: e.tensor_tensor(tt, r_, o_, ALU.mult),
                               [tr[c // 4], t_oh, t_bd, tc_[c % 2]])
                        tc_[c % 2] = do(DV, lambda e, c=c: e.tensor_reduce(
                            cand[:, c * 4:c * 4 + 4, :].rearrange("p a b -> p (a b)"), tmp[c % 2][:].rearrange("p (q e) -> p q e", e=32), X, ALU.add), [t])
                    t = do(DV, lambda e: e.tensor_reduce(best[:], cand[:], X, ALU.max), [tc_[1]])
                    i4b = i48.unsqueeze(1).to_broadcast([128, 32, 4])
                    tb = t
                    t = do(DV, lambda e: e.tensor_tensor(e4[:], cand[:], up(best[:], 4), ALU.is_equal), [tb])
                    t = do(DV, lambda e: e.tensor_tensor(e4[:], e4[:], i4b, ALU.mult), [t])
                    t = do(DV, lambda e: e.tensor_reduce(fi[:], e4[:], X, ALU.min), [t])
                    t = do(DV, lambda e: e.tensor_tensor(e4[:], up(fi[:], 4), i4b, ALU.is_equal), [t])
                    v3 = v8[:, :, 4:8]
                    ge3, wa3 = ge[:].rearrange("p (c j) -> p c j", j=4), wa[:].rearrange("p (c j) -> p c j", j=4)
                    tg_ = do(DV, lambda e: e.tensor_scalar(ge[:], best[:], 0.5, None, ALU.is_ge), [tb])
                    ta = do(DV, lambda e: e.tensor_tensor(wa3, v3, ge3, ALU.mult), [tg_, t_wt])
                    t2 = do(DV, lambda e: e.tensor_tensor(co[:, :, 4:8], v3, wa3, ALU.subtract), [ta])
                    t = do(DV, lambda e: e.tensor_tensor(e4[:], e4[:], up(wa[:], 4), ALU.mult), [t, ta])
                    t = do(DV, lambda e: e.tensor_reduce(ac_[:], e4[:].rearrange("p (c j) i -> p c i j", j=4), X, ALU.add), [t])
                    t = do(DV, lambda e: e.tensor_tensor(co[:, :, 0:4], v8[:, :, 0:4], ac_[:], ALU.add), [t])
                    t = do(DV, lambda e: e.tensor_tensor(OH[:], OH[:], up(co[:].rearrange("p a b -> p (a b)"), 32), ALU.mult), [t, t2])
                    t = do(DV, lambda e: e.tensor_reduce(cw[:], OH[:].rearrange("p (c r) e -> p c e r", r=8), X, ALU.add), [t])
                    for z in range(3):
                        cz = c3[:, :, 32 * z:32 * z + 32]
                        t = do(DV, lambda e, cz=cz: e.tensor_copy(cz, cw[:]), [t])
                        if z < 2:
                            t = do(DV, lambda e, cz=cz: e.tensor_tensor(cw[:], cw[:], cz, ALU.subtract), [t])
                    yield
                    b, w = rtake()
                    pb = PS[0:96, b, :].bitcast(BF)
                    t = do(PE, [lambda e, c=c, pb=pb: e.transpose(pb[:, c * 128:(c + 1) * 128], c3[:, c, :], idb[:, :])
                                for c in range(8)], [*w, t, t_g])
                    t_cw = do(AC, lambda e, pb=pb: e.activation(cwT[:], pb, ACT.Copy), [t])
                    rfree(b, t_cw)
                    state["cw"] = t_cw
                    yield

                r4, hr, sg, hf, hh, hl, front, down = gated(c1, xh, xl, "m_")
                NPRE = 8
                pre = [sb(f"m_pre{i}", [128, 512], F32, c1) for i in range(2 * NPRE)]
                ub = [sb(f"m_ub{i}", [128, 512], F32, c1) for i in range(2)]
                ur = Ring(2)
                t_pre = {}

                def gu_of(j):
                    v = lambda W: W[:].rearrange("p a b -> p (a b)")[:, j % 6 * 512:j % 6 * 512 + 512].rearrange(
                        "p (g k m) -> p g k m", g=2, k=2)
                    return v(WH), v(WL)

                def dn_of(j):
                    return [xq[z][:].rearrange("p a b -> p (a b)")[:, j % 8 * 256:j % 8 * 256 + 256] for z in (2, 3)]

                def fronted(j, h):
                    bg, tg, bu, tu = front(gu_of(j), h, [state["gu", j], *[t for bb in (2 * h, 2 * h + 1) for t in state["xs", bb]]])
                    state.setdefault(("guu", j), []).append(tu)
                    return bg, tg, bu, tu

                def early(j, h):
                    bg, tg, bu, tu = fronted(j, h)
                    p_ = pre[2 * j + h]
                    ts = do(AC, lambda e: e.activation(p_[:], PS[:, bg, :], ACT.Silu), [tg])
                    r4.free(bg, ts)
                    i, w = ur.take()
                    t = do(AC, lambda e: e.activation(ub[i][:], PS[:, bu, :], ACT.Copy), [tu, *w])
                    r4.free(bu, t)
                    t_pre[j, h] = do(PO, lambda e: e.tensor_tensor(p_[:], p_[:], ub[i][:], ALU.mult), [ts, t])
                    ur.free(i, t_pre[j, h])

                def weighed(j, h):
                    if j >= NPRE:
                        bg, tg, bu, tu = fronted(j, h)
                    b, w = r4.take()
                    tcb = do(PE, lambda e: e.matmul(PS[:, b, :], sel[:, j * 128:(j + 1) * 128],
                                                    cwT[:, h * 512:(h + 1) * 512], start=True, stop=True), [*w, state["cw"]])
                    i, hw = hr.take()
                    if j >= NPRE:
                        ts = do(AC, lambda e: e.activation(sg[i][:], PS[:, bg, :], ACT.Silu), [tg, *hw])
                        r4.free(bg, ts)
                        t = do(DV, lambda e: e.tensor_tensor(sg[i][:], sg[i][:], PS[:, bu, :], ALU.mult), [ts, tu])
                        r4.free(bu, t)
                        src = sg[i]
                    else:
                        src, t = pre[2 * j + h], t_pre[j, h]
                    t = do(DV, lambda e: e.tensor_tensor(hf[i][:], src[:], PS[:, b, :], ALU.mult), [t, tcb, *hw])
                    r4.free(b, t)
                    return j, h, i, split(hf[i][:], hh[i][:], hl[i][:], [t], hw)

                def multiplied(u, last=False):
                    j, h, i, t_h = u
                    waits = [*t_h, state["dn", j], *([w for us in rb4.users for w in us] if j == 0 else [])]
                    t = down(h, i, dn_of(j), waits, last)
                    state.setdefault(("dnu", j), []).append(t)
                    if h == 1 and j + 8 < 24:
                        dn_load(j + 8)
                    return t

                route = router()
                next(route)
                order = [(0, 0), (1, 0), (0, 1), (1, 1)] + [(j, h) for j in range(2, NPRE) for h in range(2)]
                for n, (j, h) in enumerate(order):
                    early(j, h)
                    if j + 6 < 24 and h == 1:
                        moe_load(j + 6, PO)
                    if n in (3, 4, 12):
                        next(route)
                pend = None
                for j in range(24):
                    for h in range(2):
                        u = weighed(j, h)
                        if h == 1 and NPRE - 2 < j + 5 < 24 and j >= NPRE:
                            if j + 6 < 24:
                                moe_load(j + 6, DV)
                        if pend:
                            multiplied(pend)
                        pend = u
                t_y = multiplied(pend, True)
                end = [do(DV, lambda e, j=j: e.tensor_tensor(
                    xt[:, 2 * j:2 * j + 2, :].rearrange("p a b -> p (a b)"), PS[:, 4 + j, :],
                    xt[:, 2 * j:2 * j + 2, :].rearrange("p a b -> p (a b)"), ALU.add), [t_y]) for j in range(4)]

        cm.close()
        c2 = ExitStack()
        with c2:
            if stages > 2:
                fence(end)
                banks = Ring(8)
                fh, fl = (sb(f"f_{n}", [128, 6, 512], FR, c2) for n in ("h", "l"))
                fdh, fdl = (sb(f"f_d{n}", [128, 6, 256], FR, c2) for n in ("h", "l"))
                fxh, fxl = (sb(f"f_x{n}", [128, 2, 1024], FR, c2) for n in ("h", "l"))
                t_fw = []
                for j in range(9):
                    i, w = wring.take()
                    if j < 6:
                        src, hi, lo = A["fgu"][j], fh[:, j, :], fl[:, j, :]
                    else:
                        q_ = 2 * (j - 6)
                        src, hi, lo = A["fdn"][:, q_ * 256:q_ * 256 + 512], fdh[:, q_:q_ + 2, :].rearrange("p a b -> p (a b)"), \
                            fdl[:, q_:q_ + 2, :].rearrange("p a b -> p (a b)")
                    wf = wst[i][:].rearrange("p a b -> p (a b)")
                    td = Q.dma(SP, [(wf.bitcast(I32), src)], w)
                    t = do(PO, lambda e, wf=wf: e.tensor_scalar(wf, wf.bitcast(I32), -128.0, 1.0, ALU.add, ALU.mult), [td])
                    th = do(PO, lambda e, wf=wf, hi=hi: e.tensor_scalar(hi, wf, 1.0, 1.0, ALU.mult, ALU.mult), [t])
                    tl = do(PO, lambda e, wf=wf, hi=hi, lo=lo: e.tensor_tensor(lo, wf, hi.bitcast(F32), ALU.subtract), [th])
                    wring.free(i, tl)
                    t_fw.append(tl)
                fsc = sb("f_sc", [128, 12 + 256], F32, c2)
                t_fs = Q.dma(SP, [(fsc[:], A["fsc"])])

                cl = ExitStack()
                with cl:
                    def sl(name, shape, dt=F32):
                        return sb("l_" + name, shape, dt, cl)
                    x2T = sl("x2T", [128, 2, 1024])
                    PT1 = sl("PT1", [128, 8, 256])
                    wdq = sl("wdq", [128, 2, 96])
                    wkvc = sl("wkvc", [128, 2, 64])
                    wuq = sl("wuq", [128, 16, 96])
                    wuk = sl("wuk", [128, 16, 64])
                    wuv = sl("wuv", [128, 16, 64])
                    QA = [sl(f"QA{i}", [128, 16, 256]) for i in range(2)]
                    wo = QA[1]
                    aw = sl("aw", [96, 16, 128])
                    wrt = sl("wrt", [96, 1024])
                    wkr = sl("wkr", [64, 2, 128])
                    tb_ = sl("tb", [128, 512 + 128 + 64])
                    seg = sl("seg", [128, 8], I32)
                    segf = sl("segf", [128, 8])
                    dd = sl("dd", [128, 8, 64])
                    mk = sl("mk", [128, 8, 64])
                    td1 = Q.dma(AC, [(wdq[:], A["wdq"]), (wkvc[:], A["wkvc"]), (wkr[:], A["wkr"]), (tb_[:], A["rope"]), (seg[:], A["seg"])])
                    td2 = Q.dma(AC, [(wuq[:], A["wuq"]), (wuk[:], A["wuk"]), (aw[:, :, 64:128], A["wqr"]), (wrt[:], A["wrt"])])
                    td3 = Q.dma(AC, [(wuv[:], A["wuv"]), (wo[:], A["wo"])])
                    qcT = sl("qcT", [96, 1024])
                    KA = sl("KA", [128, 256])
                    K2 = sl("K2", [128, 256])
                    kt = sl("kt", [128, 2, 256])
                    KZ = sl("KZ", [128, 4, 2, 64])
                    BDK = sl("BDK", [128, 4, 128])
                    Bp = sl("Bp", [128, 8, 256])
                    QB = [sl(f"QB{i}", [128, 8, 256]) for i in range(2)]
                    S = [sl(f"S{i}", [128, 1024]) for i in range(2)]
                    s16 = [sl(f"s16{i}", [128, 2, 16]) for i in range(2)]
                    CT = x2T[:].rearrange("p k (a t) -> p (k a) t", t=256)

                    t = do(DV, lambda e: e.tensor_copy(segf[:], seg[:]), [td1])
                    t = do(DV, lambda e: e.tensor_tensor(dd[:], segf[:].unsqueeze(2).to_broadcast([128, 8, 64]),
                                                         tb_[:, 640:704].unsqueeze(1).to_broadcast([128, 8, 64]), ALU.subtract), [t])
                    t = do(DV, lambda e: e.tensor_scalar(mk[:], dd[:], 0.0, None, ALU.is_ge), [t])
                    t = do(DV, lambda e: e.scalar_tensor_tensor(mk[:], dd[:], 8.0, mk[:], ALU.is_le, ALU.mult), [t])
                    t_mk = do(DV, lambda e: e.tensor_scalar(mk[:], mk[:], NEG, -NEG, ALU.mult, ALU.add), [t])
                    tz1 = do(DV, lambda e: e.memset(KZ[:], 0.0))
                    tz2 = do(DV, lambda e: e.memset(BDK[:], 0.0))

                    b, w = banks.take()
                    t = do(PE, [lambda e, b=b, k=k: e.matmul(PS[0:64, b, 0:256], wkvc[:, k, :], ctxT[:, k, :],
                                                             start=(k == 0), stop=(k == 1)) for k in range(2)], [*w, td1, t_ctx])
                    t_ka = do(AC, lambda e, b=b: e.activation(KA[0:64, :], PS[0:64, b, 0:256], ACT.Copy), [t])
                    banks.free(b, t_ka)
                    b, w = banks.take()
                    t = do(PE, [lambda e, b=b, bb=bb, k=k, o=o: e.matmul(
                        PS[o:o + 64, b, bb * 64:(bb + 1) * 64], ctxT[:, k, bb * 64:(bb + 1) * 64], wkvc[:, k, :],
                        start=(k == 0), stop=(k == 1)) for o in (0, 64) for bb in range(4) for k in range(2)], [*w])
                    for o in (0, 64):
                        t_bk = do(AC, lambda e, b=b, o=o: e.activation(
                            BDK[o:o + 64, :, o:o + 64], PS[o:o + 64, b, 0:256].rearrange("p (a c) -> p a c", a=4), ACT.Copy), [t, tz2])
                    banks.free(b, t_bk)
                    b, w = banks.take()
                    t = do(PE, [lambda e, b=b, z=z: e.matmul(PS[:, b, z * 256:(z + 1) * 256], wkr[:, z, :], KA[0:64, :],
                                                             start=True, stop=True) for z in range(2)], [*w, t_ka])
                    tk_ = [do(DV, lambda e, b=b, z=z: e.tensor_tensor(
                        kt[:, z, :].rearrange("p (a t) -> p a t", a=4), PS[:, b, z * 256:(z + 1) * 256].rearrange("p (a t) -> p a t", a=4),
                        tb_[:, 512 + 64 * z:576 + 64 * z].unsqueeze(1).to_broadcast([128, 4, 64]), ALU.mult), [t, td1]) for z in range(2)]
                    banks.free(b, *tk_)
                    t = do(DV, lambda e: e.tensor_tensor(K2[:], kt[:, 0, :], kt[:, 1, :], ALU.add), tk_)
                    t_kz = [do(AC, lambda e, o=o: e.activation(
                        KZ[o:o + 64, :, o // 64, :], kt[o:o + 64, 0, :].rearrange("p (a t) -> p a t", a=4), ACT.Copy), [t, tz1])
                        for o in ()]
                    k23 = K2[:].rearrange("p (a t) -> p a t", a=4)
                    t_kz += [do(AC, lambda e, o=o: e.activation(KZ[o:o + 64, :, o // 64, :], k23[o:o + 64], ACT.Copy), [t, tz1])
                             for o in (0, 64)]
                    t_kz.append(do(AC, lambda e: e.activation(KA[64:128, :], K2[64:128, :], ACT.Copy), [t]))
                    t_kz.append(t_ka)

                    t_aw = []
                    for z in range(2):
                        b, w = banks.take()
                        t = do(PE, [lambda e, b=b, h=h: e.matmul(PS[0:96, b, h % 8 * 64:h % 8 * 64 + 64], wuq[:, h, :], wuk[:, h, :],
                                                                 start=True, stop=True) for h in range(8 * z, 8 * z + 8)], [*w, td2])
                        t_aw.append(do(AC, lambda e, b=b, z=z: e.activation(
                            aw[:, 8 * z:8 * z + 8, 0:64], PS[0:96, b, :].rearrange("p (h c) -> p h c", h=8), ACT.Copy), [t]))
                        banks.free(b, t_aw[-1])
                    t_bp = []
                    for z in range(4):
                        b, w = banks.take()
                        t = do(PE, [lambda e, b=b, p=p, o=o: e.matmul(
                            PS[64 * o:64 * o + 64, b, p % 2 * 256:p % 2 * 256 + 256], wuv[:, 2 * p + o, :], wo[:, 2 * p + o, :],
                            start=True, stop=True) for o in range(2) for p in (2 * z, 2 * z + 1)], [*w, td3])
                        t_bp.append(do(AC, lambda e, b=b, z=z: e.activation(
                            Bp[:, 2 * z:2 * z + 2, :].rearrange("p a b -> p (a b)"), PS[:, b, :], ACT.Copy), [t]))
                        banks.free(b, t_bp[-1])

                    t_n = layernorm(xt, end, xn)
                    t_x2 = []

                    def ev2(k, h, b, t):
                        t = do(AC, lambda e: e.activation(x2T[:, k, h * 512:(h + 1) * 512], PS[:, b, :], ACT.Copy), [t])
                        t_x2.append(t)
                        return t
                    turn(xn, t_n, ev2)
                    t_qc = []
                    for h in range(2):
                        b, w = banks.take()
                        t = do(PE, [lambda e, b=b, k=k, h=h: e.matmul(PS[0:96, b, :], wdq[:, k, :], x2T[:, k, h * 512:(h + 1) * 512],
                                                                      start=(k == 0), stop=(k == 1)) for k in range(2)], [*w, *t_x2, td1])
                        t_qc.append(do(AC, lambda e, b=b, h=h: e.activation(qcT[:, h * 512:(h + 1) * 512], PS[0:96, b, :], ACT.Copy), [t]))
                        banks.free(b, t_qc[-1])

                    qu = {}

                    def queries(bb):
                        toks = []
                        i = bb % 2
                        for kind, n, W, dst, tab in (("A", 8, aw, QA[i], 0), ("B", 4, None, QB[i], 256)):
                            for p in range(n):
                                b, w = banks.take()
                                t = do(PE, [lambda e, b=b, hh=hh, p=p, kind=kind: e.matmul(
                                    PS[:, b, hh * 256:(hh + 1) * 256],
                                    aw[:, 2 * p + hh, :] if kind == "A" else wrt[:, (2 * p + hh) * 128:(2 * p + hh + 1) * 128],
                                    qcT[:, bb * 256:(bb + 1) * 256], start=True, stop=True) for hh in range(2)],
                                    [*w, *t_qc, *t_aw, td2])
                                toks.append(do(DV, lambda e, b=b, p=p, dst=dst, tab=tab: e.tensor_tensor(
                                    dst[:, 2 * p:2 * p + 2, :], PS[:, b, :].rearrange("p (a t) -> p a t", a=2),
                                    tb_[:, tab:tab + 256].unsqueeze(1).to_broadcast([128, 2, 256]), ALU.mult),
                                    [t, td1, *(t_bp if bb == 1 else []), *qu.get(bb - 2, [])]))
                                banks.free(b, toks[-1])
                        return toks

                    su = {}

                    def soft(c, tq):
                        bb, i = c // 2, c % 2
                        cc = c % 2 * 128
                        S_ = S[i]
                        ms = []
                        for z in range(2):
                            b, w = banks.take()
                            fns = []
                            for p in range(4 * z, 4 * z + 4):
                                fns.append(lambda e, b=b, p=p: e.matmul(
                                    PS[:, b, p % 4 * 128:p % 4 * 128 + 128], QB[bb % 2][:, p, cc:cc + 128],
                                    KZ[:, bb, :, :].rearrange("p a t -> p (a t)"), start=True, stop=False, skip_group_check=True))
                                for o in range(2):
                                    fns.append(lambda e, b=b, p=p, o=o: e.matmul(
                                        PS[:, b, p % 4 * 128 + o * 64:p % 4 * 128 + o * 64 + 64], QA[bb % 2][:, 2 * p + o, cc:cc + 128],
                                        KA[:, bb * 64:(bb + 1) * 64], start=False, stop=True, skip_group_check=True))
                            t = do(PE, fns, [*w, *tq, *t_kz])
                            ms.append(do(DV, lambda e, b=b, z=z: e.scalar_tensor_tensor(
                                S_[:, z * 512:(z + 1) * 512].rearrange("p (h t) -> p h t", h=8),
                                PS[:, b, :].rearrange("p (h t) -> p h t", h=8), float(1.0 / np.sqrt(np.float32(192.0))),
                                mk[:, c, :].unsqueeze(1).to_broadcast([128, 8, 64]), ALU.mult, ALU.add),
                                [t, t_mk, *su.get(i, [])]))
                            banks.free(b, ms[-1])
                        qu.setdefault(bb, []).append(t)
                        s3 = S_[:].rearrange("p (h t) -> p h t", h=16)
                        t = do(DV, lambda e: e.tensor_reduce(s16[i][:, 0, :], s3, X, ALU.max), ms)
                        t = do(DV, lambda e: e.tensor_tensor(s3, s3, s16[i][:, 0, :].unsqueeze(2).to_broadcast([128, 16, 64]), ALU.subtract), [t])
                        t = do(AC, lambda e: e.activation(S_[:], S_[:], ACT.Exp), [t])
                        t = do(DV, lambda e: e.tensor_reduce(s16[i][:, 1, :], s3, X, ALU.add), [t])
                        t = do(DV, lambda e: e.reciprocal(s16[i][:, 1, :], s16[i][:, 1, :]), [t])
                        return do(DV, lambda e: e.tensor_tensor(s3, s3, s16[i][:, 1, :].unsqueeze(2).to_broadcast([128, 16, 64]), ALU.mult), [t])

                    pu = {"PT": [], "CT": []}

                    def attend(bb, tsm):
                        te = []
                        for ci in range(2):
                            for z in range(2):
                                b, w = banks.take()
                                t = do(PE, [lambda e, b=b, p=p, ci=ci: e.transpose(
                                    PS[:, b, p % 4 * 128:p % 4 * 128 + 128], S[ci][:, p * 128:(p + 1) * 128], idf[:, :])
                                    for p in range(4 * z, 4 * z + 4)], [*w, tsm[ci]])
                                te.append(do(AC, lambda e, b=b, z=z, ci=ci: e.activation(
                                    PT1[:, 4 * z:4 * z + 4, ci * 128:(ci + 1) * 128], PS[:, b, :].rearrange("p (a t) -> p a t", a=4), ACT.Copy),
                                    [t, *pu["PT"]]))
                                banks.free(b, te[-1])
                            su[ci] = [t]
                        tcx = []
                        for z in range(4):
                            b, w = banks.take()
                            t = do(PE, lambda e, b=b, z=z: e.matmul(PS[:, b, :], BDK[:, bb, :], PT1[:, 2 * z:2 * z + 2, :].rearrange("p a b -> p (a b)"),
                                                                    start=True, stop=True), [*w, *te, t_bk])
                            tcx.append(do(AC, lambda e, b=b, z=z: e.activation(
                                CT[:, 2 * z:2 * z + 2, :].rearrange("p a b -> p (a b)"), PS[:, b, :], ACT.Copy), [t, *pu["CT"], *t_qc]))
                            banks.free(b, tcx[-1])
                        pu["PT"] = [t]
                        b, w = banks.take()
                        t = do(PE, [lambda e, b=b, ci=ci, p=p: e.matmul(
                            PS[:, b, ci * 256:(ci + 1) * 256], CT[:, p, ci * 128:(ci + 1) * 128], Bp[:, p, :],
                            start=(p == 0), stop=(p == 7)) for ci in range(2) for p in range(8)], [*w, *tcx, *t_bp])
                        pu["CT"] = [t]
                        xv = xt[:, 2 * bb:2 * bb + 2, :].rearrange("p a b -> p (a b)")
                        t = do(DV, lambda e, b=b: e.tensor_tensor(xv, PS[:, b, :], xv, ALU.add), [t, *t_n])
                        banks.free(b, t)
                        return t

                    tq = {0: queries(0)}
                    end = []
                    for bb in range(4):
                        ts = [soft(2 * bb, tq[bb]), soft(2 * bb + 1, tq[bb])]
                        if bb < 3:
                            tq[bb + 1] = queries(bb + 1)
                        end.append(attend(bb, ts))

                if stages > 3:
                    fence(end)
                    banks = Ring(8)
                    t_n = layernorm(xt, end, xn)
                    tx = []
                    split_turn(t_n, fxh, fxl, tx)

                    r4, hr, fsg, fhf, fhh, fhl, front, down = gated(c2, fxh, fxl, "f_")
                    pend = None
                    for j in range(6):
                        for h in range(2):
                            v = lambda a: a[:, j, :].rearrange("p (g k m) -> p g k m", g=2, k=2)
                            bg, tg, bu, tu = front((v(fh), v(fl)), h, [*tx, *t_fw])
                            i, hw = hr.take()
                            ts = do(AC, lambda e, i=i, bg=bg, j=j: e.activation(
                                fsg[i][:], PS[:, bg, :], ACT.Silu, scale=fsc[:, j:j + 1]), [tg, t_fs, *hw])
                            r4.free(bg, ts)
                            t = do(DV, lambda e, i=i, bu=bu, j=j: e.scalar_tensor_tensor(
                                fhf[i][:], PS[:, bu, :], fsc[:, 6 + j:7 + j], fsg[i][:], ALU.mult, ALU.mult), [ts, tu, *hw])
                            r4.free(bu, t)
                            t_h = split(fhf[i][:], fhh[i][:], fhl[i][:], [t], hw)
                            if pend:
                                down(*pend)
                            pend = (h, i, (fdh[:, j, :], fdl[:, j, :]), t_h)
                    t_y = down(*pend, last=True)
                    end = []
                    for j in range(4):
                        xv = xt[:, 2 * j:2 * j + 2, :]
                        nv = xn[:, 2 * j:2 * j + 2, :]
                        t = do(DV, lambda e, j=j, nv=nv: e.tensor_tensor(
                            nv, PS[:, 4 + j, :].rearrange("p (a b) -> p a b", a=2),
                            fsc[:, 12:268].unsqueeze(1).to_broadcast([128, 2, 256]), ALU.mult), [t_y, t_fs])
                        end.append(do(DV, lambda e, xv=xv, nv=nv: e.tensor_tensor(xv, xv, nv, ALU.add), [t]))

        t_out = Q.dma(SP, [(out.rearrange("(c p) d -> p c d", p=128), xt[:])], end)
        Q.wait(SP, [t_out])

        block = ctx.enter_context(nc.Block())

        @block.sync
        def _(e):
            Q.play(SP, e)

        @block.scalar
        def _(e):
            Q.play(AC, e)

        @block.vector
        def _(e):
            Q.play(DV, e)

        @block.tensor
        def _(e):
            Q.play(PE, e)

        @block.gpsimd
        def _(e):
            Q.play(PO, e)


def layout(v):
    f = np.ascontiguousarray
    g = {k: np.asarray(a) for k, a in v.items()}
    o = {}
    o["x"] = f(g["x"].reshape(1024, 256))
    o["ctxT"] = f(g["ctx_2048"].reshape(256, 256).T)
    o["idf"] = np.eye(128, dtype=np.float32)
    L = "L0_xattn_"
    two = lambda a: a.reshape(2, 128).T
    o["vec"] = f(np.concatenate([two(g[L + n]) for n in (
        "ln_w", "ln_b", "q_in_scale", "qx_in_scale", "k_in_scale", "v_in_scale")], axis=1))
    o["ln8"] = f(np.stack([g[L + n] for n in (
        "qln_w", "qln_b", "kln_w", "kln_b", "qxln_w", "qxln_b", "kxln_w", "kxln_b")], axis=1))
    s = g[L + "proj_smooth"].reshape(2, 4, 4, 128)
    o["smo"] = f(s.transpose(3, 1, 0, 2).reshape(128, 32))
    o["sca"] = f(np.tile(np.stack([g[L + n].reshape(()) for n in (
        "wq_scale", "wqx_scale", "wk_scale", "wv_scale", "proj_w_scale", "proj_in_scale")])[None], (128, 1)))
    q4 = lambda n, m: g[L + n].reshape(4, m, 2, 128).transpose(0, 3, 2, 1)
    o["wall"] = f(np.concatenate([q4("wq", 512), q4("wqx", 512), q4("wk", 256), q4("wv", 256)], axis=3))
    kv = g[L + "w_kv_x"].reshape(2, 4, 256, 2, 128)
    o["wkvx"] = f(kv.transpose(1, 4, 3, 0, 2).reshape(4, 128, 2, 512))
    wp = g[L + "wproj"].reshape(256, 2, 4, 4, 128)
    o["wproj"] = f(wp.transpose(2, 4, 1, 3, 0).reshape(4, 128, 8, 256))
    wg = g["L0_ffn_gate_up_proj"].reshape(32, 2, 96, 256).transpose(1, 0, 2, 3).reshape(2, 24, 128, 2, 128)
    o["wgu"] = f(wg.transpose(1, 4, 0, 3, 2))
    o["wdn"] = f(g["L0_ffn_down_proj"].transpose(0, 2, 1).reshape(24, 128, 256))
    o["gate"] = f(g["L0_ffn_gate_weight"].reshape(32, 2, 128).transpose(2, 1, 0).reshape(128, 64))
    o["sim"] = f(g["L0_ffn_similarity"])
    o["cst"] = f(np.tile(np.concatenate([np.arange(32), np.arange(4) - 8]).astype(np.float32)[None], (128, 1)))
    bf = mybir.dt.np(BF)
    o["idb"] = np.eye(128, dtype=np.float32).astype(bf)
    o["sel"] = f((np.arange(96)[:, None] % 32 == np.arange(3072)[None] // 96).astype(np.float32).astype(bf))
    M = "L1_xattn_"
    kp = lambda a: a.reshape(2, 128, -1).transpose(1, 0, 2)
    o["wdq"] = f(kp(g[M + "W_dq"]))
    o["wkvc"] = f(kp(g[M + "W_kvc"]))
    hT = lambda a: a.reshape(-1, 16, 128).transpose(2, 1, 0)
    o["wuq"], o["wuk"], o["wuv"] = f(hT(g[M + "W_uq"])), f(hT(g[M + "W_uk"])), f(hT(g[M + "W_uv"]))
    o["wo"] = f(g[M + "W_o"].reshape(16, 128, 256).transpose(1, 0, 2))
    o["wqr"] = f(g[M + "W_qr"].reshape(96, 16, 64))
    o["wrt"] = f(g[M + "W_qr"].reshape(96, 16, 2, 32)[:, :, ::-1].reshape(96, 1024))
    kr = g[M + "W_kr"]
    krr = kr.reshape(64, 2, 32)[:, ::-1].reshape(64, 64)
    o["wkr"] = f(np.stack([np.tile(kr, (1, 2)), np.tile(krr, (1, 2))], axis=1))
    half = np.arange(32, dtype=np.float32)
    inv = (np.float32(1.0) / np.float32(10000.0) ** (half / np.float32(32))).astype(np.float32)
    ang = np.arange(256, dtype=np.float32)[:, None] * inv
    cos, sin = np.cos(ang).T, np.sin(ang).T
    c4, s4 = np.tile(cos, (4, 1)), np.concatenate([-sin, sin, -sin, sin])
    ones = np.ones((64, 256), np.float32)
    o["rope"] = f(np.concatenate([np.concatenate([ones, c4[64:]]), s4, c4[:, :64], s4[:, :64],
                                  np.tile(np.arange(64, dtype=np.float32)[None], (128, 1))], axis=1).astype(np.float32))
    o["seg"] = f(g["itok_BxS_0_1023"].reshape(8, 128).T)
    F = "L1_ffn_"

    def wide(a):
        z = np.full((768, a.shape[1]), 128, a.dtype)
        z[:704] = a
        return z
    gu = np.stack([wide(g[F + "wq_gate"]), wide(g[F + "wq_up"])]).reshape(2, 6, 128, 2, 128)
    o["fgu"] = f(gu.transpose(1, 4, 0, 3, 2).reshape(6, 128, 512))
    o["fdn"] = f(wide(g[F + "wq_down"].T).reshape(6, 128, 256).transpose(1, 0, 2).reshape(128, 1536))
    sc = np.zeros((2, 768), np.float32)
    sc[0, :704], sc[1, :704] = g[F + "s_gate"], g[F + "s_up"]
    o["fsc"] = f(np.concatenate([sc.reshape(12, 128).T, np.tile(g[F + "s_down"][None], (128, 1))], axis=1))
    return o


def kernel(**inputs):
    import concourse.bacc as bacc
    from concourse.bass_utils import run_bass_kernel_spmd

    nc = bacc.Bacc("TRN2", target_bir_lowering=False, num_devices=1)
    arrays = layout(inputs)
    A = {n: nc.dram_tensor(f"in_{n}", a.shape, mybir.dt.from_np(a.dtype), kind="ExternalInput").ap()
         for n, a in arrays.items()}
    out = nc.dram_tensor("out_x", (1024, 256), F32, kind="ExternalOutput").ap()
    program(nc, A, out)
    r = run_bass_kernel_spmd(nc, [{f"in_{n}": a for n, a in arrays.items()}], core_ids=[0])
    return r.results[0]["out_x"].reshape(4, 256, 256)
```

```python
from contextlib import ExitStack

import concourse.bass as bass
from concourse import mybir
import numpy as np

ALU = mybir.AluOpType
ACT = mybir.ActivationFunctionType
F32 = mybir.dt.float32
FR = mybir.dt.float32r
BF = mybir.dt.bfloat16
U16 = mybir.dt.uint16
U32 = mybir.dt.uint32
I32 = mybir.dt.int32
X = mybir.AxisListType.X

PE, AC, DV, PO, SP = "pe", "ac", "dv", "po", "sp"
EPS = 1e-5
NEG = 1e30


class Queues:

    LIMIT = 3000

    def __init__(self, nc, ctx):
        self.nc, self.ctx = nc, ctx
        self.q = {e: [] for e in (PE, AC, DV, PO, SP)}
        self.sem, self.n, self.made = {}, {}, 0

    def fresh(self, name):
        self.made += 1
        return self.ctx.enter_context(self.nc.semaphore(f"{name}{self.made}"))

    def do(self, e, fns, waits=()):
        if e not in self.sem or self.n[e] >= self.LIMIT:
            self.sem[e], self.n[e] = self.fresh(f"s_{e}_"), 0
        self.n[e] += 1
        self.q[e].append(("run", tuple(w for w in waits if w), fns if isinstance(fns, list) else [fns], self.sem[e], 1))
        return (self.sem[e], self.n[e])

    def dma(self, e, pairs, waits=()):
        s = self.fresh("d_")
        for i, (o, a) in enumerate(pairs):
            self.q[e].append(("dma", tuple(w for w in waits if w) if i == 0 else (), (o, a), s, 16))
        return (s, 16 * len(pairs))

    def wait(self, e, waits):
        self.q[e].append(("wait", tuple(waits), None, None, 0))

    def play(self, e, eng):
        seen = {}
        for kind, waits, what, s, inc in self.q[e]:
            for ws, wv in waits:
                if seen.get(ws.name, 0) < wv:
                    eng.wait_ge(ws, wv)
                    seen[ws.name] = wv
            if kind == "run":
                for f in what:
                    ins = f(eng)
                ins.then_inc(s, inc)
            elif kind == "dma":
                eng.dma_start(what[0], what[1]).then_inc(s, inc)


def weave(*gens):
    gens = list(gens)
    while gens:
        for g in list(gens):
            try:
                next(g)
            except StopIteration:
                gens.remove(g)


def chain(*gens):
    for g in gens:
        yield from g()


class Ring:

    def __init__(self, n, base=0, users=None):
        self.n, self.at, self.base = n, 0, base
        self.users = [list(u) for u in users] if users else [[] for _ in range(n)]

    def take(self):
        i = self.at % self.n
        self.at += 1
        w, self.users[i] = self.users[i], []
        return i + self.base, w

    def free(self, i, *tokens):
        self.users[i - self.base] += tokens


def program(nc, A, out, stages=4):
    ctx = ExitStack()
    Q = Queues(nc, ctx)
    do = Q.do

    def bcast(ap, shape):
        return ap.to_broadcast(shape) if hasattr(ap, "to_broadcast") else ap.broadcast_to(shape)

    with ctx:
        def sb(name, shape, dt, c=ctx):
            return c.enter_context(nc.sbuf_tensor(name, shape, dt))

        PS = ctx.enter_context(nc.psum_tensor("PS", [128, 8, 512], F32))
        banks, obank = Ring(7), Ring(1, 7)

        xt = sb("xt", [128, 8, 256], F32)
        idf = sb("idf", [128, 128], F32)
        ctxT = sb("ctxT", [128, 2, 256], F32)
        st = sb("st", [128, 8, 6], F32)
        mv = sb("mv", [128, 8, 2], F32)
        rs = sb("rs", [128, 8], F32)
        xn = sb("xn", [128, 8, 256], F32)

        xin = A["x"].rearrange("(c p) d -> p c d", p=128)
        t_x = [Q.dma(SP, [(xt[:, 4 * h:4 * h + 4, :], xin[:, 4 * h:4 * h + 4, :])]) for h in range(2)]
        t_id = Q.dma(AC, [(idf[:], A["idf"])])
        t_ctx = Q.dma(AC, [(ctxT[:], A["ctxT"].rearrange("(k p) t -> p k t", p=128))])

        NWS = 3
        NWS = 3
        wst = [sb(f"wst{i}", [128, 2, 256], F32) for i in range(NWS)]
        wring = Ring(NWS)
        state = {}
        r2 = sb("r2", [128, 8], F32)
        ve = sb("ve", [128, 8], F32)
        nt = sb("nt", [128, 8], F32)
        dring = Ring(2)

        def newton(y, v, n, t):
            t = do(DV, lambda e: e.tensor_tensor(n, y, y, ALU.mult), [t])
            t = do(DV, lambda e: e.tensor_tensor(n, n, v, ALU.mult), [t])
            t = do(DV, lambda e: e.tensor_scalar(n, n, -0.5, 1.5, ALU.mult, ALU.add), [t])
            return do(DV, lambda e: e.tensor_tensor(y, y, n, ALU.mult), [t])

        def root(y, v, n, ready):
            t = do(DV, lambda e: e.tensor_scalar(v, v, EPS, None, ALU.add), ready)
            t = do(AC, lambda e: e.activation(y, v, ACT.Sqrt), [t])
            t = do(DV, lambda e: e.reciprocal(y, y), [t])
            return newton(y, v, n, t)

        def layernorm_twice(half, ready):
            cs, b2 = range(4 * half, 4 * half + 4), slice(4 * half, 4 * half + 4)
            for c in cs:
                t = do(DV, lambda e, c=c: e.bn_stats(st[:, c, :], xt[:, c, :]), ready)
            for c in cs:
                t = do(DV, lambda e, c=c: e.bn_aggr(mv[:, c, :], st[:, c, :]), [t])
            t = do(DV, lambda e: e.tensor_copy(ve[:, b2], mv[:, b2, 1]), [t])
            t = root(rs[:, b2], ve[:, b2], nt[:, b2], [t])
            t = do(DV, lambda e: e.tensor_tensor(ve[:, b2], rs[:, b2], rs[:, b2], ALU.mult), [t])
            t = do(DV, lambda e: e.tensor_tensor(ve[:, b2], ve[:, b2], mv[:, b2, 1], ALU.mult), [t])
            t = root(r2[:, b2], ve[:, b2], nt[:, b2], [t])
            t = do(DV, lambda e: e.tensor_tensor(rs[:, b2], rs[:, b2], r2[:, b2], ALU.mult), [t])
            return [do(DV, lambda e, c=c: e.tensor_scalar(xn[:, c, :], xt[:, c, :], mv[:, c, 0:1], rs[:, c:c + 1],
                                                          ALU.subtract, ALU.mult), [t]) for c in cs]

        def rsqrt(v, y, n, ready, eng, out):
            t = do(DV, lambda e: e.tensor_scalar(v, v, EPS, None, ALU.add), ready)
            yield
            t = do(DV, lambda e: e.tensor_scalar(y.bitcast(I32), v.bitcast(I32), 1, None, ALU.logical_shift_right), [t])
            yield
            t = do(DV, lambda e: e.tensor_scalar(y.bitcast(I32), y.bitcast(I32), -1.0, float(0x5F3759DF), ALU.mult, ALU.add), [t])
            yield
            for _ in range(3):
                for f in (lambda e: e.tensor_tensor(n, y, y, ALU.mult), lambda e: e.tensor_tensor(n, n, v, ALU.mult),
                          lambda e: e.tensor_scalar(n, n, -0.5, 1.5, ALU.mult, ALU.add),
                          lambda e: e.tensor_tensor(y, y, n, ALU.mult)):
                    t = do(eng, f, [t])
                    if eng == DV:
                        yield
            out.append(t)

        def split(src, hi, lo, ready, users, eh=AC, el=DV):
            if eh == AC:
                th = do(AC, lambda e: e.activation(hi, src, ACT.Copy), [*ready, *users])
            else:
                th = do(eh, lambda e: e.tensor_copy(hi, src), [*ready, *users])
            tl = do(el, lambda e: e.tensor_tensor(lo, src, hi.bitcast(F32), ALU.subtract), [*ready, th, *users])
            return [th, tl]

        def ln_steps(bb, ready, n, done):
            cs, b2 = range(2 * bb, 2 * bb + 2 * n), slice(2 * bb, 2 * bb + 2 * n)
            for c in cs:
                t = do(DV, lambda e, c=c: e.bn_stats(st[:, c, :], xt[:, c, :]), ready)
                yield
            for c in cs:
                ta = do(DV, lambda e, c=c: e.bn_aggr(mv[:, c, :], st[:, c, :]), [t])
                yield
            got = []
            yield from rsqrt(mv[:, b2, 1], rs[:, b2], nt[:, b2], [ta], DV, got)
            for c in cs:
                t = do(DV, lambda e, c=c: e.tensor_scalar(xn[:, c, :], xt[:, c, :], mv[:, c, 0:1], rs[:, c:c + 1],
                                                          ALU.subtract, ALU.mult), got)
                yield
            done(t)

        def ln_batch(bb, ready):
            got = []
            weave(ln_steps(bb, ready, 1, got.append))
            return got[0]

        def turn_batch(bb, t_n, evac):
            b, w = banks.take()
            t = do(PE, [lambda e, b=b, k=k, ci=ci: e.transpose(
                PS[:, b, k * 256 + ci * 128:k * 256 + ci * 128 + 128], xn[:, 2 * bb + ci, k * 128:(k + 1) * 128], idf[:, :])
                for k in range(2) for ci in range(2)], [*w, t_n, t_id])
            r = evac(b, t)
            banks.free(b, *r)
            return r

        def turn(src, t_src, evac, halves=(0, 1)):
            for h in halves:
                for k in range(2):
                    b, w = banks.take()
                    t = do(PE, [lambda e, b=b, c=c, k=k: e.transpose(PS[:, b, (c % 4) * 128:(c % 4 + 1) * 128],
                                                                    src[:, c, k * 128:(k + 1) * 128], idf[:, :])
                                for c in range(4 * h, 4 * h + 4)], [*w, *t_src[4 * h:4 * h + 4], t_id])
                    banks.free(b, evac(k, h, b, t))

        cm = ctx.enter_context(ExitStack())
        xq = [sb(f"xq{i}", [128, 2, 1024], FR, cm) for i in range(4)]
        WH = sb("WH", [128, 2, 1536], FR, cm)
        WL = sb("WL", [128, 2, 1536], FR, cm)
        dst_ = [sb(f"dst{i}", [128, 256], F32, cm) for i in range(2)]

        def sl(name, shape, dt=F32, c=ctx):
            return sb("l_" + name, shape, dt, c)
        wdq = sl("wdq", [128, 2, 96])
        wkvc = sl("wkvc", [128, 2, 64])
        wkr = sl("wkr", [64, 2, 128])
        tb_ = sl("tb", [128, 512 + 128 + 64])
        KA = sl("KA", [128, 256])
        K2 = sl("K2", [128, 256])
        kt = sl("kt", [128, 2, 256])
        KZ = sl("KZ", [128, 4, 2, 64])
        BDK = sl("BDK", [128, 4, 128])
        tk = {}

        def keys():
            td1 = Q.dma(SP, [(wdq[:], A["wdq"]), (wkvc[:], A["wkvc"]), (wkr[:], A["wkr"]), (tb_[:], A["rope"])])
            tk["tb"] = td1
            tz1 = do(PO, lambda e: e.memset(KZ[:], 0.0))
            tz2 = do(PO, lambda e: e.memset(BDK[:], 0.0))
            yield
            b, w = banks.take()
            t = do(PE, [lambda e, b=b, k=k: e.matmul(PS[0:64, b, 0:256], wkvc[:, k, :], ctxT[:, k, :],
                                                     start=(k == 0), stop=(k == 1)) for k in range(2)], [*w, td1, t_ctx])
            t_ka = do(AC, lambda e, b=b: e.activation(KA[0:64, :], PS[0:64, b, 0:256], ACT.Copy), [t])
            banks.free(b, t_ka)
            b, w = banks.take()
            t = do(PE, [lambda e, b=b, bb=bb, k=k, o=o: e.matmul(
                PS[o:o + 64, b, bb * 64:(bb + 1) * 64], ctxT[:, k, bb * 64:(bb + 1) * 64], wkvc[:, k, :],
                start=(k == 0), stop=(k == 1)) for o in (0, 64) for bb in range(4) for k in range(2)], w)
            for o in (0, 64):
                tk["bk"] = do(AC, lambda e, b=b, o=o: e.activation(
                    BDK[o:o + 64, :, o:o + 64], PS[o:o + 64, b, 0:256].rearrange("p (a c) -> p a c", a=4), ACT.Copy), [t, tz2])
            banks.free(b, tk["bk"])
            b, w = banks.take()
            t = do(PE, [lambda e, b=b, z=z: e.matmul(PS[:, b, z * 256:(z + 1) * 256], wkr[:, z, :], KA[0:64, :],
                                                     start=True, stop=True) for z in range(2)], [*w, t_ka])
            te = do(AC, lambda e, b=b: e.activation(kt[:].rearrange("p a b -> p (a b)"), PS[:, b, :], ACT.Copy), [t])
            banks.free(b, te)
            for z in range(2):
                t = do(PO, lambda e, z=z: e.tensor_tensor(
                    kt[:, z, :].rearrange("p (a t) -> p a t", a=4), kt[:, z, :].rearrange("p (a t) -> p a t", a=4),
                    tb_[:, 512 + 64 * z:576 + 64 * z].unsqueeze(1).to_broadcast([128, 4, 64]), ALU.mult), [te, td1])
            t = do(PO, lambda e: e.tensor_tensor(K2[:], kt[:, 0, :], kt[:, 1, :], ALU.add), [t])
            k23 = K2[:].rearrange("p (a t) -> p a t", a=4)
            tk["kz"] = [do(AC, lambda e, o=o: e.activation(KZ[o:o + 64, :, o // 64, :], k23[o:o + 64], ACT.Copy), [t, tz1])
                        for o in (0, 64)]
            tk["kz"].append(do(AC, lambda e: e.activation(KA[64:128, :], K2[64:128, :], ACT.Copy), [t]))
            tk["kz"].append(t_ka)
            yield
            td2 = Q.dma(SP, [(wuq[:], A["wuq"]), (wuk[:], A["wuk"]), (aw[:, :, 64:128], A["wqr"]), (wrt[:], A["wrt"])])
            yield
            tk["aw"] = [td2]
            for z in range(2):
                b, w = banks.take()
                t = do(PE, [lambda e, b=b, h=h: e.matmul(PS[0:96, b, h % 8 * 64:h % 8 * 64 + 64], wuq[:, h, :], wuk[:, h, :],
                                                         start=True, stop=True) for h in range(8 * z, 8 * z + 8)], [*w, td2])
                tk["aw"].append(do(AC, lambda e, b=b, z=z: e.activation(
                    aw[:, 8 * z:8 * z + 8, 0:64], PS[0:96, b, :].rearrange("p (h c) -> p h c", h=8), ACT.Copy), [t]))
                banks.free(b, tk["aw"][-1])
            yield

        c0 = ExitStack()
        with c0:
            vec = sb("vec", [128, 12], F32, c0)
            ln8 = sb("ln8", [128, 8], F32, c0)
            smo = sb("smo", [128, 32], F32, c0)
            sca = sb("sca", [128, 6], F32, c0)
            t_vec = Q.dma(AC, [(vec[:], A["vec"]), (ln8[:], A["ln8"]), (smo[:], A["smo"]), (sca[:], A["sca"])])
            ivec = sb("ivec", [128, 4, 2], F32, c0)
            ismo = sb("ismo", [128, 32], F32, c0)
            sproj = sb("sproj", [128, 1], F32, c0)

            nivec = sb("nivec", [128, 4, 2], F32, c0)
            yb = sb("yb0", [128, 2, 512], BF, c0)
            fb = sb("fb0", [128, 2, 512], BF, c0)
            with ExitStack() as cq:
                lnT = sb("lnT", [128, 2, 1024], F32, cq)
                tbs = sb("tbs", [128, 2, 2, 512], F32, cq)
                rb = sb("rb", [128, 2, 512], F32, cq)
            PH = sb("PH", [128, 8, 256], FR, c0)
            PL = sb("PL", [128, 8, 256], FR, c0)
            cat = sb("cat", [128, 8, 256], FR, c0)
            t_ln = [[], []]

            def ev_ln(k, h, b, t):
                t = do(AC, lambda e: e.activation(lnT[:, k, h * 512:(h + 1) * 512], PS[:, b, :], ACT.Identity,
                                                  bias=vec[:, 2 + k:3 + k], scale=vec[:, k:k + 1]), [t, t_vec])
                t_ln[h].append(t)
                return t

            t_h0 = []

            def start(h):
                t_h = layernorm_twice(h, [t_x[h]])
                t_h0.append(t_h[-1])
                turn(xn, [None] * (4 * h) + t_h, ev_ln, (h,))

            first = layernorm_twice(0, [t_x[0]])
            t_h0.append(first[-1])
            t_iv = do(DV, lambda e: e.reciprocal(ivec[:].rearrange("p a b -> p (a b)"), vec[:, 4:12]), [t_vec])
            t_is = do(DV, lambda e: e.reciprocal(ismo[:, :], smo[:, :]), [t_vec])
            t_sp = do(DV, lambda e: e.tensor_tensor(sproj[:], sca[:, 4:5], sca[:, 5:6], ALU.mult), [t_vec])
            t_l8 = [do(DV, lambda e, j=j: e.tensor_scalar(ln8[:, j:j + 2], ln8[:, j:j + 2], float(128 ** -0.5), None, ALU.mult),
                       [t_vec]) for j in (0, 4)]
            t_niv = do(DV, lambda e: e.tensor_scalar(nivec[:], ivec[:], -1.0, None, ALU.mult), [t_iv])
            def quant(y, tmpF, tmpT, dst, t_y, free, done):
                t = do(DV, lambda e: e.tensor_scalar(y, y, 448.0, -448.0, ALU.min, ALU.max), [*t_y])
                yield
                t = do(DV, lambda e: e.tensor_scalar(tmpF.bitcast(U16), y.bitcast(U16), 0x7F80, 0x0040,
                                                     ALU.bitwise_and, ALU.bitwise_or), [t, *free])
                yield
                t = do(DV, lambda e: e.tensor_scalar(tmpF, tmpF, 1.5 * 2.0 ** -6, None, ALU.max), [t])
                yield
                t = do(DV, lambda e: e.scalar_tensor_tensor(tmpT, tmpF, float(2 ** 20), y, ALU.mult, ALU.add), [t])
                yield
                done(do(DV, lambda e: e.scalar_tensor_tensor(dst, tmpF, -float(2 ** 20), tmpT, ALU.mult, ALU.add), [t]))
                yield

            t_xq = {}
            t_q = {}
            QORDER = [(h, i) for h in range(2) for i in (2, 3, 0, 1)]

            def div(n):
                h, i = QORDER[n]
                for k in range(2):
                    t_q[n] = do(AC, lambda e, k=k: e.activation(
                        tbs[:, n % 2, k, :], lnT[:, k, h * 512:(h + 1) * 512], ACT.Copy, scale=ivec[:, i, k:k + 1]),
                        [t_iv, *t_ln[h], t_xq.get(n - 2)])

            def quantise(n):
                h, i = QORDER[n]
                tr, ts = [], []
                for k in range(2):
                    x_, q_, s_ = lnT[:, k, h * 512:(h + 1) * 512], tbs[:, n % 2, k, :], vec[:, 4 + 2 * i + k:5 + 2 * i + k]
                    tr.append(do(DV, lambda e, k=k, x_=x_, q_=q_, s_=s_: e.scalar_tensor_tensor(
                        rb[:, k, :], q_, s_, x_, ALU.mult, ALU.subtract), [t_q[n], t_xq.get(n - 1)]))
                    yield
                for k in range(2):
                    q_ = tbs[:, n % 2, k, :]
                    ts.append(do(DV, lambda e, k=k, q_=q_: e.scalar_tensor_tensor(
                        yb[:, k, :], rb[:, k, :], nivec[:, i, k:k + 1], q_, ALU.mult, ALU.add), [tr[k], t_niv]))
                    yield

                def done(t):
                    t_xq[n] = t_xq[h, i] = t
                yield from quant(yb[:], fb[:], tbs[:, n % 2, :, :], xq[i][:, :, h * 512:(h + 1) * 512], ts, [], done)
                if n < 2:
                    div(n + 2)

            w_users = [[] for _ in range(6)]

            def pieces(src, hi, lo, users, scale=None, eh=PO, el=PO):
                i, w = wring.take()
                t = Q.dma(SP, [(wst[i][:], src)], w)
                if scale is not None:
                    for k in range(2):
                        ts = do(PO, lambda e, i=i, k=k: e.tensor_scalar(
                            wst[i][:, k, :], wst[i][:, k, :], scale[:, k:k + 1], 1.0, ALU.mult, ALU.mult), [t, t_vec])
                    t = ts
                if eh == AC:
                    th = do(AC, lambda e, i=i: e.activation(hi, wst[i][:], ACT.Copy), [t, *users])
                else:
                    th = do(PO, lambda e, i=i: e.tensor_scalar(hi, wst[i][:], 1.0, 1.0, ALU.mult, ALU.mult), [t, *users])
                tl = do(el, lambda e, i=i: e.tensor_tensor(lo, wst[i][:], hi.bitcast(F32), ALU.subtract), [th, *users])
                wring.free(i, tl)
                return tl

            def load_w(gp, js=range(6)):
                toks = state.setdefault(("w", gp), {})
                for j in js:
                    s, o = (0, 0, 1, 1, 2, 3)[j], slice(j * 256, (j + 1) * 256)
                    toks[j] = pieces(A["wall"][gp, :, :, o], WH[:, :, o], WL[:, :, o], w_users[j], vec[:, 4 + 2 * s:6 + 2 * s])
                    w_users[j] = []

            def load_p(gp, j, users, eh=AC, el=DV):
                state.setdefault(("p", gp), {})[j] = pieces(
                    A["wproj"][gp, :, 2 * j:2 * j + 2, :], PH[:, 2 * j:2 * j + 2, :], PL[:, 2 * j:2 * j + 2, :], users, None, eh, el)

            qT = [sb(f"qT{i}", [128, 4, 256], F32, c0) for i in range(2)]
            qxT = [sb(f"qxT{i}", [128, 4, 256], F32, c0) for i in range(2)]
            kT = [sb(f"kT{i}", [128, 2, 256], F32, c0) for i in range(2)]
            NP_ = 5
            P = [sb(f"P{i}", [128, 2, 256], F32, c0) for i in range(NP_)]
            raw = sb("raw", [128, 4, 1280], F32, c0)
            raws = Ring(4)
            vr = sb("vr", [128, 8, 256], F32, c0)
            vrs = Ring(8)
            kraw = sb("kraw", [128, 2, 256], F32, c0)
            vx = sb("vx", [64, 4, 256], F32, c0)
            st6 = sb("st6", [128, 24, 6], F32, c0)
            mvq = sb("mvq", [128, 2, 20, 2], F32, c0)
            rsq = sb("rsq", [128, 2, 20], F32, c0)
            ntq = sb("ntq", [128, 20], F32, c0)
            mvk = sb("mvk", [128, 4, 2], F32, c0)
            rsk = sb("rsk", [128, 4], F32, c0)
            kxT = sb("kxT", [128, 2, 256], F32, c0)
            sm = [sb(f"sm{i}", [128, 3, 8], F32, c0) for i in range(NP_)]
            smr = Ring(NP_)
            NPT = 4
            PT = [sb(f"PT{i}", [128, 2, 256], F32, c0) for i in range(NPT)]
            ptr = Ring(NPT)
            yT = sb("yT", [128, 8, 256], BF, c0)
            yt = yb[:].rearrange("p a b -> p (a b)").bitcast(F32)
            yF = fb[:, 0, :]

            slot, vslot, t_st = {}, {}, {}

            SEG = [[(0, 0, 512, 0)], [(1, 512, 512, 0)], [(2, 1024, 256, 0), (3, 1280, 256, 256)]]

            def P1(gp, c, j):
                if (gp, c) not in slot:
                    slot[gp, c], state["rw", gp, c] = raws.take()
                    vslot[gp, c], state["vw", gp, c] = vrs.take()
                r, rv = slot[gp, c], vslot[gp, c]
                rw, vw = state["rw", gp, c], state["vw", gp, c]
                tw = state["w", gp]
                tc = slice(c * 128, (c + 1) * 128)
                b, w = banks.take()
                fns = []
                for s, w0, n, o in SEG[j]:
                    for k in range(2):
                        for i, W in enumerate((WH, WL)):
                            fns.append(lambda e, s=s, k=k, W=W, w0=w0, n=n, o=o, b=b, i=i: e.matmul(
                                PS[:, b, o:o + n], xq[s][:, k, tc], W[:, k, w0:w0 + n],
                                start=(k == 0 and i == 0), stop=(k == 1 and i == 1)))
                t = do(PE, fns, [*w, *[t_xq[c // 4, s] for s, _, _, _ in SEG[j]], tw[2 * j], tw[2 * j + 1]])
                ev = [do(AC, lambda e, s=s, w0=w0, n=n, o=o, b=b: e.activation(
                    vr[:, rv, :] if s == 3 else raw[:, r, w0:w0 + n], PS[:, b, o:o + n], ACT.Copy,
                    scale=sca[:, s:s + 1]), [t, *(vw if s == 3 else rw), t_vec])
                    for s, w0, n, o in SEG[j]]
                banks.free(b, *ev)
                w_users[2 * j] = [t]
                w_users[2 * j + 1] = [t]
                if j == 2:
                    state["v", gp, c] = ev[1]
                state["ev", gp, c, j] = ev[0]

            def ST(gp, c, j):
                r = slot[gp, c]
                par = (gp * 4 + c // 2) % 2
                o = c % 2 * 10
                hs = (range(0, 4), range(4, 8), range(8, 10))[j]
                for h in hs:
                    ts = do(DV, lambda e, h=h: e.bn_stats(st6[:, o + h, :], raw[:, r, h * 128:(h + 1) * 128]),
                            [state["ev", gp, c, j], state.get(("st", o, j))])
                    yield
                for h in hs:
                    ta = do(DV, lambda e, h=h: e.bn_aggr(mvq[:, par, o + h, :], st6[:, o + h, :]),
                            [ts, state.get(("nm", gp * 4 + c // 2 - 2))])
                    yield
                state["st", o, j] = ta
                t_st[gp, c, j] = ta

            def NM(s):
                gp, bb = s // 4, s % 4
                par = s % 2
                ready = [t_st[gp, c, j] for c in (2 * bb, 2 * bb + 1) for j in range(3)]
                got = []
                yield from rsqrt(mvq[:, par, :, 1], rsq[:, par, :], ntq[:, :], ready, PO, got)
                t = got[0]
                t = do(PO, lambda e: e.tensor_scalar(mvq[:, par, :, 0], mvq[:, par, :, 0], -1.0, 1.0, ALU.mult, ALU.mult), [t])
                for h in (8, 9, 0, 1, 2, 3, 4, 5, 6, 7):
                    for ci in range(2):
                        v = raw[:, slot[gp, 2 * bb + ci], h * 128:(h + 1) * 128]
                        tn = do(PO, lambda e, v=v, ci=ci, h=h: e.tensor_scalar(
                            v, v, mvq[:, par, ci * 10 + h, 0:1], rsq[:, par, ci * 10 + h:ci * 10 + h + 1],
                            ALU.add, ALU.mult), [t])
                        state["nmh", s, ci, h] = tn
                state["nm", s] = tn

            def KX(gp):
                i, w = wring.take()
                td = Q.dma(SP, [(wst[i][:], A["wkvx"][gp, :, :, 0:256])], w)
                b, w = banks.take()
                t = do(PE, [lambda e, c=c, k=k, b=b: e.matmul(
                    PS[:, b, c * 256:(c + 1) * 256], ctxT[:, k, c * 128:(c + 1) * 128], wst[i][:, k, :],
                    start=(k == 0), stop=(k == 1)) for c in range(2) for k in range(2)], [*w, td, t_ctx])
                wring.free(i, t)
                state["kx", gp] = do(AC, lambda e, b=b: e.activation(kraw[:].rearrange("p a b -> p (a b)"), PS[:, b, :], ACT.Copy),
                                     [t, *state.get("kraw", [])])
                banks.free(b, state["kx", gp])

            def KS(gp):
                for i in range(4):
                    ts = do(DV, lambda e, i=i: e.bn_stats(st6[:, 20 + i, :], kraw[:, i // 2, (i % 2) * 128:(i % 2 + 1) * 128]),
                            [state["kx", gp], state.get("st2")])
                    yield
                for i in range(4):
                    ta = do(DV, lambda e, i=i: e.bn_aggr(mvk[:, i, :], st6[:, 20 + i, :]), [ts, state.get("kn")])
                    yield
                state["st2"] = ta
                got = []
                yield from rsqrt(mvk[:, :, 1], rsk[:, :], ntq[:, 0:4], [ta], PO, got)
                t = got[0]
                t = do(PO, lambda e: e.tensor_scalar(mvk[:, :, 0], mvk[:, :, 0], -1.0, 1.0, ALU.mult, ALU.mult), [t])
                for i in range(4):
                    v = kraw[:, i // 2, (i % 2) * 128:(i % 2 + 1) * 128]
                    t2 = do(PO, lambda e, v=v, i=i: e.tensor_scalar(v, v, mvk[:, i, 0:1], rsk[:, i:i + 1],
                                                                   ALU.add, ALU.mult), [t])
                state["kn"] = t2

            def KT(gp):
                b, w = banks.take()
                tp = do(PE, [lambda e, b=b, i=i: e.transpose(
                    PS[:, b, (i % 2) * 256 + (i // 2) * 128:(i % 2) * 256 + (i // 2) * 128 + 128],
                    kraw[:, i // 2, (i % 2) * 128:(i % 2 + 1) * 128], idf[:, :]) for i in range(4)], [*w, state["kn"], t_id])
                state["kraw"] = [tp]
                te = do(AC, lambda e, b=b: e.activation(kxT[:].rearrange("p a b -> p (a b)"), PS[:, b, :], ACT.Identity,
                                                        scale=ln8[:, 6:7], bias=ln8[:, 7:8]),
                        [tp, *state.get(("kxu", gp - 1), [])])
                banks.free(b, te)
                state["kxT", gp] = te

            def VX(gp):
                i, w = wring.take()
                td = Q.dma(SP, [(wst[i][:], A["wkvx"][gp, :, :, 256:512])], w)
                tv = []
                for j in range(2):
                    b, w = banks.take()
                    t = do(PE, [lambda e, q=q, k=k, b=b: e.matmul(
                        PS[0:64, b, (q % 2) * 256:(q % 2 + 1) * 256], ctxT[:, k, q * 64:(q + 1) * 64], wst[i][:, k, :],
                        start=(k == 0), stop=(k == 1)) for q in (2 * j, 2 * j + 1) for k in range(2)], [*w, td])
                    tv.append(do(AC, lambda e, b=b, j=j: e.activation(
                        vx[:, 2 * j:2 * j + 2, :].rearrange("p a b -> p (a b)"), PS[0:64, b, :], ACT.Copy),
                        [t, *state.get(("vxu", gp - 1), [])]))
                    banks.free(b, tv[-1])
                wring.free(i, t)
                state["vx", gp] = tv

            def P2(s, j):
                gp, bb = s // 4, s % 4
                b, w = banks.take()
                fns = []
                for hh in range(2):
                    for ci in range(2):
                        fns.append(lambda e, b=b, hh=hh, ci=ci: e.transpose(
                            PS[:, b, hh * 256 + ci * 128:hh * 256 + ci * 128 + 128],
                            raw[:, slot[gp, 2 * bb + ci], (2 * j + hh) * 128:(2 * j + hh + 1) * 128], idf[:, :]))
                tp = do(PE, fns, [*w, *[state["nmh", s, ci, 2 * j + 1] for ci in range(2)], t_id])
                dst = (qT, qT, qxT, qxT, kT)[j][s % 2]
                o = (0, 2, 0, 2, 0)[j]
                v = (0, 0, 4, 4, 2)[j]
                te = do(AC, lambda e, b=b: e.activation(
                    dst[:, o:o + 2, :].rearrange("p a b -> p (a b)"), PS[:, b, :], ACT.Identity,
                    scale=ln8[:, v:v + 1], bias=ln8[:, v + 1:v + 2]), [tp, *t_l8, *state.get(("qu", s - 2), [])])
                banks.free(b, te)
                state["qT", s, j] = te
                if j == P2ORDER[-1]:
                    for c in (2 * bb, 2 * bb + 1):
                        raws.free(slot[gp, c], tp)

            P2ORDER = (4, 0, 1, 2, 3)

            def scores(u):
                s, h = u
                g = h // 2
                q_, k_ = qT[s % 2], kT[s % 2]
                i, w = smr.take()
                b, bw = banks.take()
                t = do(PE, [lambda e, b=b, c=c: e.matmul(
                    PS[:, b, c * 256:(c + 1) * 256], q_[:, h, c * 128:(c + 1) * 128], k_[:, g, :],
                    start=True, stop=True) for c in range(2)], [*bw, state["qT", s, h // 2], state["qT", s, 4]])
                tm = do(DV, lambda e, b=b: e.tensor_reduce(
                    sm[i][:, 0, 0:2], PS[:, b, :].rearrange("p (c t) -> p c t", c=2), X, ALU.max, negate=True), [t, *w])
                for c in range(2):
                    tx = do(AC, lambda e, b=b, c=c: e.activation(
                        P[i][:, c, :], PS[:, b, c * 256:(c + 1) * 256], ACT.Exp,
                        bias=sm[i][:, 0, c:c + 1], accum_out=sm[i][:, 1, c:c + 1]), [tm, *w])
                banks.free(b, tx)
                state.setdefault(("qu", s), []).append(t)
                return i, tx

            def norm(u, st_):
                i, tx = st_
                tr = do(DV, lambda e: e.reciprocal(sm[i][:, 2, 0:2], sm[i][:, 1, 0:2]), [tx])
                for j in range(2):
                    tn = do(DV, lambda e, j=j: e.tensor_scalar(P[i][:, j, :], P[i][:, j, :], sm[i][:, 2, j:j + 1], None,
                                                               ALU.mult), [tr])
                return i, tn

            def turn_p(u, st_):
                s, h = u
                i, tn = st_
                z, zw = ptr.take()
                b, bw = banks.take()
                t = do(PE, [lambda e, b=b, c=c, tc=tc: e.transpose(
                    PS[:, b, tc * 256 + c * 128:tc * 256 + c * 128 + 128], P[i][:, c, tc * 128:(tc + 1) * 128], idf[:, :])
                    for tc in range(2) for c in range(2)], [*bw, tn])
                dst = PT[z][:].rearrange("p a b -> p (a b)")
                te = do(AC, lambda e, b=b: e.activation(dst, PS[:, b, :], ACT.Copy), [t, *zw])
                banks.free(b, te)
                smr.free(i, t)
                return z, te

            def times_v(u, st_):
                s, h = u
                gp, bb = s // 4, s % 4
                g = h // 2
                z, te = st_
                b, bw = banks.take()
                t = do(PE, [lambda e, b=b, tc=tc: e.matmul(
                    PS[:, b, 0:256], vr[:, vslot[gp, 2 * bb + tc], g * 128:(g + 1) * 128], PT[z][:, tc, :],
                    start=(tc == 0), stop=(tc == 1)) for tc in range(2)],
                    [*bw, te, state["v", gp, 2 * bb], state["v", gp, 2 * bb + 1]])
                ptr.free(z, t)
                k = 8 * gp + h
                ty = do(AC, lambda e, b=b: e.activation(
                    yT[:, h, :], PS[:, b, 0:256], ACT.Copy, scale=ismo[:, k:k + 1]), [t, t_is, state.get(("q8", s - 1, h // 2))])
                banks.free(b, ty)
                state["yt", s, h] = ty
                if h == 3:
                    for c in (2 * bb, 2 * bb + 1):
                        vrs.free(vslot[gp, c], t)

            def x_scores(u):
                s, _ = u
                gp, bb = s // 4, s % 4
                q_ = qxT[s % 2]
                i, w = smr.take()
                b, bw = banks.take()
                t = do(PE, [lambda e, b=b, h=h, c=c: e.matmul(
                    PS[:, b, (2 * h + c) * 64:(2 * h + c + 1) * 64], q_[:, h, c * 128:(c + 1) * 128],
                    kxT[:, h // 2, bb * 64:(bb + 1) * 64], start=True, stop=True)
                    for h in range(4) for c in range(2)], [*bw, state["qT", s, 2], state["qT", s, 3], state["kxT", gp]])
                state.setdefault(("qu", s), []).append(t)
                state.setdefault(("kxu", gp), []).append(t)
                pf = P[i][:].rearrange("p a b -> p (a b)")
                p3 = pf.rearrange("p (j t) -> p j t", t=64)
                ps3 = PS[:, b, :].rearrange("p (j t) -> p j t", t=64)
                tm = do(DV, lambda e: e.tensor_reduce(sm[i][:, 0, :], ps3, X, ALU.max), [t, *w])
                ts = do(DV, lambda e: e.tensor_tensor(p3, ps3, sm[i][:, 0, :].unsqueeze(2).to_broadcast([128, 8, 64]),
                                                      ALU.subtract), [tm, *w])
                banks.free(b, ts)
                return i, do(AC, lambda e: e.activation(pf, pf, ACT.Exp), [ts])

            def x_norm(u, st_):
                i, tx = st_
                p3 = P[i][:].rearrange("p a b -> p (a b)").rearrange("p (j t) -> p j t", t=64)
                tm = do(DV, lambda e: e.tensor_reduce(sm[i][:, 1, :], p3, X, ALU.add), [tx])
                tr = do(DV, lambda e: e.reciprocal(sm[i][:, 2, :], sm[i][:, 1, :]), [tm])
                return i, do(DV, lambda e: e.tensor_tensor(
                    p3, p3, sm[i][:, 2, :].unsqueeze(2).to_broadcast([128, 8, 64]), ALU.mult), [tr])

            def x_turn(u, st_):
                i, tn = st_
                zs = []
                for g in range(2):
                    z, zw = ptr.take()
                    b, bw = banks.take()
                    t = do(PE, [lambda e, b=b, j=j, g=g: e.transpose(
                        PS[0:64, b, j * 128:(j + 1) * 128],
                        P[i][:].rearrange("p a b -> p (a b)")[:, (4 * g + j) * 64:(4 * g + j + 1) * 64],
                        idf[:, :]) for j in range(4)], [*bw, tn])
                    dst = PT[z][0:64].rearrange("p a b -> p (a b)")
                    te = do(AC, lambda e, b=b, dst=dst: e.activation(dst, PS[0:64, b, :], ACT.Copy), [t, *zw])
                    zs.append((z, te))
                    banks.free(b, te)
                smr.free(i, t)
                return zs

            def x_times_v(u, zs):
                s, _ = u
                gp, bb = s // 4, s % 4
                for g, (z, te) in enumerate(zs):
                    b, bw = banks.take()
                    t = do(PE, lambda e, b=b, g=g, z=z: e.matmul(
                        PS[:, b, :], vx[:, bb, g * 128:(g + 1) * 128], PT[z][0:64].rearrange("p a b -> p (a b)"),
                        start=True, stop=True), [*bw, te, *state["vx", gp]])
                    ptr.free(z, t)
                    for h in range(2):
                        k = 8 * gp + 4 + 2 * g + h
                        ty = do(AC, lambda e, b=b, h=h, k=k, g=g: e.activation(
                            yT[:, 4 + 2 * g + h, :], PS[:, b, h * 256:(h + 1) * 256], ACT.Copy, scale=ismo[:, k:k + 1]),
                            [t, t_is, state.get(("q8", s - 1, 2 + g))])
                        state["yt", s, 4 + 2 * g + h] = ty
                    banks.free(b, ty)
                state.setdefault(("vxu", gp), []).append(t)

            def QO(s, p):
                two = lambda v: v[:, 2 * p:2 * p + 2, :].rearrange("p a b -> p (a b)")
                yield from quant(two(yT), yF, yt, two(cat), [state["yt", s, 2 * p + 1]], [state.get(("catu", p))],
                                 lambda t: state.update({("q8", s, p): t}))

            def OP(s, p):
                gp, bb = s // 4, s % 4
                if p == 0:
                    state["ob", s] = obank.take()
                b, w = state["ob", s]
                t = do(PE, [lambda e, c=c, j=j, W=W: e.matmul(
                    PS[:, b, c * 256:(c + 1) * 256], cat[:, j, c * 128:(c + 1) * 128], W[:, j, :],
                    start=(j == 0 and W is PH and c == 0), stop=(j == 7 and W is PL), skip_group_check=True)
                    for c in range(2) for j in (2 * p, 2 * p + 1) for W in (PH, PL)],
                    [*(w if p == 0 else []), state["q8", s, p], state["p", gp][p]])
                state["catu", p] = t
                if bb == 3 and gp < 3:
                    load_p(gp + 1, p, [t])
                if p == 3:
                    xv = xt[:, 2 * bb:2 * bb + 2, :].rearrange("p a b -> p (a b)")
                    tx = do(DV, lambda e: e.scalar_tensor_tensor(xv, PS[:, b, :], sproj[:, 0:1], xv, ALU.mult, ALU.add),
                            [t, t_sp, *t_h0] + state.get(("x", bb), []))
                    obank.free(b, tx)
                    state["x", bb] = [tx]

            STEPS = 16
            PARTS = (2, 0, 1)
            KX(0)
            VX(0)
            turn(xn, first, ev_ln, (0,))
            load_w(0, (4, 5, 0, 1, 2, 3))
            div(0)
            div(1)
            sts = lambda n, cs: [lambda c=c: ST(0, c, PARTS[n]) for c in cs]
            weave(KS(0))
            weave(quantise(0))
            weave(quantise(1))
            for c in range(4):
                P1(0, c, PARTS[0])
            weave(quantise(2))
            for c in range(4):
                P1(0, c, PARTS[1])
            weave(quantise(3), chain(*sts(0, range(4))))
            for c in range(4):
                P1(0, c, PARTS[2])
            KT(0)
            weave(chain(*sts(1, (0, 1)), *sts(2, (0, 1)), lambda: NM(0)))
            start(1)
            div(4)
            div(5)
            weave(chain(*sts(1, (2, 3))), chain(*sts(2, (2, 3)), lambda: NM(1)))
            weave(quantise(4))
            for j in P2ORDER:
                P2(0, j)

            xv = xq[0], xq[1]

            def x_split(b, t):
                bb = state["xs"]
                cols = slice(bb * 256, (bb + 1) * 256)
                ps = PS[:, b, :].rearrange("p (k t) -> p k t", k=2)
                return split(ps, xv[0][:, :, cols], xv[1][:, :, cols], [t], state["lastP1"])

            def moe_load(j, el):
                i = j % 6
                v = lambda W: W[:].rearrange("p a b -> p (a b)")[:, i * 512:(i + 1) * 512].rearrange("p (a b) -> p a b", a=2)
                state["gu", j] = pieces(A["wgu"][j].rearrange("p g k m -> p g (k m)"), v(WH), v(WL),
                                        state["lastP1"] if j < 6 else state["guu", j - 6], None, AC, el)

            def dn_load(j):
                i, w = dring.take()
                o = slice(j % 8 * 256, j % 8 * 256 + 256)
                hi, lo = (xq[z][:].rearrange("p a b -> p (a b)")[:, o] for z in (2, 3))
                users = state["lastP1"] if j < 8 else state["dnu", j - 8]
                t = Q.dma(SP, [(dst_[i][:], A["wdn"][j])], w)
                th = do(PO, lambda e: e.tensor_scalar(hi, dst_[i][:], 1.0, 1.0, ALU.mult, ALU.mult), [t, *users])
                tl = do(PO, lambda e: e.tensor_tensor(lo, dst_[i][:], hi.bitcast(F32), ALU.subtract), [th])
                dring.free(i, tl)
                state["dn", j] = tl

            line = []

            def flow(u):
                for n in range(len(line) - 1, -1, -1):
                    u_, k, st_ = line[n]
                    x = u_[1] == 4
                    if k == 2:
                        (x_times_v if x else times_v)(u_, st_)
                        line.pop(n)
                    elif k == 1:
                        line[n] = (u_, 2, (x_turn if x else turn_p)(u_, st_))
                    else:
                        line[n] = (u_, 1, (x_norm if x else norm)(u_, st_))
                if u:
                    line.insert(0, (u, 0, (x_scores if u[1] == 4 else scores)(u)))

            def filler(s, k):
                gp = s // 4
                one, other = [], []
                if s == 0 and k < 3:
                    if k < 2:
                        div(6 + k)
                    if k:
                        other.append(lambda: quantise(5 + k))
                    else:
                        weave(quantise(5))
                if 0 < s < STEPS and k == 0:
                    P2(s, P2ORDER[4])
                if s + 2 < STEPS:
                    g2, b2 = (s + 2) // 4, (s + 2) % 4
                    q = k - 1 if s == 0 else k
                    if 0 <= q < 3:
                        for c in (2 * b2, 2 * b2 + 1):
                            P1(g2, c, PARTS[q])
                        if b2 == 3 and g2 < 3:
                            load_w(g2 + 1, (2 * PARTS[q], 2 * PARTS[q] + 1))
                    if 0 < q < 4:
                        for c in (2 * b2, 2 * b2 + 1):
                            one.append(lambda c=c: ST(g2, c, PARTS[q - 1]))
                    if q == 3:
                        one.append(lambda: NM(s + 2))
                if s + 1 < STEPS and k:
                    P2(s + 1, P2ORDER[k - 1])
                if s == 0 and k > 2:
                    load_p(0, 2 * k - 6, [])
                    load_p(0, 2 * k - 5, [])
                if s % 4 == 3 and gp < 3 and k == 2:
                    KX(gp + 1)
                if s % 4 == 3 and gp < 3 and k == 4:
                    one.append(lambda: KS(gp + 1))
                if s % 4 == 0 and 0 < s < STEPS:
                    if k == 2:
                        KT(gp)
                    elif k == 3:
                        VX(gp)
                if s > 1 and k < 2:
                    OP(s - 2, 2 + k)
                if s > 1 and k == 0:
                    other.append(lambda: QO(s - 2, 3))
                if s and k in (1, 2, 4):
                    other.append(lambda: QO(s - 1, (None, 0, 1, None, 2)[k]))
                weave(chain(*one), chain(*other))
                if s and k in (2, 3):
                    OP(s - 1, k - 2)
                if s == STEPS and k == 4:
                    weave(QO(s - 1, 3))
                    OP(s - 1, 2)
                    OP(s - 1, 3)
                if s == 13 and k == 4:
                    state["lastP1"] = [t for u in w_users for t in u]
                if s > 13 and stages > 1:
                    bb = s - 14
                    if k == 2:
                        state["ln", bb] = ln_batch(bb, state["x", bb])
                    elif k == 4:
                        state["xs"] = bb
                        state["xs", bb] = turn_batch(bb, state["ln", bb], x_split)
                    if s == 15:
                        moe_load(k, PO)
                        dn_load(k)
                    if s == 16 and k == 0:
                        moe_load(5, PO)
                    if s == 16 and k < 3:
                        dn_load(5 + k)

            key = keys()
            for s in range(STEPS):
                if s == 12 and stages > 1:
                    next(key)
                for k in range(5):
                    flow((s, k))
                    filler(s, k)
            for k in range(5):
                flow(None)
                if stages > 1 and k == 1:
                    next(key)
                filler(STEPS, k)
            if stages > 1:
                state["ln", 3] = ln_batch(3, state["x", 3])


        def fence(tokens):
            for e in (PE, AC, DV, PO, SP):
                Q.wait(e, tokens)

        def gated(c, xh, xl, name, held, nb=3):
            r4, hr = Ring(4, 0, held[:4]), Ring(nb)
            sg = [sb(f"{name}sg{i}", [128, 512], F32, c) for i in range(nb)]
            hh, hl = ([sb(f"{name}{n}{i}", [128, 512], FR, c) for i in range(nb)] for n in ("hh", "hl"))
            begun = set()

            def front(W, h, waits):
                out_ = []
                cols = slice(h * 512, (h + 1) * 512)
                for gu in range(2):
                    b, w = r4.take()
                    ops = [(k, wi, a) for k in range(2) for wi, a in ((0, xh), (0, xl), (1, xh))]
                    fns = [lambda e, b=b, k=k, wi=wi, a=a, n=n, gu=gu: e.matmul(
                        PS[:, b, :], W[wi][:, gu, k, :], a[:, k, cols], start=(n == 0), stop=(n == 5))
                        for n, (k, wi, a) in enumerate(ops)]
                    out_ += [b, do(PE, fns, [*w, *waits])]
                return out_

            def down(h, i, D, waits, last=False):
                first = h not in begun
                begun.add(h)
                fns = []
                for cc in range(4):
                    ch = 4 * h + cc
                    for p, (a, w) in enumerate(((hh, 0), (hh, 1), (hl, 0))):
                        fns.append(lambda e, a=a, w=w, ch=ch, cc=cc, p=p: e.matmul(
                            PS[:, 4 + ch // 2, ch % 2 * 256:ch % 2 * 256 + 256], a[i][:, cc * 128:(cc + 1) * 128],
                            D[w], start=(first and p == 0 and ch % 2 == 0), stop=(last and p == 2),
                            skip_group_check=True))
                t = do(PE, fns, [*waits, *([w for b in (4 + 2 * h, 5 + 2 * h) for w in held[b]] if first else [])])
                hr.free(i, t)
                return t

            return r4, hr, sg, hh, hl, front, down

        end = [state["x", bb][0] for bb in range(4)]
        wuq = sl("wuq", [128, 16, 96])
        wuk = sl("wuk", [128, 16, 64])
        aw = sl("aw", [96, 16, 128])
        wrt = sl("wrt", [96, 1024])
        Bp = sl("Bp", [128, 8, 256])
        c1 = ExitStack()
        with c1:
            if stages > 1:
                fence([*end, (Q.sem[PO], Q.n[PO])] if Q.n.get(PO) else end)
                low, banks = banks.users[:4], Ring(4, 4, banks.users[4:] + obank.users)
                xh, xl = xq[0], xq[1]
                cst = sb("m_cst", [128, 32 + 4], F32, c1)
                idb = sb("m_idb", [128, 128], BF, c1)
                sel = sb("m_sel", [96, 3072], BF, c1)
                gst = sb("m_gst", [128, 64], F32, c1)
                gh = sb("m_gh", [128, 2, 32], FR, c1)
                gl = sb("m_gl", [128, 2, 32], FR, c1)
                bd = sb("m_bd", [128, 128], F32, c1)
                pr = sb("m_pr", [128, 8, 32], F32, c1)
                s8 = sb("m_s8", [128, 8], F32, c1)
                v8 = sb("m_v8", [128, 8, 8], F32, c1)
                i8 = sb("m_i8", [128, 8, 8], U32, c1)
                i8f = sb("m_i8f", [128, 64], F32, c1)
                OH = sb("m_OH", [128, 64, 32], F32, c1)
                OT = sb("m_OT", [128, 8, 128], F32, c1)
                RR = sb("m_RR", [128, 8, 128], F32, c1)
                tmp = [sb(f"m_tmp{i}", [128, 512], F32, c1) for i in range(2)]
                cand = sb("m_cand", [128, 32, 4], F32, c1)
                best = sb("m_best", [128, 32], F32, c1)
                e4 = sb("m_e4", [128, 32, 4], F32, c1)
                fi = sb("m_fi", [128, 32], F32, c1)
                ge = sb("m_ge", [128, 32], F32, c1)
                wa = sb("m_wa", [128, 32], F32, c1)
                co = sb("m_co", [128, 8, 8], F32, c1)
                ac_ = sb("m_ac", [128, 8, 4], F32, c1)
                cw = sb("m_cw", [128, 8, 32], F32, c1)
                c3 = sb("m_c3", [128, 8, 96], BF, c1)
                cwT = sb("m_cwT", [96, 1024], BF, c1)
                t_g = Q.dma(SP, [(gst[:], A["gate"]), (cst[:], A["cst"]), (idb[:], A["idb"]), (sel[:], A["sel"])])
                t_z = do(DV, lambda e: e.memset(bd[:], 0.0))
                t_bd = Q.dma(SP, [(bd[32 * j:32 * j + 32, 32 * j:32 * j + 32], A["sim"]) for j in range(4)], [t_z])
                iota, i48 = cst[:, 0:32], cst[:, 32:36]

                next(key)
                def router():
                    b, w = banks.take()
                    fns = []
                    for c in range(8):
                        n = 0
                        for k in range(2):
                            for a, g_ in ((xh, gh), (xh, gl), (xl, gh)):
                                fns.append(lambda e, c=c, k=k, a=a, g_=g_, n=n, b=b: e.matmul(
                                    PS[:, b, c * 32:(c + 1) * 32], a[:, k, c * 128:(c + 1) * 128], g_[:, k, :],
                                    start=(n == 0), stop=(n == 5)))
                                n += 1
                    t = do(PE, fns, [*w, *tx, *tgs])
                    lg = PS[:, b, 0:256].rearrange("p (c n) -> p c n", n=32)
                    up = lambda ap, n: ap.unsqueeze(2).to_broadcast([128, ap.shape[1], n])
                    tm = do(DV, lambda e: e.tensor_reduce(s8[:], lg, X, ALU.max), [t])
                    t = do(DV, lambda e: e.tensor_tensor(pr[:], lg, up(s8[:], 32), ALU.subtract), [tm])
                    banks.free(b, t)
                    t = do(AC, lambda e: e.activation(pr[:], pr[:], ACT.Exp), [t])
                    t = do(DV, lambda e: e.tensor_reduce(s8[:], pr[:], X, ALU.add), [t])
                    t = do(DV, lambda e: e.reciprocal(s8[:], s8[:]), [t])
                    t = do(DV, lambda e: e.tensor_tensor(pr[:], pr[:], up(s8[:], 32), ALU.mult), [t])
                    for c in range(8):
                        tv = do(DV, lambda e, c=c: e.max(v8[:, c, :], pr[:, c, :]), [t])
                    for c in range(8):
                        ti = do(DV, lambda e, c=c: e.max_index(i8[:, c, :], v8[:, c, :], pr[:, c, :]), [tv])
                    t = do(DV, lambda e: e.tensor_copy(i8f[:], i8[:].rearrange("p a b -> p (a b)")), [ti])
                    t_oh = do(DV, lambda e: e.tensor_tensor(OH[:], up(i8f[:], 32),
                                                            iota.unsqueeze(1).to_broadcast([128, 64, 32]), ALU.is_equal), [t, t_g])
                    t = do(DV, lambda e: e.tensor_reduce(s8[:], v8[:], X, ALU.add), [tv])
                    t = do(DV, lambda e: e.tensor_scalar(s8[:], s8[:], 1e-12, None, ALU.max), [t])
                    t = do(DV, lambda e: e.reciprocal(s8[:], s8[:]), [t])
                    t_wt = do(DV, lambda e: e.tensor_tensor(v8[:], v8[:], up(s8[:], 8), ALU.mult), [t, ti])
                    yield
                    te = []
                    for hh_ in range(2):
                        b, w = banks.take()
                        t = do(PE, [lambda e, b=b, c=c: e.transpose(
                            PS[:, b, c % 4 * 128:c % 4 * 128 + 128], OH[:, c * 8 + 4:c * 8 + 8, :].rearrange("p a b -> p (a b)"),
                            idf[:, :]) for c in range(4 * hh_, 4 * hh_ + 4)], [*w, t_oh, t_id])
                        te.append(do(AC, lambda e, b=b, hh_=hh_: e.activation(
                            OT[:, 4 * hh_:4 * hh_ + 4, :].rearrange("p a b -> p (a b)"), PS[:, b, :], ACT.Copy), [t]))
                        banks.free(b, te[-1])
                    yield
                    tr = []
                    for hh_ in range(2):
                        b, w = banks.take()
                        t = do(PE, [lambda e, b=b, c=c: e.matmul(
                            PS[:, b, c % 4 * 128:c % 4 * 128 + 128], OT[:, c, :], bd[:], start=True, stop=True)
                            for c in range(4 * hh_, 4 * hh_ + 4)], [*w, te[hh_], t_bd])
                        tr.append(do(AC, lambda e, b=b, hh_=hh_: e.activation(
                            RR[:, 4 * hh_:4 * hh_ + 4, :].rearrange("p a b -> p (a b)"), PS[:, b, :], ACT.Copy), [t]))
                        banks.free(b, tr[-1])
                    tc_ = [None, None]
                    for c in range(8):
                        tt = tmp[c % 2][:].rearrange("p (j i e) -> p j i e", j=4, i=4)
                        r_ = RR[:, c, :].rearrange("p (j e) -> p j e", j=4).unsqueeze(2).to_broadcast([128, 4, 4, 32])
                        o_ = OH[:, c * 8:c * 8 + 4, :].unsqueeze(1).to_broadcast([128, 4, 4, 32])
                        t = do(DV, lambda e, tt=tt, r_=r_, o_=o_: e.tensor_tensor(tt, r_, o_, ALU.mult),
                               [tr[c // 4], t_oh, t_bd, tc_[c % 2]])
                        tc_[c % 2] = do(DV, lambda e, c=c: e.tensor_reduce(
                            cand[:, c * 4:c * 4 + 4, :].rearrange("p a b -> p (a b)"), tmp[c % 2][:].rearrange("p (q e) -> p q e", e=32), X, ALU.add), [t])
                    t = do(DV, lambda e: e.tensor_reduce(best[:], cand[:], X, ALU.max), [tc_[1]])
                    i4b = i48.unsqueeze(1).to_broadcast([128, 32, 4])
                    tb = t
                    t = do(DV, lambda e: e.tensor_tensor(e4[:], cand[:], up(best[:], 4), ALU.is_equal), [tb])
                    t = do(DV, lambda e: e.tensor_tensor(e4[:], e4[:], i4b, ALU.mult), [t])
                    t = do(DV, lambda e: e.tensor_reduce(fi[:], e4[:], X, ALU.min), [t])
                    t = do(DV, lambda e: e.tensor_tensor(e4[:], up(fi[:], 4), i4b, ALU.is_equal), [t])
                    v3 = v8[:, :, 4:8]
                    ge3, wa3 = ge[:].rearrange("p (c j) -> p c j", j=4), wa[:].rearrange("p (c j) -> p c j", j=4)
                    tg_ = do(DV, lambda e: e.tensor_scalar(ge[:], best[:], 0.5, None, ALU.is_ge), [tb])
                    ta = do(DV, lambda e: e.tensor_tensor(wa3, v3, ge3, ALU.mult), [tg_, t_wt])
                    t2 = do(DV, lambda e: e.tensor_tensor(co[:, :, 4:8], v3, wa3, ALU.subtract), [ta])
                    t = do(DV, lambda e: e.tensor_tensor(e4[:], e4[:], up(wa[:], 4), ALU.mult), [t, ta])
                    t = do(DV, lambda e: e.tensor_reduce(ac_[:], e4[:].rearrange("p (c j) i -> p c i j", j=4), X, ALU.add), [t])
                    t = do(DV, lambda e: e.tensor_tensor(co[:, :, 0:4], v8[:, :, 0:4], ac_[:], ALU.add), [t])
                    t = do(DV, lambda e: e.tensor_tensor(OH[:], OH[:], up(co[:].rearrange("p a b -> p (a b)"), 32), ALU.mult), [t, t2])
                    t = do(DV, lambda e: e.tensor_reduce(cw[:], OH[:].rearrange("p (c r) e -> p c e r", r=8), X, ALU.add), [t])
                    for z in range(3):
                        cz = c3[:, :, 32 * z:32 * z + 32]
                        t = do(DV, lambda e, cz=cz: e.tensor_copy(cz, cw[:]), [t])
                        if z < 2:
                            t = do(DV, lambda e, cz=cz: e.tensor_tensor(cw[:], cw[:], cz, ALU.subtract), [t])
                    yield
                    b, w = banks.take()
                    pb = PS[0:96, b, :].bitcast(BF)
                    t = do(PE, [lambda e, c=c, pb=pb: e.transpose(pb[:, c * 128:(c + 1) * 128], c3[:, c, :], idb[:, :])
                                for c in range(8)], [*w, t, t_g])
                    t_cw = do(AC, lambda e, pb=pb: e.activation(cwT[:], pb, ACT.Copy), [t])
                    banks.free(b, t_cw)
                    state["cw"] = t_cw
                    yield

                r4, hr, sg, hh, hl, front, down = gated(c1, xh, xl, "m_", low + [[]] * 4, 3)
                NPRE = 7
                prea = sb("m_pre", [128, 2 * NPRE, 512], F32, c1)
                pre = [prea[:, i, :] for i in range(2 * NPRE)]
                wo = prea[:, 0:8, :].rearrange("p a (b c) -> p (a b) c", b=2)
                wuv = prea[:, 8:10, :].rearrange("p a (b c) -> p (a b) c", b=8)
                ub = sg
                ur = Ring(2)
                t_pre = {}

                def gu_of(j):
                    v = lambda W: W[:].rearrange("p a b -> p (a b)")[:, j % 6 * 512:j % 6 * 512 + 512].rearrange(
                        "p (g k m) -> p g k m", g=2, k=2)
                    return v(WH), v(WL)

                def dn_of(j):
                    return [xq[z][:].rearrange("p a b -> p (a b)")[:, j % 8 * 256:j % 8 * 256 + 256] for z in (2, 3)]

                def fronted(j, h):
                    bg, tg, bu, tu = front(gu_of(j), h, [state["gu", j], *[t for bb in (2 * h, 2 * h + 1) for t in state["xs", bb]]])
                    state.setdefault(("guu", j), []).append(tu)
                    return bg, tg, bu, tu

                def early(j, h):
                    bg, tg, bu, tu = fronted(j, h)
                    p_ = pre[2 * j + h]
                    ts = do(AC, lambda e: e.activation(p_, PS[:, bg, :], ACT.Silu), [tg])
                    r4.free(bg, ts)
                    i, w = ur.take()
                    t = do(AC, lambda e: e.activation(ub[i][:], PS[:, bu, :], ACT.Copy), [tu, *w])
                    r4.free(bu, t)
                    t_pre[j, h] = do(PO, lambda e: e.tensor_tensor(p_, p_, ub[i][:], ALU.mult), [ts, t])
                    ur.free(i, t_pre[j, h])

                def weighed(j, h):
                    if j >= NPRE:
                        bg, tg, bu, tu = fronted(j, h)
                    b, w = r4.take()
                    tcb = do(PE, lambda e: e.matmul(PS[:, b, :], sel[:, j * 128:(j + 1) * 128],
                                                    cwT[:, h * 512:(h + 1) * 512], start=True, stop=True), [*w, state["cw"]])
                    i, hw = hr.take()
                    if j >= NPRE:
                        ts = do(AC, lambda e: e.activation(sg[i][:], PS[:, bg, :], ACT.Silu), [tg, t_pre[NPRE - 1, 1], *hw])
                        r4.free(bg, ts)
                        t = do(DV, lambda e: e.tensor_tensor(sg[i][:], sg[i][:], PS[:, bu, :], ALU.mult), [ts, tu])
                        r4.free(bu, t)
                        src = sg[i][:]
                    else:
                        src, t = pre[2 * j + h], t_pre[j, h]
                    t = do(DV, lambda e: e.tensor_tensor(src, src, PS[:, b, :], ALU.mult), [t, tcb, *hw])
                    r4.free(b, t)
                    if (j, h) == (NPRE, 0):
                        state["wo"] = Q.dma(AC, [(wuv, A["wuv"]), (wo, A["wo"])], [t])
                    return j, h, i, lambda: split(src, hh[i][:], hl[i][:], [t], hw)

                def multiplied(u, last=False):
                    j, h, i, t_h = u
                    waits = [*t_h, state["dn", j], *([w for us in banks.users for w in us] if j == 0 else [])]
                    t = down(h, i, dn_of(j), waits, last)
                    state.setdefault(("dnu", j), []).append(t)
                    if h == 1 and j + 8 < 24:
                        dn_load(j + 8)
                    return t

                early(0, 0)
                early(1, 0)
                state["xs"] = 3
                state["xs", 3] = turn_batch(3, state["ln", 3], x_split)
                tx = [t for bb in range(4) for t in state["xs", bb]]
                tgs = split(gst[:], gh[:].rearrange("p a b -> p (a b)"), gl[:].rearrange("p a b -> p (a b)"), [t_g], [])
                t = do(DV, lambda e: e.scalar_tensor_tensor(tmp[0][:, 0:128], idf[:, :], -1.0, bd[:], ALU.mult, ALU.mult), [t_bd, t_id])
                t = do(DV, lambda e: e.tensor_tensor(bd[:], bd[:], tmp[0][:, 0:128], ALU.add), [t])
                t_bd = do(DV, lambda e: e.tensor_tensor(bd[:], bd[:], idf[:, :], ALU.add), [t])
                route = router()
                next(route)
                order = [(0, 1), (1, 1)] + [(j, h) for j in range(2, NPRE) for h in range(2)]
                for n, (j, h) in enumerate(order):
                    early(j, h)
                    if j + 6 < 24 and h == 1:
                        moe_load(j + 6, PO)
                    if n == 3:
                        next(key)
                    if n in (1, 2, 10):
                        next(route)
                pend = None
                end = [None] * 4

                def settle(h, t_y):
                    for bb in (2 * h, 2 * h + 1):
                        xv = xt[:, 2 * bb:2 * bb + 2, :].rearrange("p a b -> p (a b)")
                        end[bb] = do(DV, lambda e, bb=bb, xv=xv: e.tensor_tensor(xv, PS[:, 4 + bb, :], xv, ALU.add), [t_y])
                        yield
                    yield from ln_steps(2 * h, end[2 * h:2 * h + 2], 2,
                                        lambda t: tk.update({("ln", 2 * h): t, ("ln", 2 * h + 1): t}))

                order = [(j, h) for j in range(21) for h in range(2)] + [(j, h) for h in range(2) for j in range(21, 24)]
                settling, whole, parts = None, None, None
                for u in order + [None, None]:
                    new = weighed(*u) if u else None
                    if u and u[1] == 1 and NPRE <= u[0] < 18:
                        moe_load(u[0] + 6, DV)
                    if parts:
                        t_y = multiplied(parts, parts[0] == 23)
                        if parts[:2] == (23, 0):
                            settling = settle(0, t_y)
                    parts = (*whole[:3], whole[3]()) if whole else None
                    if settling and u:
                        for _ in range(12):
                            next(settling, None)
                    whole = new
                weave(settling)
                weave(settle(1, t_y))
                t_bp = []
                for z in range(4):
                    b, w = r4.take()
                    t = do(PE, [lambda e, b=b, p=p, o=o: e.matmul(
                        PS[64 * o:64 * o + 64, b, p % 2 * 256:p % 2 * 256 + 256], wuv[:, 2 * p + o, :], wo[:, 2 * p + o, :],
                        start=True, stop=True) for o in range(2) for p in (2 * z, 2 * z + 1)], [*w, state["wo"]])
                    t_bp.append(do(AC, lambda e, b=b, z=z: e.activation(
                        Bp[:, 2 * z:2 * z + 2, :].rearrange("p a b -> p (a b)"), PS[:, b, :], ACT.Copy), [t]))
                    r4.free(b, t_bp[-1])
                t_last = [t, t_y]

        c2 = ExitStack()
        with c2:
            if stages > 2:
                banks = Ring(8, 0, [*r4.users, *[[t] for t in end]])
                for e_ in (AC, DV, PO, SP):
                    Q.wait(e_, [*t_last, end[3]])
                fsc = sb("f_sc", [128, 12 + 256], F32, c2)
                t_fs = Q.dma(SP, [(fsc[:], A["fsc"])])
                cl = ExitStack()
                with cl:
                    seg = sl("seg", [128, 8], I32, cl)
                    segf = sl("segf", [128, 8], F32, cl)
                    mk = sl("mk", [128, 8, 64], F32, cl)
                    x2T = sl("x2T", [128, 2, 1024], F32, cl)
                    PT1 = sl("PT1", [128, 8, 256], F32, cl)
                    dd = PT1[:, 0:2, :].rearrange("p a (b c) -> p (a b) c", b=4)
                    t_seg = Q.dma(SP, [(seg[:], A["seg"])])
                    qcT = sl("qcT", [96, 1024], F32, cl)
                    QA = [sl(f"QA{i}", [128, 16, 256], F32, cl) for i in range(2)]
                    QB = [sl(f"QB{i}", [128, 8, 256], F32, cl) for i in range(2)]
                    S = [sl(f"S{i}", [128, 1024], F32, cl) for i in range(2)]
                    s16 = [sl(f"s16{i}", [128, 2, 16], F32, cl) for i in range(2)]
                    CT = x2T[:].rearrange("p k (a t) -> p (k a) t", t=256)

                    fh, fl = (W[:].rearrange("p a b -> p (a b)").rearrange("p (j n) -> p j n", j=6) for W in (WH, WL))
                    fdh, fdl = (xq[z][:].rearrange("p a b -> p (a b)")[:, 0:1536].rearrange("p (j n) -> p j n", j=6)
                                for z in (2, 3))
                    t_fw = []
                    for j in range(9):
                        i, w = wring.take()
                        if j < 6:
                            src, hi, lo = A["fgu"][j], fh[:, j, :], fl[:, j, :]
                        else:
                            q_ = 2 * (j - 6)
                            src, hi, lo = A["fdn"][:, q_ * 256:q_ * 256 + 512], \
                                fdh[:, q_:q_ + 2, :].rearrange("p a b -> p (a b)"), \
                                fdl[:, q_:q_ + 2, :].rearrange("p a b -> p (a b)")
                        wf = wst[i][:].rearrange("p a b -> p (a b)")
                        td = Q.dma(SP, [(wf.bitcast(I32), src)], w)
                        t = do(PO, lambda e, wf=wf: e.tensor_scalar(wf, wf.bitcast(I32), -128.0, 1.0, ALU.add, ALU.mult), [td])
                        th = do(PO, lambda e, wf=wf, hi=hi: e.tensor_scalar(hi, wf, 1.0, 1.0, ALU.mult, ALU.mult), [t])
                        tl = do(PO, lambda e, wf=wf, hi=hi, lo=lo: e.tensor_tensor(lo, wf, hi.bitcast(F32), ALU.subtract), [th])
                        wring.free(i, tl)
                        t_fw.append(tl)

                    t_qc = {}

                    def compress(bb):
                        cols = slice(bb * 256, (bb + 1) * 256)
                        te, = turn_batch(bb, tk["ln", bb], lambda b, t: [do(AC, lambda e: e.activation(
                            x2T[:, :, cols], PS[:, b, :].rearrange("p (k t) -> p k t", k=2), ACT.Copy), [t])])
                        yield
                        b, w = banks.take()
                        t = do(PE, [lambda e, b=b, k=k: e.matmul(PS[0:96, b, 0:256], wdq[:, k, :], x2T[:, k, cols],
                                                                 start=(k == 0), stop=(k == 1)) for k in range(2)],
                               [*w, te, tk["tb"]])
                        yield
                        t_qc[bb] = do(AC, lambda e, b=b: e.activation(qcT[:, cols], PS[0:96, b, 0:256], ACT.Copy), [t])
                        banks.free(b, t_qc[bb])

                    qu, tq, su, sx, ts_, tp_, te_, pu = {}, {}, {}, {}, {}, {}, {}, {"PT": [], "CT": []}

                    def queries(bb, part):
                        i = bb % 2
                        for kind, p in [("A", p) for p in range(8)][4 * part:4 * part + 4] if part < 2 else [("B", p) for p in range(4)]:
                            dst, tab = (QA[i], 0) if kind == "A" else (QB[i], 256)
                            b, w = banks.take()
                            t = do(PE, [lambda e, b=b, hh=hh, p=p, kind=kind: e.matmul(
                                PS[:, b, hh * 256:(hh + 1) * 256],
                                aw[:, 2 * p + hh, :] if kind == "A" else wrt[:, (2 * p + hh) * 128:(2 * p + hh + 1) * 128],
                                qcT[:, bb * 256:(bb + 1) * 256], start=True, stop=True) for hh in range(2)],
                                [*w, t_qc[bb], *tk["aw"]])
                            te = do(DV, lambda e, b=b, p=p, dst=dst, tab=tab: e.tensor_tensor(
                                dst[:, 2 * p:2 * p + 2, :], PS[:, b, :].rearrange("p (a t) -> p a t", a=2),
                                tb_[:, tab:tab + 256].unsqueeze(1).to_broadcast([128, 2, 256]), ALU.mult),
                                [t, tk["tb"], *qu.get(bb - 2, [])])
                            tq.setdefault(bb, []).append(te)
                            banks.free(b, te)

                    def mask():
                        t = do(DV, lambda e: e.tensor_copy(segf[:], seg[:]), [t_seg])
                        t = do(DV, lambda e: e.tensor_tensor(dd, segf[:].unsqueeze(2).to_broadcast([128, 8, 64]),
                                                             tb_[:, 640:704].unsqueeze(1).to_broadcast([128, 8, 64]), ALU.subtract),
                               [t, tk["tb"]])
                        t = do(DV, lambda e: e.tensor_scalar(mk[:], dd, 0.0, None, ALU.is_ge), [t])
                        t = do(DV, lambda e: e.scalar_tensor_tensor(mk[:], dd, 8.0, mk[:], ALU.is_le, ALU.mult), [t])
                        tk["dd"] = t
                        tk["mk"] = do(DV, lambda e: e.tensor_scalar(mk[:], mk[:], NEG, -NEG, ALU.mult, ALU.add), [t])

                    def soft(c):
                        bb, i = c // 2, c % 2
                        cc = c % 2 * 128
                        S_ = S[i]
                        ms = []
                        for z in range(2):
                            b, w = banks.take()
                            fns = []
                            for p in range(4 * z, 4 * z + 4):
                                fns.append(lambda e, b=b, p=p: e.matmul(
                                    PS[:, b, p % 4 * 128:p % 4 * 128 + 128], QB[bb % 2][:, p, cc:cc + 128],
                                    KZ[:, bb, :, :].rearrange("p a t -> p (a t)"), start=True, stop=False, skip_group_check=True))
                                for o in range(2):
                                    fns.append(lambda e, b=b, p=p, o=o: e.matmul(
                                        PS[:, b, p % 4 * 128 + o * 64:p % 4 * 128 + o * 64 + 64], QA[bb % 2][:, 2 * p + o, cc:cc + 128],
                                        KA[:, bb * 64:(bb + 1) * 64], start=False, stop=True, skip_group_check=True))
                            t = do(PE, fns, [*w, *tq[bb], *tk["kz"]])
                            ms.append(do(DV, lambda e, b=b, z=z: e.scalar_tensor_tensor(
                                S_[:, z * 512:(z + 1) * 512].rearrange("p (h t) -> p h t", h=8),
                                PS[:, b, :].rearrange("p (h t) -> p h t", h=8), float(1.0 / np.sqrt(np.float32(192.0))),
                                mk[:, c, :].unsqueeze(1).to_broadcast([128, 8, 64]), ALU.mult, ALU.add),
                                [t, tk["mk"], *su.get(i, [])]))
                            banks.free(b, ms[-1])
                        qu.setdefault(bb, []).append(t)
                        s3 = S_[:].rearrange("p (h t) -> p h t", h=16)
                        t = do(DV, lambda e: e.tensor_reduce(s16[i][:, 0, :], s3, X, ALU.max), ms)
                        t = do(DV, lambda e: e.tensor_tensor(s3, s3, s16[i][:, 0, :].unsqueeze(2).to_broadcast([128, 16, 64]),
                                                             ALU.subtract), [t])
                        sx[c] = do(AC, lambda e: e.activation(S_[:], S_[:], ACT.Exp), [t])

                    def scaled(c):
                        i = c % 2
                        s3 = S[i][:].rearrange("p (h t) -> p h t", h=16)
                        t = do(DV, lambda e: e.tensor_reduce(s16[i][:, 1, :], s3, X, ALU.add), [sx[c]])
                        t = do(DV, lambda e: e.reciprocal(s16[i][:, 1, :], s16[i][:, 1, :]), [t])
                        ts_[c] = do(DV, lambda e: e.tensor_tensor(
                            s3, s3, s16[i][:, 1, :].unsqueeze(2).to_broadcast([128, 16, 64]), ALU.mult), [t])

                    def turned(c):
                        ci = c % 2
                        for z in range(2):
                            b, w = banks.take()
                            t = do(PE, [lambda e, b=b, p=p: e.transpose(
                                PS[:, b, p % 4 * 128:p % 4 * 128 + 128], S[ci][:, p * 128:(p + 1) * 128], idf[:, :])
                                for p in range(4 * z, 4 * z + 4)], [*w, ts_[c]])
                            tp_.setdefault(c // 2, []).append(do(AC, lambda e, b=b, z=z: e.activation(
                                PT1[:, 4 * z:4 * z + 4, ci * 128:(ci + 1) * 128], PS[:, b, :].rearrange("p (a t) -> p a t", a=4), ACT.Copy),
                                [t, tk["dd"], *pu["PT"]]))
                            banks.free(b, tp_[c // 2][-1])
                        su[ci] = [t]

                    def values(bb):
                        for z in range(4):
                            b, w = banks.take()
                            t = do(PE, lambda e, b=b, z=z: e.matmul(
                                PS[:, b, :], BDK[:, bb, :], PT1[:, 2 * z:2 * z + 2, :].rearrange("p a b -> p (a b)"),
                                start=True, stop=True), [*w, *tp_[bb], tk["bk"]])
                            te_.setdefault(bb, []).append(do(AC, lambda e, b=b, z=z: e.activation(
                                CT[:, 2 * z:2 * z + 2, :].rearrange("p a b -> p (a b)"), PS[:, b, :], ACT.Copy),
                                [t, *pu["CT"], *t_qc.values()]))
                            banks.free(b, te_[bb][-1])
                        pu["PT"] = [t]

                    def project(bb):
                        b, w = banks.take()
                        t = do(PE, [lambda e, b=b, ci=ci, p=p: e.matmul(
                            PS[:, b, ci * 256:(ci + 1) * 256], CT[:, p, ci * 128:(ci + 1) * 128], Bp[:, p, :],
                            start=(p == 0), stop=(p == 7)) for ci in range(2) for p in range(8)], [*w, *te_[bb], *t_bp])
                        pu["CT"] = [t]
                        xv = xt[:, 2 * bb:2 * bb + 2, :].rearrange("p a b -> p (a b)")
                        end[bb] = do(DV, lambda e, b=b: e.tensor_tensor(xv, PS[:, b, :], xv, ALU.add), [t, tk["ln", bb]])
                        banks.free(b, end[bb])
                        if stages > 3:
                            state["ln", bb] = ln_batch(bb, [end[bb], t_tb[bb]])

                    def f_split(bb):
                        cols = slice(bb * 256, (bb + 1) * 256)
                        state["fs", bb] = turn_batch(bb, state["ln", bb], lambda b, t: split(
                            PS[:, b, :].rearrange("p (k t) -> p k t", k=2), xq[0][:, :, cols], xq[1][:, :, cols], [t], []))

                    mask()
                    weave(compress(0), compress(1))
                    for part in range(3):
                        queries(0, part)
                    weave(compress(2), compress(3))
                    t_tb = t_qc
                    for bb in range(4):
                        more = bb < 3
                        soft(2 * bb)
                        if more:
                            queries(bb + 1, 0)
                        scaled(2 * bb)
                        soft(2 * bb + 1)
                        if more:
                            queries(bb + 1, 1)
                        turned(2 * bb)
                        scaled(2 * bb + 1)
                        if bb:
                            project(bb - 1)
                        if more:
                            queries(bb + 1, 2)
                        turned(2 * bb + 1)
                        if more and bb and stages > 3:
                            f_split(bb - 1)
                        values(bb)
                        if not more and stages > 3:
                            f_split(bb - 1)
                    project(3)
                    t_end = pu["CT"]

                if stages > 3:
                    for e_ in (AC, DV):
                        Q.wait(e_, t_end)
                    r4, hr, fsg, fhh, fhl, front, down = gated(c2, xq[0], xq[1], "f_", banks.users)
                    old, banks = banks, Ring(1, 7, [banks.users[7]])

                    def f_front(j, h):
                        v = lambda a: a[:, j, :].rearrange("p (g k m) -> p g k m", g=2, k=2)
                        bg, tg, bu, tu = front((v(fh), v(fl)), h, [*state["fs", 2 * h], *state["fs", 2 * h + 1], *t_fw])
                        i, hw = hr.take()
                        ts = do(AC, lambda e: e.activation(fsg[i][:], PS[:, bg, :], ACT.Silu, scale=fsc[:, j:j + 1]), [tg, t_fs, *hw])
                        r4.free(bg, ts)
                        t = do(DV, lambda e: e.scalar_tensor_tensor(fsg[i][:], PS[:, bu, :], fsc[:, 6 + j:7 + j], fsg[i][:],
                                                                    ALU.mult, ALU.mult), [ts, tu, *hw])
                        r4.free(bu, t)
                        return j, h, i, lambda: split(fsg[i][:], fhh[i][:], fhl[i][:], [t], hw)

                    def f_end(bb, t_y):
                        xv, nv = xt[:, 2 * bb:2 * bb + 2, :], xn[:, 2 * bb:2 * bb + 2, :]
                        t = do(DV, lambda e: e.tensor_tensor(
                            nv, PS[:, 4 + bb, :].rearrange("p (a b) -> p a b", a=2),
                            fsc[:, 12:268].unsqueeze(1).to_broadcast([128, 2, 256]), ALU.mult), [t_y, t_fs])
                        end[bb] = do(DV, lambda e: e.tensor_tensor(xv, xv, nv, ALU.add), [t])

                    order = [(j, h) for h in range(2) for j in range(3)] + [(j, h) for j in range(3, 6) for h in range(2)]
                    whole, parts = None, None
                    for n, u in enumerate(order + [None, None]):
                        if n == 2:
                            f_split(3)
                            old.users[7] = banks.users[0]
                        new = f_front(*u) if u else None
                        if parts:
                            j, h, i, t_h = parts
                            t_y = down(h, i, (fdh[:, j, :], fdl[:, j, :]), t_h, last=(j == 5))
                        ended = parts and parts[:2] == (5, 0)
                        parts = (*whole[:3], whole[3]()) if whole else None
                        if ended:
                            f_end(0, t_y)
                            f_end(1, t_y)
                        whole = new
                    f_end(2, t_y)
                    f_end(3, t_y)

        xo = out.rearrange("(c p) d -> p c d", p=128)
        t_out = [Q.dma(SP, [(xo[:, 4 * h:4 * h + 4, :], xt[:, 4 * h:4 * h + 4, :])], end[2 * h:2 * h + 2]) for h in range(2)]
        Q.wait(SP, t_out)

        block = ctx.enter_context(nc.Block())

        @block.sync
        def _(e):
            Q.play(SP, e)

        @block.scalar
        def _(e):
            Q.play(AC, e)

        @block.vector
        def _(e):
            Q.play(DV, e)

        @block.tensor
        def _(e):
            Q.play(PE, e)

        @block.gpsimd
        def _(e):
            Q.play(PO, e)


def layout(v):
    f = np.ascontiguousarray
    g = {k: np.asarray(a) for k, a in v.items()}
    o = {}
    o["x"] = f(g["x"].reshape(1024, 256))
    o["ctxT"] = f(g["ctx_2048"].reshape(256, 256).T)
    o["idf"] = np.eye(128, dtype=np.float32)
    L = "L0_xattn_"
    two = lambda a: a.reshape(2, 128).T
    o["vec"] = f(np.concatenate([two(g[L + n]) for n in (
        "ln_w", "ln_b", "q_in_scale", "qx_in_scale", "k_in_scale", "v_in_scale")], axis=1))
    o["ln8"] = f(np.stack([g[L + n] for n in (
        "qln_w", "qln_b", "kln_w", "kln_b", "qxln_w", "qxln_b", "kxln_w", "kxln_b")], axis=1))
    s = g[L + "proj_smooth"].reshape(2, 4, 4, 128)
    o["smo"] = f(s.transpose(3, 1, 0, 2).reshape(128, 32))
    o["sca"] = f(np.tile(np.stack([g[L + n].reshape(()) for n in (
        "wq_scale", "wqx_scale", "wk_scale", "wv_scale", "proj_w_scale", "proj_in_scale")])[None], (128, 1)))
    q4 = lambda n, m: g[L + n].reshape(4, m, 2, 128).transpose(0, 3, 2, 1)
    o["wall"] = f(np.concatenate([q4("wq", 512), q4("wqx", 512), q4("wk", 256), q4("wv", 256)], axis=3))
    kv = g[L + "w_kv_x"].reshape(2, 4, 256, 2, 128)
    o["wkvx"] = f(kv.transpose(1, 4, 3, 0, 2).reshape(4, 128, 2, 512))
    wp = g[L + "wproj"].reshape(256, 2, 4, 4, 128)
    o["wproj"] = f(wp.transpose(2, 4, 1, 3, 0).reshape(4, 128, 8, 256))
    wg = g["L0_ffn_gate_up_proj"].reshape(32, 2, 96, 256).transpose(1, 0, 2, 3).reshape(2, 24, 128, 2, 128)
    o["wgu"] = f(wg.transpose(1, 4, 0, 3, 2))
    o["wdn"] = f(g["L0_ffn_down_proj"].transpose(0, 2, 1).reshape(24, 128, 256))
    o["gate"] = f(g["L0_ffn_gate_weight"].reshape(32, 2, 128).transpose(2, 1, 0).reshape(128, 64))
    o["sim"] = f(g["L0_ffn_similarity"])
    o["cst"] = f(np.tile(np.concatenate([np.arange(32), np.arange(4) - 8]).astype(np.float32)[None], (128, 1)))
    bf = mybir.dt.np(BF)
    o["idb"] = np.eye(128, dtype=np.float32).astype(bf)
    o["sel"] = f((np.arange(96)[:, None] % 32 == np.arange(3072)[None] // 96).astype(np.float32).astype(bf))
    M = "L1_xattn_"
    kp = lambda a: a.reshape(2, 128, -1).transpose(1, 0, 2)
    o["wdq"] = f(kp(g[M + "W_dq"]))
    o["wkvc"] = f(kp(g[M + "W_kvc"]))
    hT = lambda a: a.reshape(-1, 16, 128).transpose(2, 1, 0)
    o["wuq"], o["wuk"], o["wuv"] = f(hT(g[M + "W_uq"])), f(hT(g[M + "W_uk"])), f(hT(g[M + "W_uv"]))
    o["wo"] = f(g[M + "W_o"].reshape(16, 128, 256).transpose(1, 0, 2))
    o["wqr"] = f(g[M + "W_qr"].reshape(96, 16, 64))
    o["wrt"] = f(g[M + "W_qr"].reshape(96, 16, 2, 32)[:, :, ::-1].reshape(96, 1024))
    kr = g[M + "W_kr"]
    krr = kr.reshape(64, 2, 32)[:, ::-1].reshape(64, 64)
    o["wkr"] = f(np.stack([np.tile(kr, (1, 2)), np.tile(krr, (1, 2))], axis=1))
    half = np.arange(32, dtype=np.float32)
    inv = (np.float32(1.0) / np.float32(10000.0) ** (half / np.float32(32))).astype(np.float32)
    ang = np.arange(256, dtype=np.float32)[:, None] * inv
    cos, sin = np.cos(ang).T, np.sin(ang).T
    c4, s4 = np.tile(cos, (4, 1)), np.concatenate([-sin, sin, -sin, sin])
    ones = np.ones((64, 256), np.float32)
    o["rope"] = f(np.concatenate([np.concatenate([ones, c4[64:]]), s4, c4[:, :64], s4[:, :64],
                                  np.tile(np.arange(64, dtype=np.float32)[None], (128, 1))], axis=1).astype(np.float32))
    o["seg"] = f(g["itok_BxS_0_1023"].reshape(8, 128).T)
    F = "L1_ffn_"

    def wide(a):
        z = np.full((768, a.shape[1]), 128, a.dtype)
        z[:704] = a
        return z
    gu = np.stack([wide(g[F + "wq_gate"]), wide(g[F + "wq_up"])]).reshape(2, 6, 128, 2, 128)
    o["fgu"] = f(gu.transpose(1, 4, 0, 3, 2).reshape(6, 128, 512))
    o["fdn"] = f(wide(g[F + "wq_down"].T).reshape(6, 128, 256).transpose(1, 0, 2).reshape(128, 1536))
    sc = np.zeros((2, 768), np.float32)
    sc[0, :704], sc[1, :704] = g[F + "s_gate"], g[F + "s_up"]
    o["fsc"] = f(np.concatenate([sc.reshape(12, 128).T, np.tile(g[F + "s_down"][None], (128, 1))], axis=1))
    return o


def kernel(**inputs):
    import concourse.bacc as bacc
    from concourse.bass_utils import run_bass_kernel_spmd

    nc = bacc.Bacc("TRN2", target_bir_lowering=False, num_devices=1)
    arrays = layout(inputs)
    A = {n: nc.dram_tensor(f"in_{n}", a.shape, mybir.dt.from_np(a.dtype), kind="ExternalInput").ap()
         for n, a in arrays.items()}
    out = nc.dram_tensor("out_x", (1024, 256), F32, kind="ExternalOutput").ap()
    program(nc, A, out)
    r = run_bass_kernel_spmd(nc, [{f"in_{n}": a for n, a in arrays.items()}], core_ids=[0])
    return r.results[0]["out_x"].reshape(4, 256, 256)
```
